# Optimizing a Trainium2 kernel written in Bass

```python
import numpy as np
import jax
import jax.numpy as jnp

def _softmax(x, axis=-1):
    return jax.nn.softmax(x, axis=axis)

def _gelu(x):
    return jax.nn.gelu(x, approximate=True)

def _silu(x):
    return jax.nn.silu(x)

def _sigmoid(x):
    return jax.nn.sigmoid(x)

def _layernorm(x, axis=-1, eps=1e-05):
    m = jnp.mean(x, axis=axis, keepdims=True)
    v = jnp.var(x, axis=axis, keepdims=True)
    return (x - m) / jnp.sqrt(v + eps)

def _scatter_add(tgt, idx, src, axis=0):
    return tgt.at[idx].add(src)

def _segment_sum(src, seg, n):
    return jax.ops.segment_sum(src, seg, n)
kernel_name = 'mk_vit_tower_postln_d4_tok_img768_r4_233254'

def setup_inputs(seed: int=0):
    np.random.seed(seed)
    _w = jnp.asarray

    def _rec_inputs():
        import jax
        import jax.numpy as jnp
        _rk = jax.random.key(seed)
        x = 7.57192e-06 + 1.00007 * jax.random.normal(jax.random.fold_in(_rk, 1), (32, 3, 84, 84), jnp.float32)
        return x
    x = _rec_inputs()

    def _L0_tok_setup():
        import jax, jax.numpy as jnp
        import numpy as np
        PATCH = 16
        EPS = 1e-05

        def _conv_offsets(x, offset_w, offset_b):
            off = jax.lax.conv_general_dilated(x, offset_w, window_strides=(PATCH, PATCH), padding='VALID', dimension_numbers=('NCHW', 'OIHW', 'NCHW'))
            return off + offset_b[None, :, None, None]

        def _deform_conv(x, offset_w, offset_b, dconv_w):
            B, C, H, W = x.shape
            kh = kw = PATCH
            K = kh * kw
            Ho, Wo = (H // PATCH, W // PATCH)
            off = _conv_offsets(x, offset_w, offset_b)
            off = off.reshape(B, K, 2, Ho, Wo)
            dy = off[:, :, 0].transpose(0, 2, 3, 1)
            dx = off[:, :, 1].transpose(0, 2, 3, 1)
            ii, jj = jnp.meshgrid(jnp.arange(kh), jnp.arange(kw), indexing='ij')
            ki = ii.reshape(-1).astype(x.dtype)
            kj = jj.reshape(-1).astype(x.dtype)
            base_y = (jnp.arange(Ho, dtype=x.dtype) * PATCH)[:, None] + ki[None, :]
            base_x = (jnp.arange(Wo, dtype=x.dtype) * PATCH)[:, None] + kj[None, :]
            py = base_y[None, :, None, :] + dy
            px = base_x[None, None, :, :] + dx
            y0 = jnp.floor(py)
            x0 = jnp.floor(px)
            wy1 = py - y0
            wx1 = px - x0
            wy0 = 1.0 - wy1
            wx0 = 1.0 - wx1
            y0i = y0.astype(jnp.int32)
            x0i = x0.astype(jnp.int32)
            y1i = y0i + 1
            x1i = x0i + 1
            xt = x.transpose(0, 2, 3, 1)
            bidx = jnp.arange(B)[:, None, None, None]

            def gather(yi, xi):
                ok = ((yi >= 0) & (yi < H) & (xi >= 0) & (xi < W)).astype(x.dtype)
                v = xt[bidx, jnp.clip(yi, 0, H - 1), jnp.clip(xi, 0, W - 1)]
                return v * ok[..., None]
            sampled = gather(y0i, x0i) * (wy0 * wx0)[..., None] + gather(y0i, x1i) * (wy0 * wx1)[..., None] + gather(y1i, x0i) * (wy1 * wx0)[..., None] + gather(y1i, x1i) * (wy1 * wx1)[..., None]
            Wk = dconv_w.reshape(dconv_w.shape[0], C, K)
            out = jnp.einsum('bhwkc,ock->bohw', sampled, Wk)
            return out
        key = jax.random.key(seed)
        ks = jax.random.split(key, 3)
        B, C, H, W = (64, 3, 224, 224)
        O = 192
        x = jax.random.normal(ks[0], (B, C, H, W), jnp.float32)
        offset_w = jax.random.normal(ks[1], (2 * PATCH * PATCH, C, PATCH, PATCH), jnp.float32) * 0.01
        offset_b = jnp.zeros((2 * PATCH * PATCH,), jnp.float32)
        dconv_w = jax.random.normal(ks[2], (O, C, PATCH, PATCH), jnp.float32) * 0.02
        bn_gamma = jnp.ones((O,), jnp.float32)
        bn_beta = jnp.zeros((O,), jnp.float32)
        return {'x': x, 'offset_w': offset_w, 'offset_b': offset_b, 'dconv_w': dconv_w, 'bn_gamma': bn_gamma, 'bn_beta': bn_beta}
    _L0_tok_all = _L0_tok_setup()
    _L0_tok_in = {k: v for k, v in _L0_tok_all.items() if k in ('offset_w', 'offset_b', 'dconv_w', 'bn_gamma', 'bn_beta')}
    del _L0_tok_all

    def _L0_attn_setup():
        import jax, jax.numpy as jnp
        import numpy as np
        B, N, DIM, H = (8, 256, 192, 12)
        DH = DIM // H
        LATENT = 32
        EPS = 1e-05

        def _heads(t):
            b, n, _ = t.shape
            return t.reshape(b, n, H, DH).transpose(0, 2, 1, 3).reshape(b * H, n, DH)

        def _merge(t, b):
            _, n, dh = t.shape
            return t.reshape(b, H, n, dh).transpose(0, 2, 1, 3).reshape(b, n, H * dh)

        def _ln(v, g, bta):
            mu = v.mean(-1, keepdims=True)
            var = ((v - mu) ** 2).mean(-1, keepdims=True)
            return (v - mu) * jax.lax.rsqrt(var + EPS) * g + bta

        def _rope(t):
            n, dh = (t.shape[-2], t.shape[-1])
            inv = 1.0 / 10000.0 ** (jnp.arange(0, dh, 2, dtype=jnp.float32) / dh)
            f = jnp.arange(n, dtype=jnp.float32)[:, None] * inv[None, :]
            f = jnp.concatenate([f, f], -1)[None]
            x1, x2 = jnp.split(t, 2, -1)
            rot = jnp.concatenate([-x2, x1], -1)
            return t * jnp.cos(f) + rot * jnp.sin(f)
        key = jax.random.key(seed)
        ks = jax.random.split(key, 6)
        s = 0.02
        return {'x': jax.random.normal(ks[0], (B, N, DIM), jnp.float32), 'Wq': jax.random.normal(ks[1], (DIM, DIM), jnp.float32) * s, 'Wkv': jax.random.normal(ks[2], (DIM, DIM), jnp.float32) * s, 'Wo_ctx': jax.random.normal(ks[3], (DIM, DIM), jnp.float32) * s, 'bo_ctx': jnp.zeros((DIM,), jnp.float32), 'Wo_lat': jax.random.normal(ks[4], (DIM, DIM), jnp.float32) * s, 'bo_lat': jnp.zeros((DIM,), jnp.float32), 'ln_g': jnp.ones((DH,), jnp.float32), 'ln_b': jnp.zeros((DH,), jnp.float32)}
    _L0_attn_all = _L0_attn_setup()
    _L0_attn_in = {k: v for k, v in _L0_attn_all.items() if k in ('Wq', 'Wkv', 'Wo_ctx', 'bo_ctx', 'Wo_lat', 'bo_lat', 'ln_g', 'ln_b')}
    del _L0_attn_all

    def _L0_ffn_setup():
        import jax, jax.numpy as jnp
        import numpy as np
        E = 8
        TOP_K = 2
        CAP_RATIO = 1.2
        key = jax.random.key(seed)
        k1, k2, k3, k4 = jax.random.split(key, 4)
        B, L, D, H = (2, 512, 192, 512)
        x = jax.random.normal(k1, (B, L, D), dtype=jnp.float32)
        Wg = jax.random.normal(k2, (D, E), dtype=jnp.float32) * 0.02
        W1 = jax.random.normal(k3, (E, D, 2 * H), dtype=jnp.float32) * 0.02
        W2 = jax.random.normal(k4, (E, H, D), dtype=jnp.float32) * 0.02
        return {'x': x, 'Wg': Wg, 'W1': W1, 'W2': W2}
    _L0_ffn_all = _L0_ffn_setup()
    _L0_ffn_in = {k: v for k, v in _L0_ffn_all.items() if k in ('Wg', 'W1', 'W2')}
    del _L0_ffn_all

    def _L1_attn_setup():
        import math
        import jax, jax.numpy as jnp
        import numpy as np
        D_MODEL = 192
        N_HEAD = 12
        N_BR = 4
        DH = D_MODEL // N_HEAD
        H_TOT = N_BR * N_HEAD
        SCALE = math.pi / math.sqrt(3.0)
        ATTNSCALE = DH ** (-0.5)

        def _chebyshev(T, max_deg, dtype):
            if T > 1:
                x = 2.0 * jnp.arange(T, dtype=dtype) / (T - 1) - 1.0
            else:
                x = jnp.zeros(1, dtype=dtype)
            cols = [jnp.ones_like(x), x]
            for _ in range(2, max_deg + 1):
                cols.append(2.0 * x * cols[-1] - cols[-2])
            return jnp.stack(cols, axis=1)

        def _attention(X, Wq, bq, Wk, bk, Wv, bv, A, id_bias, sink_scalars, v_nulls, Wo, bo):
            B, T, C = X.shape
            dtype = X.dtype
            q = (X @ Wq.T + bq).reshape(B, T, H_TOT, DH).transpose(0, 2, 1, 3)
            v = (X @ Wv.T + bv).reshape(B, T, N_HEAD, DH).transpose(0, 2, 1, 3)
            v = jnp.tile(v, (1, N_BR, 1, 1))
            k = (X @ Wk.T + bk).reshape(B, T, N_HEAD, DH).transpose(0, 2, 1, 3)
            k = jnp.tile(k, (1, N_BR, 1, 1))
            S = (A - A.T)[None] + jax.vmap(jnp.diag)(id_bias)
            q = q + jnp.einsum('bhtd,hde->bhte', q, S)
            H = DH // 2
            max_deg = max(3, 2 * H)
            T_all = _chebyshev(T, max_deg, dtype)
            frac = jnp.arange(H, dtype=dtype) / (H - 1) if H > 1 else jnp.zeros(1, dtype)
            n_f = jnp.clip(1 + jnp.round(frac * (max_deg - 2)).astype(jnp.int32), 1, max_deg - 1)
            raw1 = T_all[:, n_f]
            raw2 = T_all[:, n_f + 1]
            nrm = jnp.sqrt(raw1 * raw1 + raw2 * raw2 + 1e-08)
            base1 = (raw1 / nrm)[None, None]
            base2 = (raw2 / nrm)[None, None]

            def apply_rot(x_in):
                x1, x2 = (x_in[..., :H], x_in[..., H:])
                return jnp.concatenate([x1 * base1 - x2 * base2, x1 * base2 + x2 * base1], axis=-1)
            q = apply_rot(q)
            k = apply_rot(k)
            scores = jnp.einsum('bhtd,bhsd->bhts', q, k) * ATTNSCALE
            key_self = jnp.maximum((k * k).sum(-1), 1e-06)
            denom = jnp.sqrt(key_self)[:, :, None, :]
            w = jax.nn.softplus(scores / denom)
            causal = jnp.tril(jnp.ones((T, T), bool))
            w = jnp.where(causal, w, 0.0)
            w = w * jax.nn.sigmoid(SCALE * w)
            sinks = sink_scalars.reshape(1, H_TOT, 1, 1)
            alpha = 1.0 / (w.sum(-1, keepdims=True) + sinks + 1e-06)
            probs_tokens = w * alpha
            probs_sink = jnp.broadcast_to(sinks, (B, H_TOT, T, 1)) * alpha
            out_tokens = jnp.einsum('bhts,bhsd->bhtd', probs_tokens, v)
            v_null = v_nulls.reshape(H_TOT, DH)[None, :, None, :]
            context = out_tokens + probs_sink * v_null
            context = context.reshape(B, N_BR, N_HEAD, T, DH)
            context = context.transpose(0, 1, 3, 2, 4).reshape(B, N_BR, T, C)
            y = jnp.einsum('bntc,ncd->bntd', context, Wo) + bo[None, :, None, :]
            return y.mean(axis=1)
        key = jax.random.key(seed)
        ks = jax.random.split(key, 12)
        s = 0.02
        return {'X': jax.random.normal(ks[0], (2, 256, D_MODEL), jnp.float32), 'Wq': jax.random.normal(ks[1], (D_MODEL * N_BR, D_MODEL), jnp.float32) * s, 'bq': jax.random.normal(ks[2], (D_MODEL * N_BR,), jnp.float32) * s, 'Wk': jax.random.normal(ks[3], (D_MODEL, D_MODEL), jnp.float32) * s, 'bk': jax.random.normal(ks[4], (D_MODEL,), jnp.float32) * s, 'Wv': jax.random.normal(ks[5], (D_MODEL, D_MODEL), jnp.float32) * s, 'bv': jax.random.normal(ks[6], (D_MODEL,), jnp.float32) * s, 'A': jax.random.normal(ks[7], (DH, DH), jnp.float32) * s, 'id_bias': jax.random.normal(ks[8], (H_TOT, DH), jnp.float32) * s, 'sink_scalars': jax.random.normal(ks[9], (H_TOT, 1, 1), jnp.float32) * s, 'v_nulls': jax.random.normal(ks[10], (N_BR, D_MODEL), jnp.float32) * s, 'Wo': jax.random.normal(ks[11], (N_BR, D_MODEL, D_MODEL), jnp.float32) * s, 'bo': jnp.zeros((N_BR, D_MODEL), jnp.float32)}
    _L1_attn_all = _L1_attn_setup()
    _L1_attn_in = {k: v for k, v in _L1_attn_all.items() if k in ('Wq', 'bq', 'Wk', 'bk', 'Wv', 'bv', 'A', 'id_bias', 'sink_scalars', 'v_nulls', 'Wo', 'bo')}
    del _L1_attn_all

    def _L1_ffn_setup():
        import jax, jax.numpy as jnp
        import numpy as np
        DIM = 192
        NUM_HEADS = 12
        HEAD_DIM = DIM // NUM_HEADS
        SCALE = HEAD_DIM ** (-0.5)
        NUM_EXPERTS = 8
        RANK = 16
        ALPHA = 32
        TOPK = 2
        SCALING = ALPHA / RANK
        B, S = (8, 256)
        key = jax.random.key(seed)
        ks = jax.random.split(key, 12)
        d, e, r = (DIM, NUM_EXPERTS, RANK)
        inp = {'x': jax.random.normal(ks[0], (B, S, d), jnp.float32), 'Wg': jax.random.normal(ks[1], (e, d), jnp.float32) * 0.02, 'bg': jax.random.normal(ks[2], (e,), jnp.float32) * 0.02, 'Wqkv': jax.random.normal(ks[3], (3 * d, d), jnp.float32) * 0.02, 'bqkv': jax.random.normal(ks[4], (3 * d,), jnp.float32) * 0.02, 'Wproj': jax.random.normal(ks[5], (d, d), jnp.float32) * 0.02, 'bproj': jax.random.normal(ks[6], (d,), jnp.float32) * 0.02, 'A': jax.random.normal(ks[7], (e, r, d), jnp.float32) * 0.05, 'ba': jax.random.normal(ks[8], (e, r), jnp.float32) * 0.02, 'Bm': jax.random.normal(ks[9], (e, 3 * d, r), jnp.float32) * 0.05, 'bb': jax.random.normal(ks[10], (e, 3 * d), jnp.float32) * 0.02}
        return inp
    _L1_ffn_all = _L1_ffn_setup()
    _L1_ffn_in = {k: v for k, v in _L1_ffn_all.items() if k in ('Wg', 'bg', 'Wqkv', 'bqkv', 'Wproj', 'bproj', 'A', 'ba', 'Bm', 'bb')}
    del _L1_ffn_all

    def _L2_attn_setup():
        import jax, jax.numpy as jnp
        import numpy as np
        B, N, C, H = (8, 256, 192, 12)
        D = C // H
        SCALE = D ** (-0.5)

        def _norm_unbiased(t):
            mu = t.mean(axis=-1, keepdims=True)
            var = ((t - mu) ** 2).sum(axis=-1, keepdims=True) / (t.shape[-1] - 1)
            return (t - mu) / jnp.sqrt(var)
        key = jax.random.key(seed)
        kx, kq, kp, kb = jax.random.split(key, 4)
        x = jax.random.normal(kx, (B, N, C), dtype=jnp.float32)
        s = 1.0 / np.sqrt(C)
        qkv_w = jax.random.uniform(kq, (3 * C, C), minval=-s, maxval=s, dtype=jnp.float32)
        proj_w = jax.random.uniform(kp, (C, C), minval=-s, maxval=s, dtype=jnp.float32)
        proj_b = jax.random.uniform(kb, (C,), minval=-s, maxval=s, dtype=jnp.float32)
        return {'x': x, 'qkv_w': qkv_w, 'proj_w': proj_w, 'proj_b': proj_b}
    _L2_attn_all = _L2_attn_setup()
    _L2_attn_in = {k: v for k, v in _L2_attn_all.items() if k in ('qkv_w', 'proj_w', 'proj_b')}
    del _L2_attn_all

    def _L2_ffn_setup():
        import math
        import jax, jax.numpy as jnp
        import numpy as np
        B, L, D = (8, 1024, 192)
        E = 16
        TOP_K = 2
        F_EXP = 4 * D
        F_SH = F_EXP * 2 // 4
        key = jax.random.key(seed)
        ks = jax.random.split(key, 8)
        s = lambda fan_in: 1.0 / math.sqrt(fan_in)
        return {'hidden_states': jax.random.normal(ks[0], (B, L, D), jnp.float32), 'gate_weight': jax.random.uniform(ks[1], (E, D), jnp.float32, -s(D), s(D)), 'Wg': jax.random.uniform(ks[2], (E, F_EXP, D), jnp.float32, -s(D), s(D)), 'Wu': jax.random.uniform(ks[3], (E, F_EXP, D), jnp.float32, -s(D), s(D)), 'Wd': jax.random.uniform(ks[4], (E, D, F_EXP), jnp.float32, -s(F_EXP), s(F_EXP)), 'Ws_g': jax.random.uniform(ks[5], (F_SH, D), jnp.float32, -s(D), s(D)), 'Ws_u': jax.random.uniform(ks[6], (F_SH, D), jnp.float32, -s(D), s(D)), 'Ws_d': jax.random.uniform(ks[7], (D, F_SH), jnp.float32, -s(F_SH), s(F_SH))}
    _L2_ffn_all = _L2_ffn_setup()
    _L2_ffn_in = {k: v for k, v in _L2_ffn_all.items() if k in ('gate_weight', 'Wg', 'Wu', 'Wd', 'Ws_g', 'Ws_u', 'Ws_d')}
    del _L2_ffn_all

    def _L3_attn_setup():
        import jax, jax.numpy as jnp
        import numpy as np
        B, S, DIM, H = (8, 256, 192, 12)
        HD = DIM // H
        SCALE = HD ** (-0.5)

        def _split_heads(t):
            b, s, _ = t.shape
            return t.reshape(b, s, H, HD).transpose(0, 2, 1, 3)
        key = jax.random.key(seed)
        ks = jax.random.split(key, 9)
        std = DIM ** (-0.5)
        x = jax.random.normal(ks[0], (B, S, DIM), dtype=jnp.float32)
        Wq = jax.random.normal(ks[1], (DIM, DIM), dtype=jnp.float32) * std
        bq = jax.random.normal(ks[2], (DIM,), dtype=jnp.float32) * 0.01
        Wk = jax.random.normal(ks[3], (DIM, DIM), dtype=jnp.float32) * std
        bk = jax.random.normal(ks[4], (DIM,), dtype=jnp.float32) * 0.01
        Wv = jax.random.normal(ks[5], (DIM, DIM), dtype=jnp.float32) * std
        bv = jax.random.normal(ks[6], (DIM,), dtype=jnp.float32) * 0.01
        Wp = jax.random.normal(ks[7], (DIM, DIM), dtype=jnp.float32) * std
        bp = jax.random.normal(ks[8], (DIM,), dtype=jnp.float32) * 0.01
        return {'x': x, 'Wq': Wq, 'bq': bq, 'Wk': Wk, 'bk': bk, 'Wv': Wv, 'bv': bv, 'Wp': Wp, 'bp': bp}
    _L3_attn_all = _L3_attn_setup()
    _L3_attn_in = {k: v for k, v in _L3_attn_all.items() if k in ('Wq', 'bq', 'Wk', 'bk', 'Wv', 'bv', 'Wp', 'bp')}
    del _L3_attn_all

    def _L3_ffn_setup():
        import jax, jax.numpy as jnp
        import numpy as np
        B_SZ, S, D = (8, 128, 192)
        H = 12
        N_EXP = 8
        RANK = 16
        ALPHA = 32
        TOP_K = 2
        key = jax.random.key(seed)
        ks = jax.random.split(key, 9)
        x = jax.random.normal(ks[0], (B_SZ, S, D), jnp.float32)
        W_qkv = jax.random.normal(ks[1], (3 * D, D), jnp.float32) * 0.02
        b_qkv = jnp.zeros((3 * D,), jnp.float32)
        W_gate = jax.random.normal(ks[2], (N_EXP, D), jnp.float32) * 0.02
        b_gate = jnp.zeros((N_EXP,), jnp.float32)
        A = jax.random.normal(ks[3], (N_EXP, RANK, D), jnp.float32) * 0.02
        B_lora = jax.random.normal(ks[4], (N_EXP, 3 * D, RANK), jnp.float32) * 0.02
        W_proj = jax.random.normal(ks[5], (D, D), jnp.float32) * 0.02
        b_proj = jnp.zeros((D,), jnp.float32)
        return {'x': x, 'W_qkv': W_qkv, 'b_qkv': b_qkv, 'W_gate': W_gate, 'b_gate': b_gate, 'A': A, 'B_lora': B_lora, 'W_proj': W_proj, 'b_proj': b_proj}
    _L3_ffn_all = _L3_ffn_setup()
    _L3_ffn_in = {k: v for k, v in _L3_ffn_all.items() if k in ('W_qkv', 'b_qkv', 'W_gate', 'b_gate', 'A', 'B_lora', 'W_proj', 'b_proj')}
    del _L3_ffn_all
    return {'x': x, 'L0_tok_offset_w': _L0_tok_in['offset_w'], 'L0_tok_offset_b': _L0_tok_in['offset_b'], 'L0_tok_dconv_w': _L0_tok_in['dconv_w'], 'L0_tok_bn_gamma': _L0_tok_in['bn_gamma'], 'L0_tok_bn_beta': _L0_tok_in['bn_beta'], 'L0_attn_Wq': _L0_attn_in['Wq'], 'L0_attn_Wkv': _L0_attn_in['Wkv'], 'L0_attn_Wo_ctx': _L0_attn_in['Wo_ctx'], 'L0_attn_bo_ctx': _L0_attn_in['bo_ctx'], 'L0_attn_Wo_lat': _L0_attn_in['Wo_lat'], 'L0_attn_bo_lat': _L0_attn_in['bo_lat'], 'L0_attn_ln_g': _L0_attn_in['ln_g'], 'L0_attn_ln_b': _L0_attn_in['ln_b'], 'L0_ffn_Wg': _L0_ffn_in['Wg'], 'L0_ffn_W1': _L0_ffn_in['W1'], 'L0_ffn_W2': _L0_ffn_in['W2'], 'L1_attn_Wq': _L1_attn_in['Wq'], 'L1_attn_bq': _L1_attn_in['bq'], 'L1_attn_Wk': _L1_attn_in['Wk'], 'L1_attn_bk': _L1_attn_in['bk'], 'L1_attn_Wv': _L1_attn_in['Wv'], 'L1_attn_bv': _L1_attn_in['bv'], 'L1_attn_A': _L1_attn_in['A'], 'L1_attn_id_bias': _L1_attn_in['id_bias'], 'L1_attn_sink_scalars': _L1_attn_in['sink_scalars'], 'L1_attn_v_nulls': _L1_attn_in['v_nulls'], 'L1_attn_Wo': _L1_attn_in['Wo'], 'L1_attn_bo': _L1_attn_in['bo'], 'L1_ffn_Wg': _L1_ffn_in['Wg'], 'L1_ffn_bg': _L1_ffn_in['bg'], 'L1_ffn_Wqkv': _L1_ffn_in['Wqkv'], 'L1_ffn_bqkv': _L1_ffn_in['bqkv'], 'L1_ffn_Wproj': _L1_ffn_in['Wproj'], 'L1_ffn_bproj': _L1_ffn_in['bproj'], 'L1_ffn_A': _L1_ffn_in['A'], 'L1_ffn_ba': _L1_ffn_in['ba'], 'L1_ffn_Bm': _L1_ffn_in['Bm'], 'L1_ffn_bb': _L1_ffn_in['bb'], 'L2_attn_qkv_w': _L2_attn_in['qkv_w'], 'L2_attn_proj_w': _L2_attn_in['proj_w'], 'L2_attn_proj_b': _L2_attn_in['proj_b'], 'L2_ffn_gate_weight': _L2_ffn_in['gate_weight'], 'L2_ffn_Wg': _L2_ffn_in['Wg'], 'L2_ffn_Wu': _L2_ffn_in['Wu'], 'L2_ffn_Wd': _L2_ffn_in['Wd'], 'L2_ffn_Ws_g': _L2_ffn_in['Ws_g'], 'L2_ffn_Ws_u': _L2_ffn_in['Ws_u'], 'L2_ffn_Ws_d': _L2_ffn_in['Ws_d'], 'L3_attn_Wq': _L3_attn_in['Wq'], 'L3_attn_bq': _L3_attn_in['bq'], 'L3_attn_Wk': _L3_attn_in['Wk'], 'L3_attn_bk': _L3_attn_in['bk'], 'L3_attn_Wv': _L3_attn_in['Wv'], 'L3_attn_bv': _L3_attn_in['bv'], 'L3_attn_Wp': _L3_attn_in['Wp'], 'L3_attn_bp': _L3_attn_in['bp'], 'L3_ffn_W_qkv': _L3_ffn_in['W_qkv'], 'L3_ffn_b_qkv': _L3_ffn_in['b_qkv'], 'L3_ffn_W_gate': _L3_ffn_in['W_gate'], 'L3_ffn_b_gate': _L3_ffn_in['b_gate'], 'L3_ffn_A': _L3_ffn_in['A'], 'L3_ffn_B_lora': _L3_ffn_in['B_lora'], 'L3_ffn_W_proj': _L3_ffn_in['W_proj'], 'L3_ffn_b_proj': _L3_ffn_in['b_proj']}

def reference(x, L0_tok_offset_w, L0_tok_offset_b, L0_tok_dconv_w, L0_tok_bn_gamma, L0_tok_bn_beta, L0_attn_Wq, L0_attn_Wkv, L0_attn_Wo_ctx, L0_attn_bo_ctx, L0_attn_Wo_lat, L0_attn_bo_lat, L0_attn_ln_g, L0_attn_ln_b, L0_ffn_Wg, L0_ffn_W1, L0_ffn_W2, L1_attn_Wq, L1_attn_bq, L1_attn_Wk, L1_attn_bk, L1_attn_Wv, L1_attn_bv, L1_attn_A, L1_attn_id_bias, L1_attn_sink_scalars, L1_attn_v_nulls, L1_attn_Wo, L1_attn_bo, L1_ffn_Wg, L1_ffn_bg, L1_ffn_Wqkv, L1_ffn_bqkv, L1_ffn_Wproj, L1_ffn_bproj, L1_ffn_A, L1_ffn_ba, L1_ffn_Bm, L1_ffn_bb, L2_attn_qkv_w, L2_attn_proj_w, L2_attn_proj_b, L2_ffn_gate_weight, L2_ffn_Wg, L2_ffn_Wu, L2_ffn_Wd, L2_ffn_Ws_g, L2_ffn_Ws_u, L2_ffn_Ws_d, L3_attn_Wq, L3_attn_bq, L3_attn_Wk, L3_attn_bk, L3_attn_Wv, L3_attn_bv, L3_attn_Wp, L3_attn_bp, L3_ffn_W_qkv, L3_ffn_b_qkv, L3_ffn_W_gate, L3_ffn_b_gate, L3_ffn_A, L3_ffn_B_lora, L3_ffn_W_proj, L3_ffn_b_proj):
    import jax
    import jax.numpy as jnp

    def _L0_tok_ref(x, offset_w, offset_b, dconv_w, bn_gamma, bn_beta):
        import jax, jax.numpy as jnp
        import numpy as np
        PATCH = 16
        EPS = 1e-05

        def _conv_offsets(x, offset_w, offset_b):
            off = jax.lax.conv_general_dilated(x, offset_w, window_strides=(PATCH, PATCH), padding='VALID', dimension_numbers=('NCHW', 'OIHW', 'NCHW'))
            return off + offset_b[None, :, None, None]

        def _deform_conv(x, offset_w, offset_b, dconv_w):
            B, C, H, W = x.shape
            kh = kw = PATCH
            K = kh * kw
            Ho, Wo = (H // PATCH, W // PATCH)
            off = _conv_offsets(x, offset_w, offset_b)
            off = off.reshape(B, K, 2, Ho, Wo)
            dy = off[:, :, 0].transpose(0, 2, 3, 1)
            dx = off[:, :, 1].transpose(0, 2, 3, 1)
            ii, jj = jnp.meshgrid(jnp.arange(kh), jnp.arange(kw), indexing='ij')
            ki = ii.reshape(-1).astype(x.dtype)
            kj = jj.reshape(-1).astype(x.dtype)
            base_y = (jnp.arange(Ho, dtype=x.dtype) * PATCH)[:, None] + ki[None, :]
            base_x = (jnp.arange(Wo, dtype=x.dtype) * PATCH)[:, None] + kj[None, :]
            py = base_y[None, :, None, :] + dy
            px = base_x[None, None, :, :] + dx
            y0 = jnp.floor(py)
            x0 = jnp.floor(px)
            wy1 = py - y0
            wx1 = px - x0
            wy0 = 1.0 - wy1
            wx0 = 1.0 - wx1
            y0i = y0.astype(jnp.int32)
            x0i = x0.astype(jnp.int32)
            y1i = y0i + 1
            x1i = x0i + 1
            xt = x.transpose(0, 2, 3, 1)
            bidx = jnp.arange(B)[:, None, None, None]

            def gather(yi, xi):
                ok = ((yi >= 0) & (yi < H) & (xi >= 0) & (xi < W)).astype(x.dtype)
                v = xt[bidx, jnp.clip(yi, 0, H - 1), jnp.clip(xi, 0, W - 1)]
                return v * ok[..., None]
            sampled = gather(y0i, x0i) * (wy0 * wx0)[..., None] + gather(y0i, x1i) * (wy0 * wx1)[..., None] + gather(y1i, x0i) * (wy1 * wx0)[..., None] + gather(y1i, x1i) * (wy1 * wx1)[..., None]
            Wk = dconv_w.reshape(dconv_w.shape[0], C, K)
            out = jnp.einsum('bhwkc,ock->bohw', sampled, Wk)
            return out
        B = x.shape[0]
        y = _deform_conv(x, offset_w, offset_b, dconv_w)
        mean = jnp.mean(y, axis=(0, 2, 3), keepdims=True)
        var = jnp.mean((y - mean) ** 2, axis=(0, 2, 3), keepdims=True)
        yn = (y - mean) * jax.lax.rsqrt(var + EPS)
        yn = yn * bn_gamma[None, :, None, None] + bn_beta[None, :, None, None]
        ya = jax.nn.gelu(yn, approximate=False)
        O, Ho, Wo = (ya.shape[1], ya.shape[2], ya.shape[3])
        return ya.reshape(B, O, Ho * Wo).transpose(0, 2, 1)

    def _L0_attn_ref(x, Wq, Wkv, Wo_ctx, bo_ctx, Wo_lat, bo_lat, ln_g, ln_b):
        import jax, jax.numpy as jnp
        import numpy as np
        B, N, DIM, H = (8, 256, 192, 12)
        DH = DIM // H
        LATENT = 32
        EPS = 1e-05

        def _heads(t):
            b, n, _ = t.shape
            return t.reshape(b, n, H, DH).transpose(0, 2, 1, 3).reshape(b * H, n, DH)

        def _merge(t, b):
            _, n, dh = t.shape
            return t.reshape(b, H, n, dh).transpose(0, 2, 1, 3).reshape(b, n, H * dh)

        def _ln(v, g, bta):
            mu = v.mean(-1, keepdims=True)
            var = ((v - mu) ** 2).mean(-1, keepdims=True)
            return (v - mu) * jax.lax.rsqrt(var + EPS) * g + bta

        def _rope(t):
            n, dh = (t.shape[-2], t.shape[-1])
            inv = 1.0 / 10000.0 ** (jnp.arange(0, dh, 2, dtype=jnp.float32) / dh)
            f = jnp.arange(n, dtype=jnp.float32)[:, None] * inv[None, :]
            f = jnp.concatenate([f, f], -1)[None]
            x1, x2 = jnp.split(t, 2, -1)
            rot = jnp.concatenate([-x2, x1], -1)
            return t * jnp.cos(f) + rot * jnp.sin(f)
        b, n, _ = x.shape
        ctx = n - LATENT
        q = _heads(x @ Wq)
        kv = _heads(x @ Wkv)
        q = _rope(q)
        kv = _rope(kv)
        q = q * DH ** (-0.5)
        q_lat, q_ctx = (q[:, ctx:], q[:, :ctx])
        kv_ctx = kv[:, :ctx]
        lkv = _ln(kv, ln_g, ln_b)
        lkv_ctx = _ln(kv_ctx, ln_g, ln_b)
        attn_lat = jax.nn.softmax(jnp.einsum('bid,bkd->bik', q_lat, kv), axis=-1)
        attn_ctx = jax.nn.softmax(jnp.einsum('bid,bkd->bik', q_ctx, kv_ctx), axis=-1)
        out_lat = _merge(jnp.einsum('bik,bkd->bid', attn_lat, lkv), b) @ Wo_lat + bo_lat
        out_ctx = _merge(jnp.einsum('bik,bkd->bid', attn_ctx, lkv_ctx), b) @ Wo_ctx + bo_ctx
        return jnp.concatenate([out_ctx, out_lat], axis=1)

    def _L0_ffn_ref(x, Wg, W1, W2):
        import jax, jax.numpy as jnp
        import numpy as np
        E = 8
        TOP_K = 2
        CAP_RATIO = 1.2
        B, L, D = x.shape
        H = W2.shape[1]
        xf = x.reshape(-1, D)
        N = xf.shape[0]
        capacity = int(CAP_RATIO * N / E)
        logits = xf @ Wg
        scores, idx = jax.lax.top_k(logits, TOP_K)
        weights = jax.nn.softmax(scores, axis=-1)
        xpad = jnp.concatenate([xf, jnp.zeros((1, D), xf.dtype)], axis=0)
        wpad_zero = jnp.zeros((1,), weights.dtype)
        out = jnp.zeros((N, D), x.dtype)
        for k in range(TOP_K):
            ik = idx[:, k]
            onehot = ik[:, None] == jnp.arange(E)[None, :]
            pos = jnp.cumsum(onehot, axis=0) - 1
            posk = jnp.take_along_axis(pos, ik[:, None], axis=1)[:, 0]
            keep = posk < capacity
            buf = jnp.full((E, capacity), N, dtype=jnp.int32)
            buf = buf.at[ik, posk].set(jnp.arange(N, dtype=jnp.int32), mode='drop')
            xg = xpad[buf]
            h = jnp.einsum('ecd,edh->ech', xg, W1)
            act = h[..., :H] * jax.nn.silu(h[..., H:])
            ye = jnp.einsum('ech,ehd->ecd', act, W2)
            wk = jnp.where(keep, weights[:, k], 0.0)
            w_buf = jnp.concatenate([wk, wpad_zero])[buf]
            out = out.at[buf.reshape(-1)].add((w_buf[..., None] * ye).reshape(E * capacity, D), mode='drop')
        return out.reshape(B, L, D)

    def _L1_attn_ref(X, Wq, bq, Wk, bk, Wv, bv, A, id_bias, sink_scalars, v_nulls, Wo, bo):
        import math
        import jax, jax.numpy as jnp
        import numpy as np
        D_MODEL = 192
        N_HEAD = 12
        N_BR = 4
        DH = D_MODEL // N_HEAD
        H_TOT = N_BR * N_HEAD
        SCALE = math.pi / math.sqrt(3.0)
        ATTNSCALE = DH ** (-0.5)

        def _chebyshev(T, max_deg, dtype):
            if T > 1:
                x = 2.0 * jnp.arange(T, dtype=dtype) / (T - 1) - 1.0
            else:
                x = jnp.zeros(1, dtype=dtype)
            cols = [jnp.ones_like(x), x]
            for _ in range(2, max_deg + 1):
                cols.append(2.0 * x * cols[-1] - cols[-2])
            return jnp.stack(cols, axis=1)

        def _attention(X, Wq, bq, Wk, bk, Wv, bv, A, id_bias, sink_scalars, v_nulls, Wo, bo):
            B, T, C = X.shape
            dtype = X.dtype
            q = (X @ Wq.T + bq).reshape(B, T, H_TOT, DH).transpose(0, 2, 1, 3)
            v = (X @ Wv.T + bv).reshape(B, T, N_HEAD, DH).transpose(0, 2, 1, 3)
            v = jnp.tile(v, (1, N_BR, 1, 1))
            k = (X @ Wk.T + bk).reshape(B, T, N_HEAD, DH).transpose(0, 2, 1, 3)
            k = jnp.tile(k, (1, N_BR, 1, 1))
            S = (A - A.T)[None] + jax.vmap(jnp.diag)(id_bias)
            q = q + jnp.einsum('bhtd,hde->bhte', q, S)
            H = DH // 2
            max_deg = max(3, 2 * H)
            T_all = _chebyshev(T, max_deg, dtype)
            frac = jnp.arange(H, dtype=dtype) / (H - 1) if H > 1 else jnp.zeros(1, dtype)
            n_f = jnp.clip(1 + jnp.round(frac * (max_deg - 2)).astype(jnp.int32), 1, max_deg - 1)
            raw1 = T_all[:, n_f]
            raw2 = T_all[:, n_f + 1]
            nrm = jnp.sqrt(raw1 * raw1 + raw2 * raw2 + 1e-08)
            base1 = (raw1 / nrm)[None, None]
            base2 = (raw2 / nrm)[None, None]

            def apply_rot(x_in):
                x1, x2 = (x_in[..., :H], x_in[..., H:])
                return jnp.concatenate([x1 * base1 - x2 * base2, x1 * base2 + x2 * base1], axis=-1)
            q = apply_rot(q)
            k = apply_rot(k)
            scores = jnp.einsum('bhtd,bhsd->bhts', q, k) * ATTNSCALE
            key_self = jnp.maximum((k * k).sum(-1), 1e-06)
            denom = jnp.sqrt(key_self)[:, :, None, :]
            w = jax.nn.softplus(scores / denom)
            causal = jnp.tril(jnp.ones((T, T), bool))
            w = jnp.where(causal, w, 0.0)
            w = w * jax.nn.sigmoid(SCALE * w)
            sinks = sink_scalars.reshape(1, H_TOT, 1, 1)
            alpha = 1.0 / (w.sum(-1, keepdims=True) + sinks + 1e-06)
            probs_tokens = w * alpha
            probs_sink = jnp.broadcast_to(sinks, (B, H_TOT, T, 1)) * alpha
            out_tokens = jnp.einsum('bhts,bhsd->bhtd', probs_tokens, v)
            v_null = v_nulls.reshape(H_TOT, DH)[None, :, None, :]
            context = out_tokens + probs_sink * v_null
            context = context.reshape(B, N_BR, N_HEAD, T, DH)
            context = context.transpose(0, 1, 3, 2, 4).reshape(B, N_BR, T, C)
            y = jnp.einsum('bntc,ncd->bntd', context, Wo) + bo[None, :, None, :]
            return y.mean(axis=1)
        return _attention(X, Wq, bq, Wk, bk, Wv, bv, A, id_bias, sink_scalars, v_nulls, Wo, bo)

    def _L1_ffn_ref(x, Wg, bg, Wqkv, bqkv, Wproj, bproj, A, ba, Bm, bb):
        import jax, jax.numpy as jnp
        import numpy as np
        DIM = 192
        NUM_HEADS = 12
        HEAD_DIM = DIM // NUM_HEADS
        SCALE = HEAD_DIM ** (-0.5)
        NUM_EXPERTS = 8
        RANK = 16
        ALPHA = 32
        TOPK = 2
        SCALING = ALPHA / RANK
        B, S = (8, 256)
        b, s, d = x.shape
        t = b * s
        xf = x.reshape(t, d)
        probs = jax.nn.softmax(xf @ Wg.T + bg, axis=-1)
        top_w, top_idx = jax.lax.top_k(probs, TOPK)
        combine = jnp.zeros((t, NUM_EXPERTS), x.dtype).at[jnp.arange(t)[:, None], top_idx].add(top_w)
        h = jnp.einsum('td,erd->ter', xf, A) + ba
        hw = h * combine[:, :, None]
        delta = jnp.einsum('ter,eor->to', hw, Bm) + combine @ bb
        delta = delta * SCALING
        qkv = xf @ Wqkv.T + bqkv + delta
        qkv = qkv.reshape(b, s, 3, NUM_HEADS, HEAD_DIM)
        qkv = jnp.transpose(qkv, (2, 0, 3, 1, 4))
        q, k, v = (qkv[0], qkv[1], qkv[2])
        attn = jax.nn.softmax(jnp.einsum('bhsd,bhtd->bhst', q, k) * SCALE, axis=-1)
        out = jnp.einsum('bhst,bhtd->bhsd', attn, v)
        out = jnp.transpose(out, (0, 2, 1, 3)).reshape(b, s, d)
        return out @ Wproj.T + bproj

    def _L2_attn_ref(x, qkv_w, proj_w, proj_b):
        import jax, jax.numpy as jnp
        import numpy as np
        B, N, C, H = (8, 256, 192, 12)
        D = C // H
        SCALE = D ** (-0.5)

        def _norm_unbiased(t):
            mu = t.mean(axis=-1, keepdims=True)
            var = ((t - mu) ** 2).sum(axis=-1, keepdims=True) / (t.shape[-1] - 1)
            return (t - mu) / jnp.sqrt(var)
        Bn, Nn, Cn = x.shape
        qkv = x @ qkv_w.T
        qkv = qkv.reshape(Bn, Nn, 3, H, D).transpose(2, 0, 3, 1, 4)
        q, k, v = (qkv[0], qkv[1], qkv[2])
        q = _norm_unbiased(q)
        k = _norm_unbiased(k)
        attn = jax.nn.softmax(jnp.einsum('bhnd,bhmd->bhnm', q, k) * SCALE, axis=-1)
        out = jnp.einsum('bhnm,bhmd->bhnd', attn, v)
        out = out.transpose(0, 2, 1, 3).reshape(Bn, Nn, Cn)
        return out @ proj_w.T + proj_b

    def _L2_ffn_ref(hidden_states, gate_weight, Wg, Wu, Wd, Ws_g, Ws_u, Ws_d):
        import math
        import jax, jax.numpy as jnp
        import numpy as np
        B, L, D = (8, 1024, 192)
        E = 16
        TOP_K = 2
        F_EXP = 4 * D
        F_SH = F_EXP * 2 // 4
        b, l, d = hidden_states.shape
        n = b * l
        x = hidden_states.reshape(n, d)
        scores = jax.nn.sigmoid(x @ gate_weight.T)
        capacity = math.ceil(n / E * TOP_K)
        topk_score, topk_ids = jax.lax.top_k(scores.T, capacity)
        xg = x[topk_ids]
        gate = jax.nn.silu(jnp.einsum('ecd,efd->ecf', xg, Wg))
        up = jnp.einsum('ecd,efd->ecf', xg, Wu)
        out = jnp.einsum('ecf,edf->ecd', gate * up, Wd)
        out = out * topk_score[..., None]
        y = jnp.zeros((n, d), x.dtype).at[topk_ids.reshape(-1)].add(out.reshape(-1, d))
        y = y.reshape(b, l, d)
        shared = jax.nn.silu(hidden_states @ Ws_g.T) * (hidden_states @ Ws_u.T) @ Ws_d.T
        return y + shared

    def _L3_attn_ref(x, Wq, bq, Wk, bk, Wv, bv, Wp, bp):
        import jax, jax.numpy as jnp
        import numpy as np
        B, S, DIM, H = (8, 256, 192, 12)
        HD = DIM // H
        SCALE = HD ** (-0.5)

        def _split_heads(t):
            b, s, _ = t.shape
            return t.reshape(b, s, H, HD).transpose(0, 2, 1, 3)
        q = _split_heads(x @ Wq + bq)
        k = _split_heads(x @ Wk + bk)
        v = _split_heads(x @ Wv + bv)
        attn = jnp.einsum('bnqd,bnkd->bnqk', q, k) * SCALE
        attn = jax.nn.softmax(attn, axis=-1)
        o = jnp.einsum('bnqk,bnkd->bnqd', attn, v)
        o = o.transpose(0, 2, 1, 3).reshape(x.shape[0], x.shape[1], DIM)
        return o @ Wp + bp

    def _L3_ffn_ref(x, W_qkv, b_qkv, W_gate, b_gate, A, B_lora, W_proj, b_proj):
        import jax, jax.numpy as jnp
        import numpy as np
        B_SZ, S, D = (8, 128, 192)
        H = 12
        N_EXP = 8
        RANK = 16
        ALPHA = 32
        TOP_K = 2
        b, s, d = x.shape
        n_exp, rank = (A.shape[0], A.shape[1])
        scaling = ALPHA / rank
        head_dim = d // H
        scale = head_dim ** (-0.5)
        t = b * s
        x_flat = x.reshape(t, d)
        qkv_base = x @ W_qkv.T + b_qkv
        logits = x_flat @ W_gate.T + b_gate
        router_probs = jax.nn.softmax(logits, axis=-1)
        top_k_weights, top_k_indices = jax.lax.top_k(router_probs, TOP_K)
        a_down = jnp.einsum('td,nrd->tnr', x_flat, A)
        expert_out = jnp.einsum('tnr,nor->tno', a_down, B_lora) * scaling
        dispatch = jnp.zeros((t, n_exp), x.dtype).at[jnp.arange(t)[:, None], top_k_indices].add(top_k_weights)
        sparse_out = jnp.einsum('tno,tn->to', expert_out, dispatch)
        qkv = qkv_base + sparse_out.reshape(b, s, 3 * d)
        qkv = qkv.reshape(b, s, 3, H, head_dim).transpose(2, 0, 3, 1, 4)
        q, k, v = (qkv[0], qkv[1], qkv[2])
        attn = jax.nn.softmax(jnp.einsum('bhqd,bhkd->bhqk', q, k) * scale, axis=-1)
        out = jnp.einsum('bhqk,bhkd->bhqd', attn, v)
        out = out.transpose(0, 2, 1, 3).reshape(b, s, d)
        return out @ W_proj.T + b_proj
    h = _L0_tok_ref(x, L0_tok_offset_w, L0_tok_offset_b, L0_tok_dconv_w, L0_tok_bn_gamma, L0_tok_bn_beta)
    h = _layernorm(h + _L0_attn_ref(h, L0_attn_Wq, L0_attn_Wkv, L0_attn_Wo_ctx, L0_attn_bo_ctx, L0_attn_Wo_lat, L0_attn_bo_lat, L0_attn_ln_g, L0_attn_ln_b), axis=-1)
    h = _layernorm(h + _L0_ffn_ref(h, L0_ffn_Wg, L0_ffn_W1, L0_ffn_W2), axis=-1)
    h = _layernorm(h + _L1_attn_ref(h, L1_attn_Wq, L1_attn_bq, L1_attn_Wk, L1_attn_bk, L1_attn_Wv, L1_attn_bv, L1_attn_A, L1_attn_id_bias, L1_attn_sink_scalars, L1_attn_v_nulls, L1_attn_Wo, L1_attn_bo), axis=-1)
    h = _layernorm(h + _L1_ffn_ref(h, L1_ffn_Wg, L1_ffn_bg, L1_ffn_Wqkv, L1_ffn_bqkv, L1_ffn_Wproj, L1_ffn_bproj, L1_ffn_A, L1_ffn_ba, L1_ffn_Bm, L1_ffn_bb), axis=-1)
    h = _layernorm(h + _L2_attn_ref(h, L2_attn_qkv_w, L2_attn_proj_w, L2_attn_proj_b), axis=-1)
    h = _layernorm(h + _L2_ffn_ref(h, L2_ffn_gate_weight, L2_ffn_Wg, L2_ffn_Wu, L2_ffn_Wd, L2_ffn_Ws_g, L2_ffn_Ws_u, L2_ffn_Ws_d), axis=-1)
    h = _layernorm(h + _L3_attn_ref(h, L3_attn_Wq, L3_attn_bq, L3_attn_Wk, L3_attn_bk, L3_attn_Wv, L3_attn_bv, L3_attn_Wp, L3_attn_bp), axis=-1)
    h = _layernorm(h + _L3_ffn_ref(h, L3_ffn_W_qkv, L3_ffn_b_qkv, L3_ffn_W_gate, L3_ffn_b_gate, L3_ffn_A, L3_ffn_B_lora, L3_ffn_W_proj, L3_ffn_b_proj), axis=-1)
    return h

_drawn_inputs = setup_inputs


def setup_inputs(seed=0):
    import zlib

    import numpy as np

    out = dict(_drawn_inputs(seed))
    spreads = {'L0_tok_offset_b': (0.0, 0.1),
     'L0_tok_bn_gamma': (1.0, 0.2),
     'L0_tok_bn_beta': (0.0, 0.1),
     'L0_attn_bo_ctx': (0.0, 0.1),
     'L0_attn_bo_lat': (0.0, 0.1),
     'L0_attn_ln_g': (1.0, 0.2),
     'L0_attn_ln_b': (0.0, 0.1),
     'L1_attn_bo': (0.0, 0.1),
     'L3_ffn_b_qkv': (0.0, 0.1),
     'L3_ffn_b_gate': (0.0, 0.8),
     'L3_ffn_b_proj': (0.0, 0.1)}
    factors = {'L0_attn_Wq': 5.61,
     'L0_ffn_Wg': 3.649,
     'L0_ffn_W1': 3.613,
     'L0_ffn_W2': 3.479,
     'L1_attn_Wq': 8.0,
     'L1_attn_bq': 8.0,
     'L1_attn_Wk': 8.0,
     'L1_attn_bk': 8.0,
     'L1_attn_bv': 8.0,
     'L1_attn_A': 8.0,
     'L1_attn_id_bias': 8.0,
     'L1_attn_sink_scalars': 8.0,
     'L1_attn_v_nulls': 8.0,
     'L1_ffn_Wg': 7.396,
     'L1_ffn_bg': 8.0,
     'L1_ffn_bqkv': 7.001,
     'L1_ffn_A': 4.98,
     'L1_ffn_ba': 8.0,
     'L1_ffn_Bm': 5.299,
     'L1_ffn_bb': 8.0,
     'L3_attn_bq': 8.0,
     'L3_attn_bk': 8.0,
     'L3_attn_bv': 5.686,
     'L3_attn_bp': 5.817,
     'L3_ffn_W_gate': 8.0,
     'L3_ffn_A': 8.0,
     'L3_ffn_B_lora': 8.0}
    for name, (base, spread) in spreads.items():
        noise = np.random.default_rng([zlib.crc32(name.encode()), seed]).standard_normal(out[name].shape)
        drawn = base * np.exp(spread * noise) if base else spread * noise
        out[name] = jnp.asarray(drawn.astype(out[name].dtype))
    for name, factor in factors.items():
        out[name] = (out[name] * factor).astype(out[name].dtype)
    return out
```

```python
from contextlib import ExitStack, contextmanager

import numpy as np
import concourse.bass as bass
from concourse import mybir

F32 = mybir.dt.float32
ALU = mybir.AluOpType
ACT = mybir.ActivationFunctionType
AX_X = mybir.AxisListType.X

IMAGES, TOKENS, DIM = 32, 25, 192
HEADS, HEAD_DIM = 12, 16
QUAD = 32
IMG_PER_TILE = 4
P = QUAD * IMG_PER_TILE
TILES = IMAGES // IMG_PER_TILE
HALVES = 2
HALF = DIM // HALVES
GROUPS = HEADS // 4
LN_EPS = 1e-5
LATENT = 32


class Tower:

    def __init__(self, nc, ctx, ins):
        self.nc, self.ctx, self.ins = nc, ctx, ins
        self.scope, self.prefix = ctx, ""
        self.kept = {}
        self.sems = []
        self.y = self.sb("y", [P, TILES, DIM])
        self.moments = self.sb("moments", [P, TILES, 6])
        self.mean_var = self.sb("mean_var", [P, TILES, 2])
        self.rstd = self.sb("rstd", [P, TILES, 1])
        self.mean = self.sb("mean", [P, TILES, 1])
        self.identity = self.sb("identity", [P, P])
        self.eps = self.sb("eps", [P, 1])
        self.is_pad = self.sb("is_pad", [P, 1])
        self.minus_half = self.sb("minus_half", [P, 1])

    def sb(self, name, shape):
        return self.scope.enter_context(self.nc.sbuf_tensor(self.prefix + name, shape, F32))

    @contextmanager
    def scratch(self):
        outer = self.scope
        with ExitStack() as self.scope:
            yield
        self.scope = outer

    def keep(self, name, make):
        if name not in self.kept:
            self.kept[name] = make()
        return self.kept[name]

    def sem(self, name):
        s = self.nc.alloc_semaphore(name=self.prefix + name)
        self.sems.append(s)
        return s

    @contextmanager
    def stage(self, name):
        outer, self.sems = self.sems, []
        self.prefix = name
        with self.scratch():
            yield
        self.nc.clear_and_free_semaphores(self.sems)
        self.nc.all_engine_barrier()
        self.prefix, self.sems = "", outer


def setup(tw):
    nc = tw.nc
    zeroed, ready = tw.sem("identity_zeroed"), tw.sem("identity_ready")
    with nc.Block() as block:

        @block.gpsimd
        def _(pool):
            nc.gpsimd.memset(tw.identity[:], 0.0).then_inc(zeroed, 1)
            nc.gpsimd.memset(tw.eps[:], LN_EPS)
            nc.gpsimd.memset(tw.minus_half[:], -0.5)
            pool.wait_ge(zeroed, 1)
            nc.gpsimd.affine_select(out=tw.identity[:], in_=tw.identity[:], compare_op=ALU.not_equal, fill=1.0,
                                    base=0, pattern=[[-1, P]], channel_multiplier=1).then_inc(ready, 1)
            pool.wait_ge(ready, 1)


def finish_norm(tw, name):
    nc = tw.nc
    aggregated, rooted = tw.sem(name + "_aggregated"), tw.sem(name + "_rooted")
    done = tw.sem(name + "_norm_done")
    with nc.Block() as block:

        @block.vector
        def _(dve):
            for t in range(TILES):
                nc.vector.bn_aggr(tw.mean_var[:, t, :], tw.moments[:, t, :]).then_inc(aggregated, 1)
            dve.wait_ge(aggregated, TILES)
            nc.vector.tensor_copy(tw.mean[:], tw.mean_var[:, :, 0:1])
            dve.wait_ge(rooted, 1)
            nc.vector.reciprocal(tw.rstd[:], tw.rstd[:]).then_inc(done, 1)
            dve.wait_ge(done, 1)

        @block.scalar
        def _(act):
            act.wait_ge(aggregated, TILES)
            nc.scalar.activation(tw.rstd[:], tw.mean_var[:, :, 1:2], ACT.Sqrt, bias=tw.eps[:]).then_inc(rooted, 1)


class AttentionBuffers:

    NAMES = ("normed hT_in_psum hT_ready resid_ready qkv_in_psum qk_padded v_ready heads_in_psum qT_ready "
             "kT_act kT_dve scores_in_psum row_max shifted probs row_sum inv_sum probs_T out_in_psum out_normed "
             "outT_in_psum outT_ready proj_in_psum y_ready adapter_in_psum adapter_mixed mixT_in_psum mixT_ready masked "
             "y_part head_var head_rstd").split()

    def __init__(self, tw):
        sb = tw.sb
        nc, ctx = tw.nc, tw.ctx
        self.h = sb("h", [P, 2, DIM])
        self.resid = sb("resid", [P, 2, DIM])
        self.hT = sb("hT", [HALF, 2, HALVES, P])
        self.qk = sb("qk", [P, 2, 2 * HEADS, QUAD])
        self.v = sb("v", [P, 2, DIM])
        self.qT = sb("qT", [P, 2, GROUPS, P])
        self.kT = sb("kT", [P, 2, GROUPS, IMG_PER_TILE, 4, TOKENS])
        self.probs = sb("probs", [P, 2, HEADS, QUAD])
        self.pT = sb("pT", [P, 2, HEADS, P])
        self.row_max = sb("row_max", [P, 2, HEADS])
        self.row_sum = sb("row_sum", [P, 2, HEADS])
        self.inv_sum = sb("inv_sum", [P, 2, HEADS])
        self.out = sb("out", [P, 2, DIM])
        self.outT = sb("outT", [HALF, 2, HALVES, P])
        self.mix = sb("mix", [P, 2, P])
        self.mixT = sb("mixT", [P, 2, 2, P])
        self.weights = sb("mix_weights", [P, 2, 8])
        self.rotated = sb("rotated", [P, 2 * HEADS, HEAD_DIM])
        self.centred = sb("centred", [P, 2 * HEADS, HEAD_DIM])
        self.square = sb("square", [P, 2 * HEADS, HEAD_DIM])
        self.head_sum = sb("head_sum", [P, 2 * HEADS])
        self.head_var = sb("head_var", [P, 2, 2 * HEADS])
        self.head_rstd = sb("head_rstd", [P, 2, 2 * HEADS])
        self.sem = {n: tw.sem("attn_" + n) for n in self.NAMES}
        self.cleared = tw.sem("attn_cleared")
        self.base = 2

        with nc.Block() as block:

            @block.vector
            def _(dve):
                for s in self.sem.values():
                    dve.sem_inc(s, 2)
                nc.vector.memset(self.qk[:], 0.0).then_inc(self.cleared, 1)
                nc.vector.memset(self.probs[:], 0.0).then_inc(self.cleared, 1)
                nc.vector.memset(self.pT[:], 0.0).then_inc(self.cleared, 1)
                dve.wait_ge(self.cleared, 4)

            @block.gpsimd
            def _(pool):
                nc.gpsimd.memset(self.kT[:], 0.0).then_inc(self.cleared, 1)


def softmax_attention(tw, b, name, kind, wqkv, wproj, bproj, bqkv=None, adapter=None, rope=None):
    nc, base = tw.nc, b.base
    s = b.sem
    scale = HEAD_DIM ** -0.5
    head_step = tw.sem(name + "_head_step")
    steps = {"biased": 0, "adapted": 0, "rope": 8, "unit": 4}[kind]
    proj_cols = wproj.shape[2]

    def n(t):
        return base + t + 1

    with ExitStack() as ctx:
        def pb(nm, shape):
            return ctx.enter_context(nc.psum_tensor(name + nm, shape, F32))

        bank_h, bank_o = pb("bank_h", [P, 512]), pb("bank_o", [P, 512])
        ps_hT = bank_h[0:HALF, 0:HALVES * P].rearrange("q (k n) -> q k n", k=HALVES)
        ps_adapter = bank_h[:, 2 * P:3 * P]
        ps_outT = bank_o[0:HALF, 0:HALVES * P].rearrange("q (k n) -> q k n", k=HALVES)
        ps_mixT = bank_o[:, 2 * P:4 * P].rearrange("q (k n) -> q k n", k=2)
        ps_qk = pb("ps_qk", [P, 2 * HEADS, HEAD_DIM])
        bank_v = pb("bank_v", [P, 512])
        ps_v, ps_y = bank_v[:, 0:DIM], bank_v[:, 0:proj_cols]
        ps_qT = pb("ps_qT", [P, GROUPS, P])
        ps_kT = pb("ps_kT", [P, GROUPS, P])
        ps_s = pb("ps_s", [P, HEADS, TOKENS])
        ps_o = pb("ps_o", [P, DIM])

        def tiles(eng, step):
            step(0, 0, None, None)
            with eng.Fori(0, TILES - 2, 2) as i:
                step(i + 1, 1, i, 0)
                step(i + 2, 0, i + 1, 1)
            step(TILES - 1, 1, TILES - 2, 0)
            step(None, None, TILES - 1, 1)

        block = ctx.enter_context(nc.Block())

        @block.tensor
        def _(pe):
            def step(t, p, u, r):
                if t is not None:
                    pe.wait_ge(s["normed"], n(t))
                    pe.wait_ge(s["hT_ready"], n(t) - 1)
                    if kind == "adapted":
                        pe.wait_ge(s["adapter_mixed"], n(t) - 1)
                    for k in range(HALVES):
                        mm = nc.tensor.transpose(ps_hT[:, k, :], b.h[:, p, k * HALF:(k + 1) * HALF], tw.identity[:])
                    mm.then_inc(s["hT_in_psum"], 1)
                    pe.wait_ge(s["hT_ready"], n(t))
                    if kind == "adapted":
                        for k in range(HALVES):
                            mm = nc.tensor.matmul(ps_adapter, b.hT[:, p, k, :], adapter["down"][:, k, :], start=(k == 0), stop=(k == 1))
                        mm.then_inc(s["adapter_in_psum"], 1)
                        pe.wait_ge(s["adapter_mixed"], n(t))
                        nc.tensor.transpose(ps_mixT[:, 0, :], b.mix[:, p, :], tw.identity[:])
                        nc.tensor.transpose(ps_mixT[0:8, 1, :], b.weights[:, p, :], tw.identity[:]).then_inc(s["mixT_in_psum"], 1)
                        pe.wait_ge(s["mixT_ready"], n(t))
                    pe.wait_ge(s["qk_padded"], n(t) - 1)
                    pe.wait_ge(s["v_ready"], n(t) - 1)
                    if u is not None:
                        pe.wait_ge(s["y_ready"], n(u) - 1)
                    for at, ps in ((0, ps_qk[:]), (2 * DIM, ps_v)):
                        if at == 2 * DIM and kind == "rope":
                            continue
                        cols = slice(at, 2 * DIM if at == 0 else 3 * DIM)
                        adapted = kind == "adapted"
                        for k in range(HALVES):
                            mm = nc.tensor.matmul(ps, b.hT[:, p, k, :], wqkv[:, k, cols], start=(k == 0), stop=(k == 1 and not adapted))
                        if adapted:
                            mm = nc.tensor.matmul(ps, b.mixT[:, p, 0, :], adapter["up"][:, cols], start=False, stop="up_bias" not in adapter)
                            if "up_bias" in adapter:
                                mm = nc.tensor.matmul(ps, b.mixT[0:8, p, 1, :], adapter["up_bias"][:, cols], start=False, stop=True)
                    mm.then_inc(s["qkv_in_psum"], 1)
                if u is not None:
                    pe.wait_ge(s["probs_T"], n(u))
                    pe.wait_ge(s["v_ready"], n(u))
                    pe.wait_ge(s["out_normed"], n(u) - 1)
                    for h in range(HEADS):
                        mm = nc.tensor.matmul(ps_o[:, h * HEAD_DIM:(h + 1) * HEAD_DIM], b.pT[:, r, h, :],
                                              b.v[:, r, h * HEAD_DIM:(h + 1) * HEAD_DIM], start=True, stop=True)
                    mm.then_inc(s["out_in_psum"], 1)
                if t is not None:
                    pe.wait_ge(s["qk_padded"], n(t))
                    pe.wait_ge(s["qT_ready"], n(t) - 1)
                    pe.wait_ge(s["kT_act"], n(t) - 1)
                    pe.wait_ge(s["kT_dve"], n(t) - 1)
                    for g in range(GROUPS):
                        nc.tensor.transpose(ps_qT[:, g, :], b.qk[:, p, 4 * g:4 * g + 4, :], tw.identity[:])
                    for g in range(GROUPS):
                        mm = nc.tensor.transpose(ps_kT[:, g, :], b.qk[:, p, HEADS + 4 * g:HEADS + 4 * g + 4, :], tw.identity[:])
                    mm.then_inc(s["heads_in_psum"], 1)
                if u is not None:
                    pe.wait_ge(s["out_normed"], n(u))
                    pe.wait_ge(s["outT_ready"], n(u) - 1)
                    for k in range(HALVES):
                        mm = nc.tensor.transpose(ps_outT[:, k, :], b.out[:, r, k * HALF:(k + 1) * HALF], tw.identity[:])
                    mm.then_inc(s["outT_in_psum"], 1)
                if t is not None:
                    pe.wait_ge(s["qT_ready"], n(t))
                    pe.wait_ge(s["kT_act"], n(t))
                    pe.wait_ge(s["kT_dve"], n(t))
                    pe.wait_ge(s["masked" if kind == "rope" else "shifted"], n(t) - 1)
                    for g in range(GROUPS):
                        for j in range(IMG_PER_TILE):
                            mm = nc.tensor.matmul(ps_s[QUAD * j:QUAD * (j + 1), 4 * g:4 * g + 4, :],
                                                  b.qT[:, p, g, QUAD * j:QUAD * (j + 1)], b.kT[:, p, g, j, :, :],
                                                  start=True, stop=True)
                    mm.then_inc(s["scores_in_psum"], 1)
                if u is not None:
                    pe.wait_ge(s["outT_ready"], n(u))
                    pe.wait_ge(s["y_ready"], n(u) - 1)
                    if t is not None:
                        pe.wait_ge(s["v_ready"], n(t))
                    for k in range(HALVES):
                        mm = nc.tensor.matmul(ps_y, b.outT[:, r, k, :], wproj[:, k, :], start=(k == 0), stop=(k == 1))
                    mm.then_inc(s["proj_in_psum"], 1)

            tiles(pe, step)

        def spread(x, heads):
            return x.unsqueeze(2).to_broadcast([P, heads, HEAD_DIM])

        def rotate_heads(dve, t, p, qk):
            def after(ins, k):
                ins.then_inc(head_step, 1)
                dve.wait_ge(head_step, steps * t + k)

            half = HEAD_DIM // 2
            turn = lambda x, heads, cols: x[:, cols].unsqueeze(1).to_broadcast([P, heads, len(range(HEAD_DIM)[cols])])
            low, high, both = slice(0, half), slice(half, HEAD_DIM), slice(0, HEAD_DIM)
            after(nc.vector.tensor_tensor(b.rotated[:, :, low], ps_qk[:, :, high], turn(rope["sin"], 2 * HEADS, low), ALU.mult), 1)
            after(nc.vector.tensor_tensor(b.rotated[:, :, high], ps_qk[:, :, low], turn(rope["sin"], 2 * HEADS, high), ALU.mult), 2)
            after(nc.vector.tensor_tensor(qk, ps_qk[:], turn(rope["cos"], 2 * HEADS, both), ALU.mult), 3)
            nc.vector.tensor_tensor(qk, qk, b.rotated[:], ALU.add).then_inc(s["qk_padded"], 1)
            dve.wait_ge(s["qk_padded"], n(t))
            kv, c, sq = qk[:, HEADS:], b.centred[:, 0:HEADS], b.square[:, 0:HEADS]
            after(nc.vector.tensor_reduce(b.head_sum[:, 0:HEADS], kv, AX_X, ALU.add), 4)
            after(nc.vector.tensor_scalar(b.head_sum[:, 0:HEADS], b.head_sum[:, 0:HEADS], 1.0 / HEAD_DIM, None, ALU.mult), 5)
            after(nc.vector.tensor_tensor(c, kv, spread(b.head_sum[:, 0:HEADS], HEADS), ALU.subtract), 6)
            after(nc.vector.tensor_tensor(sq, c, c, ALU.mult), 7)
            after(nc.vector.tensor_reduce(b.head_sum[:, 0:HEADS], sq, AX_X, ALU.add), 8)
            nc.vector.tensor_scalar(b.head_var[:, p, 0:HEADS], b.head_sum[:, 0:HEADS], 1.0 / HEAD_DIM, LN_EPS,
                                    ALU.mult, ALU.add).then_inc(s["head_var"], 1)
            dve.wait_ge(s["head_rstd"], n(t))
            v = b.v[:, p, :].rearrange("p (h d) -> p h d", d=HEAD_DIM)
            dve.wait_ge(s["out_in_psum"], n(t) - 2)
            nc.vector.tensor_tensor(v, c, spread(b.head_rstd[:, p, 0:HEADS], HEADS), ALU.mult).then_inc(s["adapter_mixed"], 1)
            dve.wait_ge(s["adapter_mixed"], n(t))
            nc.vector.tensor_tensor(v, v, rope["gain"][:].unsqueeze(1).to_broadcast([P, HEADS, HEAD_DIM]), ALU.mult).then_inc(s["adapter_in_psum"], 1)
            dve.wait_ge(s["adapter_in_psum"], n(t))
            nc.vector.tensor_tensor(v, v, rope["shift"][:].unsqueeze(1).to_broadcast([P, HEADS, HEAD_DIM]), ALU.add).then_inc(s["v_ready"], 1)

        def unit_heads(dve, t, p, qk):
            def after(ins, k):
                ins.then_inc(head_step, 1)
                dve.wait_ge(head_step, steps * t + k)

            dve.wait_ge(s["out_in_psum"], n(t) - 2)
            nc.vector.tensor_copy(b.v[:, p, :], ps_v).then_inc(s["v_ready"], 1)
            after(nc.vector.tensor_reduce(b.head_sum[:], ps_qk[:], AX_X, ALU.add), 1)
            after(nc.vector.tensor_scalar(b.head_sum[:], b.head_sum[:], 1.0 / HEAD_DIM, None, ALU.mult), 2)
            nc.vector.tensor_tensor(b.centred[:], ps_qk[:], spread(b.head_sum[:], 2 * HEADS), ALU.subtract).then_inc(s["masked"], 1)
            dve.wait_ge(s["masked"], n(t))
            after(nc.vector.tensor_tensor(b.square[:], b.centred[:], b.centred[:], ALU.mult), 3)
            after(nc.vector.tensor_reduce(b.head_sum[:], b.square[:], AX_X, ALU.add), 4)
            nc.vector.tensor_scalar(b.head_var[:, p, :], b.head_sum[:], 1.0 / (HEAD_DIM - 1), tw.is_pad[:],
                                    ALU.mult, ALU.add).then_inc(s["head_var"], 1)
            dve.wait_ge(s["head_rstd"], n(t))
            nc.vector.tensor_tensor(qk, b.centred[:], spread(b.head_rstd[:, p, :], 2 * HEADS), ALU.mult).then_inc(s["qk_padded"], 1)

        @block.vector
        def _(dve):
            def step(t, p, u, r):
                if u is not None:
                    dve.wait_ge(s["scores_in_psum"], n(u))
                    scores = ps_s[:]
                    if kind == "rope":
                        scores = b.probs[:, r, :, 0:TOKENS]
                        nc.vector.tensor_tensor(scores, ps_s[:], rope["mask"][:].unsqueeze(1).to_broadcast([P, HEADS, TOKENS]),
                                                ALU.add).then_inc(s["masked"], 1)
                        dve.wait_ge(s["masked"], n(u))
                    nc.vector.tensor_reduce(b.row_max[:, r, :], scores, AX_X, ALU.max).then_inc(s["row_max"], 1)
                    dve.wait_ge(s["row_max"], n(u))
                    nc.vector.tensor_tensor(b.probs[:, r, :, 0:TOKENS], scores,
                                            b.row_max[:, r, :].unsqueeze(2).to_broadcast([P, HEADS, TOKENS]),
                                            ALU.subtract).then_inc(s["shifted"], 1)
                if t is not None:
                    dve.wait_ge(s["hT_in_psum"], n(t) - 2)
                    dve.wait_ge(s["resid_ready"], n(t) - 2)
                    nc.vector.tensor_scalar(b.h[:, p, :], tw.y[:, t, :], tw.mean[:, t, :], tw.rstd[:, t, :],
                                            ALU.subtract, ALU.mult).then_inc(s["normed"], 1)
                if u is not None:
                    dve.wait_ge(s["probs"], n(u))
                    nc.vector.tensor_reduce(b.row_sum[:, r, :], b.probs[:, r, :, 0:TOKENS], AX_X, ALU.add).then_inc(s["row_sum"], 1)
                    dve.wait_ge(s["out_in_psum"], n(u) - 2)
                    for j in range(IMG_PER_TILE):
                        q = slice(QUAD * j, QUAD * (j + 1))
                        ins = nc.vector.transpose(b.pT[q, r, :, q], b.probs[q, r, :, :])
                    ins.then_inc(s["probs_T"], 1)
                    dve.wait_ge(s["row_sum"], n(u))
                    nc.vector.reciprocal(b.inv_sum[:, r, :], b.row_sum[:, r, :]).then_inc(s["inv_sum"], 1)
                if t is not None:
                    if kind == "adapted":
                        dve.wait_ge(s["adapter_in_psum"], n(t))
                        dve.wait_ge(s["mixT_in_psum"], n(t) - 2)
                        mix, source = b.mix[:, p, :], ps_adapter
                        if "down_bias" in adapter:
                            nc.vector.tensor_tensor(mix, source, adapter["down_bias"][:], ALU.add).then_inc(s["masked"], 1)
                            dve.wait_ge(s["masked"], n(t))
                            source = mix
                        nc.vector.tensor_copy(b.weights[:, p, :], adapter["combine"][:, t, :])
                        nc.vector.tensor_tensor(mix.rearrange("p (e r) -> p e r", e=8), source.rearrange("p (e r) -> p e r", e=8),
                                                adapter["combine"][:, t, :].unsqueeze(2).to_broadcast([P, 8, P // 8]),
                                                ALU.mult).then_inc(s["adapter_mixed"], 1)
                    dve.wait_ge(s["qkv_in_psum"], n(t))
                    dve.wait_ge(s["heads_in_psum"], n(t) - 2)
                    heads_of = lambda x: x.rearrange("p (h d) -> p h d", d=HEAD_DIM)
                    qk = b.qk[:, p, :, 0:HEAD_DIM]
                    if bqkv is not None:
                        nc.vector.tensor_tensor(qk, ps_qk[:], heads_of(bqkv[:, 0:2 * DIM]), ALU.add).then_inc(s["qk_padded"], 1)
                        nc.vector.tensor_tensor(b.v[:, p, :], ps_v, bqkv[:, 2 * DIM:3 * DIM], ALU.add).then_inc(s["v_ready"], 1)
                    if kind == "rope":
                        rotate_heads(dve, t, p, qk)
                    if kind == "unit":
                        unit_heads(dve, t, p, qk)
                if u is not None:
                    dve.wait_ge(s["out_in_psum"], n(u))
                    dve.wait_ge(s["outT_in_psum"], n(u) - 2)
                    dve.wait_ge(s["inv_sum"], n(u))
                    nc.vector.tensor_tensor(b.out[:, r, :].rearrange("p (h d) -> p h d", d=HEAD_DIM),
                                            ps_o[:].rearrange("p (h d) -> p h d", d=HEAD_DIM),
                                            b.inv_sum[:, r, :].unsqueeze(2).to_broadcast([P, HEADS, HEAD_DIM]),
                                            ALU.mult).then_inc(s["out_normed"], 1)
                if t is not None:
                    dve.wait_ge(s["heads_in_psum"], n(t))
                    dve.wait_ge(s["scores_in_psum"], n(t) - 2)
                    for a in (2, 3):
                        q = slice(QUAD * a, QUAD * (a + 1))
                        ins = nc.vector.tensor_copy(b.kT[q, p, :, :, a, :],
                                                    ps_kT[q, :, :].rearrange("p g (j n) -> p g j n", n=QUAD)[:, :, :, 0:TOKENS])
                    ins.then_inc(s["kT_dve"], 1)
                if u is not None:
                    dve.wait_ge(s["proj_in_psum"], n(u))
                    dve.wait_ge(s["resid_ready"], n(u))
                    if kind == "rope":
                        nc.vector.scalar_tensor_tensor(out=b.resid[:, r, :], in0=ps_y[:, 0:DIM], scalar=rope["context"][:], in1=b.resid[:, r, :],
                                                       op0=ALU.mult, op1=ALU.add).then_inc(s["y_part"], 1)
                        dve.wait_ge(s["y_part"], n(u))
                        nc.vector.scalar_tensor_tensor(out=tw.y[:, u, :], in0=ps_y[:, DIM:2 * DIM], scalar=rope["latent"][:], in1=b.resid[:, r, :],
                                                       op0=ALU.mult, op1=ALU.add).then_inc(s["y_ready"], 1)
                    else:
                        nc.vector.tensor_tensor(tw.y[:, u, :], ps_y, b.resid[:, r, :], ALU.add).then_inc(s["y_ready"], 1)
                    dve.wait_ge(s["y_ready"], n(u))
                    nc.vector.bn_stats(tw.moments[:, u, :], tw.y[:, u, :])

            tiles(dve, step)

        @block.scalar
        def _(act):
            def step(t, p, u, r):
                if u is not None:
                    act.wait_ge(s["shifted"], n(u))
                    nc.scalar.activation(b.probs[:, r, :, 0:TOKENS], b.probs[:, r, :, 0:TOKENS], ACT.Exp,
                                         scale=scale).then_inc(s["probs"], 1)
                if t is not None:
                    act.wait_ge(s["hT_in_psum"], n(t))
                    act.wait_ge(s["qkv_in_psum"], n(t) - 2)
                    nc.scalar.copy(b.hT[:, p, :, :], ps_hT[:]).then_inc(s["hT_ready"], 1)
                    if kind == "adapted":
                        act.wait_ge(s["mixT_in_psum"], n(t))
                        nc.scalar.copy(b.mixT[:, p, 0, :], ps_mixT[:, 0, :])
                        nc.scalar.copy(b.mixT[0:8, p, 1, :], ps_mixT[0:8, 1, :]).then_inc(s["mixT_ready"], 1)
                    act.wait_ge(s["heads_in_psum"], n(t))
                    act.wait_ge(s["scores_in_psum"], n(t) - 2)
                    nc.scalar.copy(b.qT[:, p, :, :], ps_qT[:]).then_inc(s["qT_ready"], 1)
                    for a in (0, 1):
                        q = slice(QUAD * a, QUAD * (a + 1))
                        ins = nc.scalar.copy(b.kT[q, p, :, :, a, :],
                                             ps_kT[q, :, :].rearrange("p g (j n) -> p g j n", n=QUAD)[:, :, :, 0:TOKENS])
                    ins.then_inc(s["kT_act"], 1)
                if u is not None:
                    act.wait_ge(s["outT_in_psum"], n(u))
                    act.wait_ge(s["proj_in_psum"], n(u) - 2)
                    nc.scalar.copy(b.outT[:, r, :, :], ps_outT[:]).then_inc(s["outT_ready"], 1)

            tiles(act, step)

        @block.gpsimd
        def _(pool):
            def step(t, p, u, r):
                if t is not None:
                    pool.wait_ge(s["normed"], n(t))
                    pool.wait_ge(s["y_ready"], n(t) - 2)
                    nc.gpsimd.tensor_tensor(b.resid[:, p, :], b.h[:, p, :], bproj[:], ALU.add).then_inc(s["resid_ready"], 1)
                    if kind in ("rope", "unit"):
                        heads = HEADS if kind == "rope" else 2 * HEADS
                        pool.wait_ge(s["head_var"], n(t))
                        nc.gpsimd.tensor_tensor(b.head_rstd[:, p, 0:heads], b.head_var[:, p, 0:heads], tw.minus_half[:].to_broadcast([P, heads]),
                                                ALU.pow).then_inc(s["head_rstd"], 1)

            tiles(pool, step)


BRANCHES = 4
ALL_HEADS = BRANCHES * HEADS


def branch_attention(tw, name, w):
    nc = tw.nc
    names = ("prep_s prep_m prep_w prep_b prep_done normed hT_in_psum hT_ready resid_ready proj_in_psum biased turned low high "
             "rotated key_square key_sum key_var key_rstd qk_ready v_ready heads_in_psum qT_ready kT_act kT_dve scores_in_psum "
             "magnitude exp log softplus masked gate_exp gate_one gate_inv weights row_sum sunk inv_sum wT out_in_psum out_part "
             "out_ready outT_in_psum outT_ready y_in_psum y_ready resid_scaled floored cleared cleared_pool").split()
    s = {k: tw.sem(name + "_" + k) for k in names}
    QK = ALL_HEADS + HEADS
    KG = ALL_HEADS // 4
    PREP = ALL_HEADS * HEAD_DIM // P
    gate_scale = float(np.pi / np.sqrt(3.0))

    def n(t):
        return 2 + t + 1

    def tiles(eng, step):
        step(0, 0, None, None)
        with eng.Fori(0, TILES - 2, 2) as i:
            step(i + 1, 1, i, 0)
            step(i + 2, 0, i + 1, 1)
        step(TILES - 1, 1, TILES - 2, 0)
        step(None, None, TILES - 1, 1)

    def per_head(x):
        return x.rearrange("p (h d) -> p h d", d=HEAD_DIM)

    with ExitStack() as ctx:
        def sb(nm, shape):
            return ctx.enter_context(nc.sbuf_tensor(name + nm, shape, F32))

        def pb(nm, shape):
            return ctx.enter_context(nc.psum_tensor(name + nm, shape, F32))

        mix = sb("mix", [P, PREP, P])
        eye_a = sb("eye_a", [P, P])
        wq = sb("wq", [HALF, HALVES, ALL_HEADS * HEAD_DIM])
        bias = sb("bias", [P, QK * HEAD_DIM])
        bo = sb("bo", [P, DIM])
        sink_v = sb("sink_v", [P, ALL_HEADS * HEAD_DIM])
        h = sb("h", [P, 2, DIM])
        resid = sb("resid", [P, 2, DIM])
        hT = sb("hT", [HALF, 2, HALVES, P])
        flat = sb("flat", [P, QK, HEAD_DIM])
        swapped = sb("swapped", [P, QK, HEAD_DIM])
        key_sq = sb("key_sq", [P, HEADS, HEAD_DIM])
        key_var = sb("key_var", [P, HEADS])
        key_rstd = sb("key_rstd", [P, HEADS])
        qk = sb("qk", [P, QK, QUAD])
        v = sb("v", [P, 2, DIM])
        qT = sb("qT", [P, KG, P])
        kT = sb("kT", [P, GROUPS, IMG_PER_TILE, 4, TOKENS])
        work = sb("work", [P, ALL_HEADS, TOKENS])
        weight = sb("weight", [P, ALL_HEADS, QUAD])
        wT = sb("wT", [P, ALL_HEADS, P])
        row_sum = sb("row_sum", [P, ALL_HEADS])
        inv_sum = sb("inv_sum", [P, ALL_HEADS])
        out = sb("out", [P, BRANCHES, DIM])
        outT = sb("outT", [HALF, BRANCHES, HALVES, P])

        turn_bank = pb("turn_bank", [P, 4, 512])
        bank_h = pb("bank_h", [P, 512])
        bank_t = pb("bank_t", [P, 512])
        bank_o = pb("bank_o", [P, 2, 512])
        ps_hT = bank_h[0:HALF, 0:HALVES * P].rearrange("q (k n) -> q k n", k=HALVES)
        ps_s = turn_bank[:, :, 0:HEADS * TOKENS]
        def work_rows(x):
            return x[:].rearrange("p (c h) n -> p c (h n)", c=BRANCHES)

        block = ctx.enter_context(nc.Block())

        @block.tensor
        def _(pe):
            pe.wait_ge(s["prep_m"], PREP)
            for g in range(PREP):
                if g:
                    pe.wait_ge(s["prep_b"], g)
                for k in range(HALVES):
                    nc.tensor.matmul(turn_bank[0:HALF, 0, k * P:(k + 1) * P], w["Wq"][:, g, k * HALF:(k + 1) * HALF], mix[:, g, :],
                                     start=True, stop=True)
                nc.tensor.matmul(turn_bank[:, 0, 2 * P:3 * P], w["bq"][:, g:g + 1].to_broadcast([P, P]), mix[:, g, :],
                                 start=True, stop=True).then_inc(s["prep_w"], 1)
            pe.wait_ge(s["prep_b"], PREP)
            pe.wait_ge(s["prep_done"], 1)

            def step(t, p, u, r):
                if t is not None:
                    pe.wait_ge(s["normed"], n(t))
                    pe.wait_ge(s["hT_ready"], n(t) - 1)
                    for k in range(HALVES):
                        mm = nc.tensor.transpose(ps_hT[:, k, :], h[:, p, k * HALF:(k + 1) * HALF], tw.identity[:])
                    mm.then_inc(s["hT_in_psum"], 1)
                    pe.wait_ge(s["hT_ready"], n(t))
                    pe.wait_ge(s["softplus"], n(t) - 1)
                    pe.wait_ge(s["magnitude"], n(t) - 1)
                    for c in range(3):
                        for k in range(HALVES):
                            rhs = wq[:, k, c * 2 * DIM:(c + 1) * 2 * DIM] if c < 2 else w["Wkv"][:, k, :]
                            mm = nc.tensor.matmul(turn_bank[:, c, 0:2 * DIM], hT[:, p, k, :], rhs, start=(k == 0), stop=(k == 1))
                    mm.then_inc(s["proj_in_psum"], 1)

                def values(branches):
                    for c in branches:
                        for hd in range(HEADS):
                            at = (c % 2) * DIM + hd * HEAD_DIM
                            mm = nc.tensor.matmul(bank_o[:, c // 2, at:at + HEAD_DIM], wT[:, c * HEADS + hd, :],
                                                  v[:, r, hd * HEAD_DIM:(hd + 1) * HEAD_DIM], start=True, stop=True)
                    mm.then_inc(s["out_in_psum"], 1)

                if u is not None:
                    pe.wait_ge(s["wT"], n(u))
                    pe.wait_ge(s["y_ready"], n(u) - 1)
                    values((0, 1))
                if t is not None:
                    pe.wait_ge(s["qk_ready"], n(t))
                    pe.wait_ge(s["v_ready"], n(t))
                    for g in range(KG + GROUPS):
                        mm = nc.tensor.transpose(turn_bank[:, g // 4, (g % 4) * P:(g % 4 + 1) * P], qk[:, 4 * g:4 * g + 4, :], tw.identity[:])
                    mm.then_inc(s["heads_in_psum"], 1)
                if u is not None:
                    values((2, 3))
                    for half in range(2):
                        pe.wait_ge(s["out_ready"], 2 * n(u) - 1 + half)
                        pe.wait_ge(s["outT_ready"], 2 * n(u) - 2 + half)
                        for c in (2 * half, 2 * half + 1):
                            for k in range(HALVES):
                                at = ((c % 2) * HALVES + k) * P
                                mm = nc.tensor.transpose(bank_t[0:HALF, at:at + P], out[:, c, k * HALF:(k + 1) * HALF], tw.identity[:])
                        mm.then_inc(s["outT_in_psum"], 1)
                if t is not None:
                    pe.wait_ge(s["qT_ready"], n(t))
                    pe.wait_ge(s["kT_act"], n(t))
                    pe.wait_ge(s["kT_dve"], n(t))
                    for g in range(KG):
                        for j in range(IMG_PER_TILE):
                            mm = nc.tensor.matmul(ps_s[QUAD * j:QUAD * (j + 1), g // GROUPS, (g % GROUPS) * 4 * TOKENS:(g % GROUPS + 1) * 4 * TOKENS],
                                                  qT[:, g, QUAD * j:QUAD * (j + 1)], kT[:, g % GROUPS, j, :, :], start=True, stop=True)
                    mm.then_inc(s["scores_in_psum"], 1)
                if u is not None:
                    pe.wait_ge(s["outT_ready"], 2 * n(u))
                    for c in range(BRANCHES):
                        for k in range(HALVES):
                            mm = nc.tensor.matmul(bank_o[:, 0, 0:DIM], outT[:, c, k, :], w["Wo"][:, c, k, :],
                                                  start=(c == 0 and k == 0), stop=(c == BRANCHES - 1 and k == 1))
                    mm.then_inc(s["y_in_psum"], 1)

            tiles(pe, step)

        @block.vector
        def _(dve):
            for k in names[names.index("normed"):names.index("cleared")]:
                dve.sem_inc(s[k], 4 if k in ("out_part", "out_ready", "outT_ready", "out_in_psum", "outT_in_psum") else 2)
            nc.vector.tensor_tensor(eye_a[:], w["A"][:], w["AT"][:], ALU.subtract).then_inc(s["prep_s"], 1)
            dve.wait_ge(s["prep_s"], 1)
            nc.vector.tensor_tensor(eye_a[:], eye_a[:], tw.identity[:], ALU.add).then_inc(s["prep_s"], 1)
            dve.wait_ge(s["prep_s"], 2)
            for g in range(PREP):
                nc.vector.scalar_tensor_tensor(out=mix[:, g, :], in0=tw.identity[:], scalar=w["diagonal"][:, g:g + 1], in1=eye_a[:],
                                               op0=ALU.mult, op1=ALU.add).then_inc(s["prep_m"], 1)
            for g in range(PREP):
                dve.wait_ge(s["prep_w"], g + 1)
                nc.vector.tensor_copy(wq[:, :, g * P:(g + 1) * P], turn_bank[0:HALF, 0, 0:2 * P].rearrange("q (k n) -> q k n", k=HALVES))
                nc.vector.tensor_copy(bias[:, g * P:(g + 1) * P], turn_bank[:, 0, 2 * P:3 * P]).then_inc(s["prep_b"], 1)
            nc.vector.tensor_copy(bias[:, ALL_HEADS * HEAD_DIM:], w["bk"][:]).then_inc(s["prep_s"], 1)
            nc.vector.tensor_tensor(per_head(sink_v[:]), per_head(w["v_null"][:]), w["sink"][:].unsqueeze(2).to_broadcast([P, ALL_HEADS, HEAD_DIM]),
                                    ALU.mult).then_inc(s["prep_s"], 1)
            nc.vector.tensor_tensor(bo[:], w["bo"][:, 0:DIM], w["bo"][:, DIM:2 * DIM], ALU.add).then_inc(s["prep_s"], 1)
            for c in (2, 3):
                dve.wait_ge(s["prep_s"], 3 + c)
                nc.vector.tensor_tensor(bo[:], bo[:], w["bo"][:, c * DIM:(c + 1) * DIM], ALU.add).then_inc(s["prep_s"], 1)
            dve.wait_ge(s["prep_s"], 7)
            nc.vector.tensor_scalar(bo[:], bo[:], 1.0 / BRANCHES, None, ALU.mult).then_inc(s["prep_s"], 1)
            nc.vector.memset(weight[:], 0.0).then_inc(s["prep_s"], 1)
            dve.wait_ge(s["prep_s"], 9)
            dve.wait_ge(s["cleared"], 1)
            dve.wait_ge(s["prep_b"], PREP)
            dve.sem_inc(s["prep_done"], 1)

            def step(t, p, u, r):
                wts = weight[:, :, 0:TOKENS]
                if u is not None:
                    dve.wait_ge(s["log"], n(u))
                    nc.vector.scalar_tensor_tensor(out=work_rows(work), in0=ps_s, scalar=0.0, in1=work_rows(work),
                                                   op0=ALU.max, op1=ALU.add).then_inc(s["softplus"], 1)
                    dve.wait_ge(s["softplus"], n(u))
                    nc.vector.tensor_tensor(wts, work[:], w["causal"][:].unsqueeze(1).to_broadcast([P, ALL_HEADS, TOKENS]),
                                            ALU.mult).then_inc(s["masked"], 1)
                if t is not None:
                    dve.wait_ge(s["hT_in_psum"], n(t) - 2)
                    dve.wait_ge(s["resid_ready"], n(t) - 2)
                    nc.vector.tensor_scalar(h[:, p, :], tw.y[:, t, :], tw.mean[:, t, :], tw.rstd[:, t, :],
                                            ALU.subtract, ALU.mult).then_inc(s["normed"], 1)
                if u is not None:
                    dve.wait_ge(s["gate_exp"], n(u))
                    nc.vector.tensor_scalar(work[:], work[:], 1.0, None, ALU.add).then_inc(s["gate_one"], 1)
                    dve.wait_ge(s["gate_one"], n(u))
                    nc.vector.reciprocal(work[:], work[:]).then_inc(s["gate_inv"], 1)
                    dve.wait_ge(s["gate_inv"], n(u))
                    nc.vector.tensor_tensor(wts, wts, work[:], ALU.mult).then_inc(s["weights"], 1)
                    dve.wait_ge(s["weights"], n(u))
                    nc.vector.tensor_reduce(row_sum[:], wts, AX_X, ALU.add).then_inc(s["row_sum"], 1)
                    dve.wait_ge(s["out_in_psum"], 2 * n(u) - 2)
                    for j in range(IMG_PER_TILE):
                        q = slice(QUAD * j, QUAD * (j + 1))
                        ins = nc.vector.transpose(wT[q, :, q], weight[q, :, :])
                    ins.then_inc(s["wT"], 1)
                    dve.wait_ge(s["row_sum"], n(u))
                    nc.vector.tensor_tensor(row_sum[:], row_sum[:], w["sink"][:], ALU.add).then_inc(s["sunk"], 1)
                    dve.wait_ge(s["sunk"], n(u))
                    nc.vector.tensor_scalar(row_sum[:], row_sum[:], 1e-6, None, ALU.add).then_inc(s["floored"], 1)
                    dve.wait_ge(s["floored"], n(u))
                    nc.vector.reciprocal(inv_sum[:], row_sum[:]).then_inc(s["inv_sum"], 1)
                    dve.wait_ge(s["inv_sum"], n(u))
                if t is not None:
                    dve.wait_ge(s["proj_in_psum"], n(t))
                    dve.wait_ge(s["rotated"], n(t) - 1)
                    for c in range(3):
                        heads = 2 * HEADS if c < 2 else HEADS
                        at = slice(c * 2 * HEADS, c * 2 * HEADS + heads)
                        ins = nc.vector.tensor_tensor(flat[:, at, :], per_head(turn_bank[:, c, 0:heads * HEAD_DIM]),
                                                      per_head(bias[:])[:, at, :], ALU.add)
                    ins.then_inc(s["biased"], 1)
                    dve.wait_ge(s["out_in_psum"], 2 * n(t) - 4)
                    nc.vector.tensor_tensor(v[:, p, :], turn_bank[:, 2, DIM:2 * DIM], w["bv"][:], ALU.add).then_inc(s["v_ready"], 1)
                    half = HEAD_DIM // 2
                    lo, hi = slice(0, half), slice(half, HEAD_DIM)
                    table = lambda x, cols: x[:, cols].unsqueeze(1).to_broadcast([P, QK, len(range(HEAD_DIM)[cols])])
                    dve.wait_ge(s["biased"], n(t))
                    nc.vector.tensor_tensor(swapped[:, :, lo], flat[:, :, hi], table(w["sin"], lo), ALU.mult).then_inc(s["low"], 1)
                    nc.vector.tensor_tensor(swapped[:, :, hi], flat[:, :, lo], table(w["sin"], hi), ALU.mult).then_inc(s["high"], 1)
                    dve.wait_ge(s["low"], n(t))
                    dve.wait_ge(s["high"], n(t))
                    nc.vector.tensor_tensor(flat[:], flat[:], table(w["cos"], slice(0, HEAD_DIM)), ALU.mult).then_inc(s["turned"], 1)
                    dve.wait_ge(s["turned"], n(t))
                    dve.wait_ge(s["heads_in_psum"], n(t) - 1)
                    nc.vector.tensor_tensor(qk[:, :, 0:HEAD_DIM], flat[:], swapped[:], ALU.add).then_inc(s["rotated"], 1)
                    dve.wait_ge(s["rotated"], n(t))
                    keys = qk[:, ALL_HEADS:, 0:HEAD_DIM]
                    nc.vector.tensor_tensor(key_sq[:], keys, keys, ALU.mult).then_inc(s["key_square"], 1)
                    dve.wait_ge(s["key_square"], n(t))
                    nc.vector.tensor_reduce(key_var[:], key_sq[:], AX_X, ALU.add).then_inc(s["key_sum"], 1)
                    dve.wait_ge(s["key_sum"], n(t))
                    nc.vector.tensor_scalar(key_var[:], key_var[:], 1e-6, None, ALU.max).then_inc(s["key_var"], 1)
                    dve.wait_ge(s["key_rstd"], n(t))
                    nc.vector.tensor_scalar(key_rstd[:], key_rstd[:], HEAD_DIM ** -0.5, None, ALU.mult).then_inc(s["resid_scaled"], 1)
                    dve.wait_ge(s["resid_scaled"], n(t))
                    nc.vector.tensor_tensor(keys, keys, key_rstd[:].unsqueeze(2).to_broadcast([P, HEADS, HEAD_DIM]), ALU.mult).then_inc(s["qk_ready"], 1)

                def outputs(half):
                    dve.wait_ge(s["out_in_psum"], 2 * n(u) - 1 + half)
                    dve.wait_ge(s["outT_in_psum"], 2 * n(u) - 3 + half)
                    o = out[:, 2 * half:2 * half + 2, :].rearrange("p c n -> p (c n)")
                    cols = slice(2 * half * DIM, 2 * (half + 1) * DIM)
                    nc.vector.tensor_tensor(o, bank_o[:, half, 0:2 * DIM], sink_v[:, cols], ALU.add).then_inc(s["out_part"], 1)
                    dve.wait_ge(s["out_part"], 2 * n(u) - 1 + half)
                    nc.vector.tensor_tensor(per_head(o), per_head(o), inv_sum[:, 2 * half * HEADS:2 * (half + 1) * HEADS].unsqueeze(2).to_broadcast([P, 2 * HEADS, HEAD_DIM]),
                                            ALU.mult).then_inc(s["out_ready"], 1)

                if u is not None:
                    outputs(0)
                if t is not None:
                    dve.wait_ge(s["heads_in_psum"], n(t))
                    dve.wait_ge(s["scores_in_psum"], n(t) - 1)
                    for a in (2, 3):
                        q = slice(QUAD * a, QUAD * (a + 1))
                        ins = nc.vector.tensor_copy(kT[q, :, :, a, :], turn_bank[q, 3, 0:GROUPS * P].rearrange("p (g j n) -> p (g j) n", g=GROUPS, n=QUAD)[:, :, 0:TOKENS]
                                                    .rearrange("p (g j) n -> p g j n", g=GROUPS))
                    ins.then_inc(s["kT_dve"], 1)
                if u is not None:
                    outputs(1)
                    dve.wait_ge(s["y_in_psum"], n(u))
                    dve.wait_ge(s["resid_ready"], n(u))
                    nc.vector.scalar_tensor_tensor(out=tw.y[:, u, :], in0=bank_o[:, 0, 0:DIM], scalar=1.0 / BRANCHES, in1=resid[:, r, :],
                                                   op0=ALU.mult, op1=ALU.add).then_inc(s["y_ready"], 1)
                    dve.wait_ge(s["y_ready"], n(u))
                    nc.vector.bn_stats(tw.moments[:, u, :], tw.y[:, u, :])

            tiles(dve, step)

        @block.scalar
        def _(act):
            def step(t, p, u, r):
                if u is not None:
                    act.wait_ge(s["scores_in_psum"], n(u))
                    act.wait_ge(s["weights"], n(u) - 1)
                    nc.scalar.activation(work_rows(work), ps_s, ACT.Abs).then_inc(s["magnitude"], 1)
                    act.wait_ge(s["magnitude"], n(u))
                    nc.scalar.activation(work[:], work[:], ACT.Exp, scale=-1.0).then_inc(s["exp"], 1)
                    act.wait_ge(s["exp"], n(u))
                    nc.scalar.activation(work[:], work[:], ACT.Ln, bias=1.0).then_inc(s["log"], 1)
                    act.wait_ge(s["masked"], n(u))
                    nc.scalar.activation(work[:], weight[:, :, 0:TOKENS], ACT.Exp, scale=-gate_scale).then_inc(s["gate_exp"], 1)
                if t is not None:
                    act.wait_ge(s["hT_in_psum"], n(t))
                    act.wait_ge(s["proj_in_psum"], n(t) - 2)
                    nc.scalar.copy(hT[:, p, :, :], ps_hT).then_inc(s["hT_ready"], 1)
                    act.wait_ge(s["heads_in_psum"], n(t))
                    act.wait_ge(s["scores_in_psum"], n(t) - 1)
                    for c in range(3):
                        ins = nc.scalar.copy(qT[:, 4 * c:4 * c + 4, :].rearrange("p g n -> p (g n)"), turn_bank[:, c, :])
                    ins.then_inc(s["qT_ready"], 1)
                    for a in (0, 1):
                        q = slice(QUAD * a, QUAD * (a + 1))
                        ins = nc.scalar.copy(kT[q, :, :, a, :], turn_bank[q, 3, 0:GROUPS * P].rearrange("p (g j n) -> p (g j) n", g=GROUPS, n=QUAD)[:, :, 0:TOKENS]
                                             .rearrange("p (g j) n -> p g j n", g=GROUPS))
                    ins.then_inc(s["kT_act"], 1)
                if u is not None:
                    for half in range(2):
                        act.wait_ge(s["outT_in_psum"], 2 * n(u) - 1 + half)
                        if half == 0:
                            act.wait_ge(s["y_in_psum"], n(u) - 1)
                        nc.scalar.copy(outT[:, 2 * half:2 * half + 2].rearrange("q c k n -> q (c k n)"), bank_t[0:HALF, :]).then_inc(s["outT_ready"], 1)

            tiles(act, step)

        @block.gpsimd
        def _(pool):
            nc.gpsimd.memset(kT[:], 0.0).then_inc(s["cleared_pool"], 1)
            nc.gpsimd.memset(qk[:], 0.0).then_inc(s["cleared_pool"], 1)
            nc.gpsimd.memset(wT[:], 0.0).then_inc(s["cleared_pool"], 1)
            pool.wait_ge(s["cleared_pool"], 3)
            pool.sem_inc(s["cleared"], 1)
            pool.wait_ge(s["prep_done"], 1)

            def step(t, p, u, r):
                if t is not None:
                    pool.wait_ge(s["normed"], n(t))
                    pool.wait_ge(s["y_ready"], n(t) - 2)
                    nc.gpsimd.tensor_tensor(resid[:, p, :], h[:, p, :], bo[:], ALU.add).then_inc(s["resid_ready"], 1)
                    pool.wait_ge(s["key_var"], n(t))
                    nc.gpsimd.tensor_tensor(key_rstd[:], key_var[:], tw.minus_half[:].to_broadcast([P, HEADS]), ALU.pow).then_inc(s["key_rstd"], 1)

            tiles(pool, step)


PATCH = 16
GRID = 5
TILE_TOKENS = IMG_PER_TILE * TOKENS
KPOINTS = PATCH * PATCH
KHALVES = KPOINTS // P
CHANNELS = 3
IMAGE = 84
MARGIN = 3
WINDOW = PATCH + 2 * MARGIN
COVER = -(-IMAGE // WINDOW)
PADDED = MARGIN + COVER * WINDOW
SLABS = CHANNELS * KPOINTS // P


def offsets(tw, k, w):
    nc, ins = tw.nc, tw.ins
    names = "patches_used conv_in_psum biased pos rel_y rel_x range turned posT rel_saved".split()
    s = {x: tw.sem("offsets_" + x) for x in names}
    loaded = [tw.sem(f"offsets_patches_loaded_{p}") for p in range(2)]
    saved = [tw.sem(f"offsets_rel_saved_{p}") for p in range(2)]
    B = 2

    def n(t):
        return B + t + 1

    def tiles(eng, step):
        with eng.Fori(0, TILES // 2) as pair:
            step(2 * pair, 0, pair)
            step(2 * pair + 1, 1, pair)

    with tw.scratch(), nc.psum_tensor("ps_conv", [P, 2, 512], F32) as ps_conv, nc.psum_tensor("ps_turn", [P, 2, 512], F32) as ps_turn:
        patches = tw.sb("patches", [P, 2, SLABS, TILE_TOKENS])
        pos = tw.sb("pos", [TILE_TOKENS, 2, 2, KPOINTS])
        rel = tw.sb("rel", [TILE_TOKENS, 2, 2, KPOINTS])
        with nc.Block() as block:

            @block.sync
            def _(sp):
                src = ins["patchesT"].rearrange("(s q) (t n) -> t q s n", q=P, n=TILE_TOKENS)

                def step(t, p, pair):
                    sp.wait_ge(s["conv_in_psum"], n(t) - 2)
                    sp.dma_start(patches[:, p], src[t]).then_inc(loaded[p], 16)

                tiles(sp, step)

            @block.tensor
            def _(pe):
                def step(t, p, pair):
                    pe.wait_ge(loaded[p], 16 * (pair + 1))
                    pe.wait_ge(s["biased"], n(t) - 2)
                    for c in range(SLABS):
                        mm = nc.tensor.matmul(ps_conv[0:TILE_TOKENS, p, :], patches[:, p, c, :], w["offset_w"][:, c, :], start=(c == 0), stop=(c == SLABS - 1))
                    mm.then_inc(s["conv_in_psum"], 1)
                    pe.wait_ge(s["pos"], n(t))
                    pe.wait_ge(s["posT"], n(t) - 2)
                    for h in range(KHALVES):
                        mm = nc.tensor.transpose(ps_turn[:, p, h * TILE_TOKENS:(h + 1) * TILE_TOKENS], pos[:, p, 1, h * P:(h + 1) * P],
                                                 tw.identity[0:TILE_TOKENS, 0:TILE_TOKENS])
                    mm.then_inc(s["turned"], 1)

                tiles(pe, step)

            @block.vector
            def _(dve):
                for x in names:
                    dve.sem_inc(s[x], B)

                def step(t, p, pair):
                    both = lambda x: x.rearrange("n a k -> n (a k)")
                    dve.wait_ge(s["conv_in_psum"], n(t))
                    dve.wait_ge(s["turned"], n(t) - 2)
                    nc.vector.tensor_tensor(both(pos[:, p]), ps_conv[0:TILE_TOKENS, p, :], w["offset_b"][0:TILE_TOKENS, :], ALU.add).then_inc(s["biased"], 1)
                    dve.wait_ge(s["biased"], n(t))
                    nc.vector.tensor_tensor(both(pos[:, p]), both(pos[:, p]), w["base"][:], ALU.add).then_inc(s["pos"], 1)
                    dve.wait_ge(s["pos"], n(t))
                    dve.wait_ge(s["rel_saved"], n(t) - 2)
                    nc.vector.tensor_scalar(rel[:, p, 1, :], pos[:, p, 1, :], w["origin"][:, 1:2], None, ALU.subtract).then_inc(s["rel_x"], 1)
                    nc.vector.tensor_scalar(rel[:, p, 0, :], pos[:, p, 0, :], w["origin"][:, 0:1], None, ALU.subtract).then_inc(s["rel_y"], 1)
                    nc.vector.tensor_copy(k.pos_y[:, t, :], pos[:, p, 0, :])
                    dve.wait_ge(s["rel_y"], n(t))
                    nc.vector.tensor_reduce(k.range[:, 0, t, :], both(rel[:, p]), AX_X, ALU.min)
                    nc.vector.tensor_reduce(k.range[:, 1, t, :], both(rel[:, p]), AX_X, ALU.max).then_inc(s["range"], 1)

                tiles(dve, step)
                dve.wait_ge(s["range"], n(TILES - 1))

            @block.scalar
            def _(act):
                def step(t, p, pair):
                    act.wait_ge(s["turned"], n(t))
                    nc.scalar.copy(k.pos_xT[:, :, t, :], ps_turn[:, p, 0:KHALVES * TILE_TOKENS].rearrange("q (h n) -> q h n", h=KHALVES)).then_inc(s["posT"], 1)

                tiles(act, step)

            @block.gpsimd
            def _(pool):
                def step(t, p, pair):
                    pool.wait_ge(s["rel_y"], n(t))
                    pool.dma_start(k.rel_d[0].rearrange("(t n) c -> t n c", n=TILE_TOKENS)[t], rel[:, p, 0, :]).then_inc(saved[p], 16)
                    pool.wait_ge(s["range"], n(t))
                    pool.wait_ge(saved[p], 16 * (pair + 1))
                    pool.sem_inc(s["rel_saved"], 1)

                tiles(pool, step)


def sample(tw, k, w):
    nc, ins = tw.nc, tw.ins
    names = "hat_y_abs hat_y hat_x_sub hat_x_abs hat_x rows_in_psum multiplied summed added".split()
    NEAR, FAR = "near", "far"
    sems = {kind: {x: tw.sem(f"{kind}_{x}") for x in names} for kind in (NEAR, FAR)}
    loads = {kind: {x: [tw.sem(f"{kind}_{x}_loaded_{p}") for p in range(2)] for x in ("places", "pixels")} for kind in (NEAR, FAR)}
    moved, saved, cleared = tw.sem("places_moved"), tw.sem("places_saved"), tw.sem("samples_cleared")
    cols = CHANNELS * WINDOW
    B = 4

    def one_pass(eng, step, first, wy, wx):
        with eng.Fori(0, GRID) as ho:
            with eng.Fori(0, TILES // 2) as pair:
                for p in range(2):
                    step(first + ho * TILES + 2 * pair + p, ho, 2 * pair + p, p, wy, wx)

    def near_or_far(eng, step, before_far=None):
        far = eng.value_load(k.far[0:1, 0:1], min_val=0, max_val=2)
        with eng.If(far == 0):
            one_pass(eng, lambda *a: step(NEAR, *a), 0, 0, 0)
        with eng.Else():
            if before_far:
                before_far()
            with eng.Fori(0, COVER) as wy:
                with eng.Fori(0, COVER) as wx:
                    one_pass(eng, lambda *a: step(FAR, *a), (wy * COVER + wx) * (GRID * TILES), wy, wx)

    def all_loaded(eng, kind, what, i, p):
        eng.wait_ge(loads[kind][what][p], 16 * IMG_PER_TILE // 2 * (i - p + 2))

    with tw.scratch(), nc.psum_tensor("ps_rows", [P, KHALVES, IMG_PER_TILE, 512], F32) as ps:
        hat_y = tw.sb("hat_y", [P, 2, GRID, KPOINTS])
        strip = tw.sb("strip", [P, 2, CHANNELS, PADDED])
        window = strip[:, :, :, 0:WINDOW]
        hat_x = tw.sb("hat_x", [P, 2, KHALVES, IMG_PER_TILE, GRID, WINDOW])
        product = tw.sb("product", [P, KHALVES, IMG_PER_TILE, GRID * cols])
        part = tw.sb("part", [P, KHALVES, IMG_PER_TILE * GRID * CHANNELS])
        moved_places = tw.sb("moved_places", [TILE_TOKENS, TILES, KPOINTS])
        with nc.Block() as block:

            @block.gpsimd
            def _(pool):
                nc.gpsimd.memset(hat_y[:], 0.0)

        with nc.Block() as block:

            @block.sync
            def _(sp):
                def step(kind, i, ho, t, p, wy, wx):
                    n = B + i + 1
                    sp.wait_ge(sems[kind]["rows_in_psum"], 2 * n - 4)
                    for j in range(IMG_PER_TILE):
                        q = slice(QUAD * j, QUAD * j + WINDOW)
                        version = 0 if kind == NEAR else wy + 1
                        places = k.rel_d[version].rearrange("(t j h w) c -> t h j (w c)", t=TILES, j=IMG_PER_TILE, h=GRID)[t][ho][j:j + 1, :]
                        sp.dma_start(hat_y[q, p].rearrange("q w c -> q (w c)"), places.to_broadcast([WINDOW, GRID * KPOINTS])).then_inc(loads[kind]["places"][p], 16)
                        if kind == NEAR:
                            sp.dma_start(strip[q, p], ins["strips"][ho][t][j]).then_inc(loads[kind]["pixels"][p], 16)
                        else:
                            sp.dma_start(window[q, p], ins["windows"][wy][wx][t][j]).then_inc(loads[kind]["pixels"][p], 16)

                def store_places():
                    for wy in range(COVER):
                        sp.wait_ge(moved, wy + 1)
                        sp.dma_start(k.rel_d[1 + wy].rearrange("(t n) c -> n t c", n=TILE_TOKENS), moved_places[:]).then_inc(saved, 16)
                    sp.wait_ge(saved, 16 * COVER)

                near_or_far(sp, step, store_places)

            @block.scalar
            def _(act):
                def step(kind, i, ho, t, p, wy, wx):
                    n, s = B + i + 1, sems[kind]
                    all_loaded(act, kind, "places", i, p)
                    y = hat_y[:, p].rearrange("q w c -> q (w c)")
                    nc.scalar.activation(y, y, ACT.Abs, bias=w["minus_row"][:]).then_inc(s["hat_y_abs"], 1)
                    act.wait_ge(s["hat_x_sub"], n)
                    x = hat_x[:, p].rearrange("q h j w x -> q (h j w x)")
                    nc.scalar.activation(x, x, ACT.Abs).then_inc(s["hat_x_abs"], 1)
                    act.wait_ge(s["hat_y_abs"], n)
                    nc.scalar.activation(y, y, ACT.Relu, scale=-1.0, bias=1.0).then_inc(s["hat_y"], 1)
                    act.wait_ge(s["hat_x_abs"], n)
                    nc.scalar.activation(x, x, ACT.Relu, scale=-1.0, bias=1.0).then_inc(s["hat_x"], 1)

                near_or_far(act, step)

            @block.gpsimd
            def _(pool):
                def step(kind, i, ho, t, p, wy, wx):
                    n, s = B + i + 1, sems[kind]
                    pool.wait_ge(s["multiplied"], 2 * n - 4)
                    for h in range(KHALVES):
                        shape = [P, IMG_PER_TILE, GRID, WINDOW]
                        places = k.pos_xT[:, h, t, :].rearrange("q (j g) -> q j g", j=IMG_PER_TILE)[:, :, bass.ds(ho * GRID, GRID)]
                        grid = w["window_x"][:].unsqueeze(1) if kind == NEAR else w["cover_x"][:, wx, :].unsqueeze(1).unsqueeze(1)
                        x = nc.gpsimd.tensor_tensor(hat_x[:, p, h], places.unsqueeze(3).to_broadcast(shape), grid.to_broadcast(shape), ALU.subtract)
                    x.then_inc(s["hat_x_sub"], 1)

                near_or_far(pool, step)

            @block.tensor
            def _(pe):
                def step(kind, i, ho, t, p, wy, wx):
                    n, s = B + i + 1, sems[kind]
                    pe.wait_ge(s["hat_y"], n)
                    all_loaded(pe, kind, "pixels", i, p)
                    for h in range(KHALVES):
                        pe.wait_ge(s["multiplied"], 2 * n - 3 + h)
                        for g in range(GRID):
                            for j in range(IMG_PER_TILE):
                                q = slice(QUAD * j, QUAD * j + WINDOW)
                                rhs = strip[q, p, :, PATCH * g:PATCH * g + WINDOW] if kind == NEAR else window[q, p]
                                mm = nc.tensor.matmul(ps[:, h, j, g * cols:(g + 1) * cols], hat_y[q, p, g, h * P:(h + 1) * P], rhs, start=True, stop=True)
                        mm.then_inc(s["rows_in_psum"], 1)

                near_or_far(pe, step)

            @block.vector
            def _(dve):
                for s in sems.values():
                    for x in names:
                        dve.sem_inc(s[x], 2 * B if x in ("rows_in_psum", "multiplied", "summed", "added") else B)

                def move_places():
                    nc.vector.memset(k.samples[:], 0.0).then_inc(cleared, 1)
                    dve.wait_ge(cleared, 1)
                    for wy in range(COVER):
                        if wy:
                            dve.wait_ge(saved, 16 * wy)
                        nc.vector.tensor_scalar(moved_places[:], k.pos_y[:], float(WINDOW * wy), None, ALU.subtract).then_inc(moved, 1)

                def step(kind, i, ho, t, p, wy, wx):
                    n, s = B + i + 1, sems[kind]
                    dve.wait_ge(s["hat_x"], n)
                    for h in range(KHALVES):
                        dve.wait_ge(s["rows_in_psum"], 2 * n - 1 + h)
                        dve.wait_ge(s["summed"], 2 * n - 3 + h)
                        for j in range(IMG_PER_TILE):
                            shape = [P, GRID, CHANNELS, WINDOW]
                            split = lambda x: x.rearrange("q (g c x) -> q g c x", g=GRID, c=CHANNELS)
                            last = nc.vector.tensor_tensor(split(product[:, h, j, :]), split(ps[:, h, j, 0:GRID * cols]),
                                                           hat_x[:, p, h, j].unsqueeze(2).to_broadcast(shape), ALU.mult)
                        last.then_inc(s["multiplied"], 1)
                        dve.wait_ge(s["multiplied"], 2 * n - 1 + h)
                        into = k.samples[:, h, ho * TILES + t, :]
                        by_window = product[:, h].rearrange("q j (a x) -> q (j a) x", x=WINDOW)
                        if kind == NEAR:
                            nc.vector.tensor_reduce(into, by_window, AX_X, ALU.add).then_inc(s["summed"], 1)
                        else:
                            nc.vector.tensor_reduce(part[:, h, :], by_window, AX_X, ALU.add).then_inc(s["summed"], 1)
                            dve.wait_ge(s["summed"], 2 * n - 1 + h)
                            nc.vector.tensor_tensor(into, into, part[:, h, :], ALU.add).then_inc(s["added"], 1)

                near_or_far(dve, step, move_places)


def any_far(tw, k):
    nc = tw.nc
    reduced, compared, joined, turned, done = (tw.sem("far_" + x) for x in ("reduced", "compared", "joined", "turned", "done"))
    extreme = tw.sb("far_extreme", [TILE_TOKENS, 2])
    outside = tw.sb("far_outside", [TILE_TOKENS, 2])
    any_row = tw.sb("far_any_row", [TILE_TOKENS, 1])
    with nc.psum_tensor("ps_far", [1, 512], F32) as ps, nc.Block() as block:

        @block.vector
        def _(dve):
            lowest, highest = k.range[:, 0].rearrange("n t o -> n (t o)"), k.range[:, 1].rearrange("n t o -> n (t o)")
            nc.vector.tensor_reduce(extreme[:, 0:1], lowest, AX_X, ALU.min).then_inc(reduced, 1)
            nc.vector.tensor_reduce(extreme[:, 1:2], highest, AX_X, ALU.max).then_inc(reduced, 1)
            dve.wait_ge(reduced, 2)
            nc.vector.tensor_scalar(outside[:, 0:1], extreme[:, 0:1], 0.0, None, ALU.is_lt).then_inc(compared, 1)
            nc.vector.tensor_scalar(outside[:, 1:2], extreme[:, 1:2], float(WINDOW - 1), None, ALU.is_gt).then_inc(compared, 1)
            dve.wait_ge(compared, 2)
            nc.vector.tensor_tensor(any_row[:], outside[:, 0:1], outside[:, 1:2], ALU.add).then_inc(joined, 1)
            dve.wait_ge(turned, 1)
            nc.vector.tensor_reduce(k.far[:], ps[:, 0:TILE_TOKENS], AX_X, ALU.max).then_inc(done, 1)
            dve.wait_ge(done, 1)

        @block.tensor
        def _(pe):
            pe.wait_ge(joined, 1)
            nc.tensor.transpose(ps[:, 0:TILE_TOKENS], any_row[:], tw.identity[0:TILE_TOKENS, 0:TILE_TOKENS]).then_inc(turned, 1)


def project_and_norm(tw, k, w):
    nc = tw.nc
    names = "cleared product_in_psum stats aggregated rooted inverted normed activated turned y_ready".split()
    s = {x: tw.sem("tok_" + x) for x in names}
    half_cols = IMAGES * TOKENS // 2
    chunks = GRID * TILES // 2
    with tw.scratch(), ExitStack() as ctx:
        ps = ctx.enter_context(nc.psum_tensor("ps_tok", [HALF, HALVES, 2, 512], F32))
        ps_y = ctx.enter_context(nc.psum_tensor("ps_tok_y", [P, 2, 512], F32))
        stats = tw.sb("tok_stats", [HALF, HALVES, 2, 6])
        moments = tw.sb("tok_moments", [HALF, HALVES, 2])
        rstd = tw.sb("tok_rstd", [HALF, HALVES, 1])
        normed = tw.sb("tok_normed", [HALF, HALVES, IMAGES * TOKENS])
        yT = tw.sb("tok_yT", [HALF, HALVES, IMAGES, QUAD])
        with nc.Block() as block:

            @block.gpsimd
            def _(pool):
                nc.gpsimd.memset(yT[:], 0.0).then_inc(s["cleared"], 1)
                nc.gpsimd.memset(tw.mean[:], 0.0)
                nc.gpsimd.memset(tw.rstd[:], 1.0)

            @block.tensor
            def _(pe):
                for o in range(HALVES):
                    for half in range(2):
                        i = 0
                        for c in range(CHANNELS):
                            for h in range(KHALVES):
                                rhs = k.samples[:, h, half * chunks:(half + 1) * chunks, :].rearrange("q a (b c) -> q (a b) c", c=CHANNELS)[:, :, c]
                                mm = nc.tensor.matmul(ps[:, o, half, 0:half_cols], w["dconv"][:, c, h, o * HALF:(o + 1) * HALF], rhs,
                                                      start=(i == 0), stop=(i == CHANNELS * KHALVES - 1))
                                i += 1
                        mm.then_inc(s["product_in_psum"], 1)
                for t in range(TILES):
                    pe.wait_ge(s["activated"], HALVES)
                    if t >= 2:
                        pe.wait_ge(s["y_ready"], t - 1)
                    for o in range(HALVES):
                        mm = nc.tensor.transpose(ps_y[:, t % 2, o * HALF:(o + 1) * HALF], yT[:, o, 4 * t:4 * t + 4, :], tw.identity[0:HALF, 0:HALF])
                    mm.then_inc(s["turned"], 1)

            @block.vector
            def _(dve):
                for o in range(HALVES):
                    for half in range(2):
                        dve.wait_ge(s["product_in_psum"], 2 * o + half + 1)
                        nc.vector.bn_stats(stats[:, o, half, :], ps[:, o, half, 0:half_cols]).then_inc(s["stats"], 1)
                dve.wait_ge(s["stats"], 4)
                for o in range(HALVES):
                    nc.vector.bn_aggr(moments[:, o, :], stats[:, o].rearrange("q a b -> q (a b)")).then_inc(s["aggregated"], 1)
                dve.wait_ge(s["rooted"], 1)
                nc.vector.reciprocal(rstd[:], rstd[:]).then_inc(s["inverted"], 1)
                dve.wait_ge(s["inverted"], 1)
                for o in range(HALVES):
                    nc.vector.tensor_scalar(normed[:, o, :].rearrange("q (a b) -> q a b", a=2), ps[:, o, :, 0:half_cols], moments[:, o, 0:1], rstd[:, o, :],
                                            ALU.subtract, ALU.mult).then_inc(s["normed"], 1)
                for t in range(TILES):
                    dve.wait_ge(s["turned"], t + 1)
                    nc.vector.tensor_copy(tw.y[:, t, :], ps_y[:, t % 2, 0:DIM]).then_inc(s["y_ready"], 1)

            @block.scalar
            def _(act):
                act.wait_ge(s["aggregated"], HALVES)
                nc.scalar.activation(rstd[:], moments[:, :, 1:2], ACT.Sqrt, bias=tw.eps[0:HALF, :]).then_inc(s["rooted"], 1)
                act.wait_ge(s["cleared"], 1)
                for o in range(HALVES):
                    act.wait_ge(s["normed"], o + 1)
                    nc.scalar.activation(yT[:, o, :, 0:TOKENS].rearrange("q i (h w) -> q h i w", h=GRID),
                                         normed[:, o, :].rearrange("q (h i w) -> q h i w", h=GRID, w=GRID), ACT.Gelu,
                                         scale=w["gamma"][:, o:o + 1], bias=w["beta"][:, o:o + 1]).then_inc(s["activated"], 1)


class Tokenizer:

    def __init__(self, tw):
        self.pos_y = tw.sb("pos_y", [TILE_TOKENS, TILES, KPOINTS])
        self.pos_xT = tw.sb("pos_xT", [P, KHALVES, TILES, TILE_TOKENS])
        self.far = tw.scope.enter_context(tw.nc.sbuf_tensor("far", [1, 1], mybir.dt.int32))
        self.range = tw.sb("range", [TILE_TOKENS, 2, TILES, 1])
        self.samples = tw.sb("samples", [P, KHALVES, GRID * TILES, IMG_PER_TILE * GRID * CHANNELS])
        self.rel_d = tw.nc.dram_tensor("places_y", (1 + COVER, IMAGES * TOKENS, KPOINTS), F32, kind="Internal").ap()


def tokenizer(tw, w):
    k = Tokenizer(tw)
    offsets(tw, k, w)
    any_far(tw, k)
    sample(tw, k, w)
    project_and_norm(tw, k, w)


def front(tw, m, name, wg, experts):
    nc = tw.nc
    base = m.front_base
    s = m.front_sem

    def n(t):
        return base + t + 1

    def tiles(eng, step):
        with eng.Fori(0, TILES - 1, 2) as i:
            step(i, 0)
            step(i + 1, 1)

    with nc.psum_tensor(name + "ps_hT", [HALF, 2, 512], F32) as ps_hT, \
            nc.psum_tensor(name + "ps_gate", [P, 2, 512], F32) as ps_gate, nc.Block() as block:

        @block.vector
        def _(dve):
            def step(t, p):
                dve.wait_ge(s["hT_in_psum"], n(t) - 2)
                dve.wait_ge(s["kept"], n(t) - 2)
                nc.vector.tensor_scalar(m.row[:, p, :], tw.y[:, t, :], tw.mean[:, t, :], tw.rstd[:, t, :],
                                        ALU.subtract, ALU.mult).then_inc(s["normed"], 1)
                dve.wait_ge(s["gated"], n(t))
                nc.vector.tensor_copy(m.logits[:, t, 0:experts], ps_gate[:, p, 0:experts]).then_inc(s["logits_ready"], 1)

            tiles(dve, step)

        @block.tensor
        def _(pe):
            def step(t, p):
                pe.wait_ge(s["normed"], n(t))
                pe.wait_ge(s["hT_ready"], n(t) - 2)
                for k in range(HALVES):
                    mm = nc.tensor.transpose(ps_hT[:, p, k * P:(k + 1) * P], m.row[:, p, k * HALF:(k + 1) * HALF], tw.identity[:])
                mm.then_inc(s["hT_in_psum"], 1)
                pe.wait_ge(s["hT_ready"], n(t))
                pe.wait_ge(s["logits_ready"], n(t) - 2)
                for k in range(HALVES):
                    mm = nc.tensor.matmul(ps_gate[:, p, 0:experts], m.rowT[:, p, k, :], wg[:, k, 0:experts],
                                          start=(k == 0), stop=(k == 1))
                mm.then_inc(s["gated"], 1)

            tiles(pe, step)

        @block.scalar
        def _(act):
            def step(t, p):
                act.wait_ge(s["hT_in_psum"], n(t))
                act.wait_ge(s["gated"], n(t) - 2)
                act.wait_ge(s["keptT"], n(t) - 2)
                nc.scalar.copy(m.rowT[:, p, :, :], ps_hT[:, p, 0:HALVES * P].rearrange("q (k n) -> q k n", n=P)).then_inc(s["hT_ready"], 1)

            tiles(act, step)

        @block.gpsimd
        def _(pool):
            def step(t, p):
                pool.wait_ge(s["normed"], n(t))
                nc.gpsimd.tensor_copy(m.h[:, t, :], m.row[:, p, :]).then_inc(s["kept"], 1)
                pool.wait_ge(s["hT_ready"], n(t))
                nc.gpsimd.tensor_copy(m.hT[:, :, t, :], m.rowT[:, p, :, :]).then_inc(s["keptT"], 1)

            tiles(pool, step)


class MoeBuffers:

    def __init__(self, tw):
        nc, sb = tw.nc, tw.sb
        self.row = sb("row", [P, 2, DIM])
        self.rowT = sb("rowT", [HALF, 2, HALVES, P])
        self.h = sb("h_all", [P, TILES, DIM])
        self.hT = sb("hT_all", [HALF, HALVES, TILES, P])
        self.logits = sb("logits", [P, TILES, 16])
        self.combine = sb("combine", [P, TILES, 8])
        self.score = sb("score", [P, TILES, 8])
        self.rest = sb("rest", [P, TILES, 8])
        self.cand = sb("cand", [P, TILES, 8])
        self.best = sb("best", [P, 2, TILES, 1])
        self.first = sb("first", [P, TILES, 1])
        self.total = sb("total", [P, TILES, 1])
        self.chosen = sb("chosen", [P, TILES, 2, 2, 8])
        self.countdown = sb("countdown", [P, 8])
        self.slot_rows = sb("slot_rows", [16, IMAGES, QUAD])
        self.weight_rows = sb("weight_rows", [32, IMAGES, QUAD])
        self.slot = sb("slot", [P, TILES, 16])
        self.slot_iota = sb("slot_iota", [P, 120])
        self.row_iota = sb("row_iota", [P, 1])
        dram = lambda nm: tw.keep(nm, lambda: nc.dram_tensor(nm, (2, 16, TILES * P), F32, kind="Internal").ap())
        self.slot_scratch, self.weight_scratch = dram("slot_scratch"), dram("weight_scratch")
        names = "normed hT_in_psum hT_ready gated logits_ready kept keptT".split()
        self.front_sem = {k: tw.sem("front_" + k) for k in names}
        self.step, self.steps = tw.sem("routing_step"), 0
        self.front_base = 2
        self.const = tw.sem("moe_constants")
        with nc.Block() as block:

            @block.gpsimd
            def _(pool):
                for e in range(8):
                    nc.gpsimd.memset(self.countdown[:, e:e + 1], float(8 - e))
                nc.gpsimd.iota(self.slot_iota[:], [[1, 120]], base=0, channel_multiplier=0, allow_small_or_imprecise_dtypes=True)
                nc.gpsimd.iota(self.row_iota[:], [[0, 1]], base=0, channel_multiplier=1, allow_small_or_imprecise_dtypes=True)
                nc.gpsimd.memset(self.slot_rows[:], -1.0)
                nc.gpsimd.memset(self.weight_rows[:], 0.0).then_inc(self.const, 1)

            @block.vector
            def _(dve):
                for x in self.front_sem.values():
                    dve.sem_inc(x, 2)
                dve.wait_ge(self.const, 1)


class RowScratch:

    def __init__(self, tw, m):
        nc, sb = tw.nc, tw.sb
        n = IMAGES * TOKENS
        m.rows = sb("rows", [32, IMAGES, TOKENS])
        m.work = sb("rows_work", [16, 2, n])
        m.top = sb("rows_top", [16, 16, 8])
        m.gt, m.eq, m.cum, m.ones = (sb("rows_" + k, [16, n]) for k in ("gt", "eq", "cum", "ones"))
        m.count = sb("rows_count", [16, 2])
        with nc.Block() as block:

            @block.gpsimd
            def _(pool):
                nc.gpsimd.memset(m.ones[:], 1.0)


class Chain:

    def __init__(self, eng, m):
        self.eng, self.m = eng, m

    def __call__(self, ins):
        ins.then_inc(self.m.step, 1)
        self.m.steps += 1
        self.eng.wait_ge(self.m.step, self.m.steps)


def pick_two(nc, m, after, scores):
    shape = [P, TILES, 8]
    for k in range(2):
        x = scores if k == 0 else m.rest
        after(nc.vector.tensor_reduce(m.best[:, k], x[:, :, 0:8], AX_X, ALU.max))
        after(nc.vector.tensor_tensor(m.cand[:], x[:, :, 0:8], m.best[:, k].to_broadcast(shape), ALU.is_equal))
        after(nc.vector.tensor_tensor(m.cand[:], m.cand[:], m.countdown[:].unsqueeze(1).to_broadcast(shape), ALU.mult))
        after(nc.vector.tensor_reduce(m.first[:], m.cand[:], AX_X, ALU.max))
        after(nc.vector.tensor_tensor(m.chosen[:, :, 0, k, :], m.cand[:], m.first[:].to_broadcast(shape), ALU.is_equal))
        if k == 0:
            after(nc.vector.scalar_tensor_tensor(out=m.rest[:], in0=m.chosen[:, :, 0, 0, :], scalar=-1e30,
                                                 in1=x[:, :, 0:8], op0=ALU.mult, op1=ALU.add))


def lora_gate(tw, m, name, bg):
    nc = tw.nc
    shape = [P, TILES, 8]
    shifted, exped = tw.sem(name + "_gate_shifted"), tw.sem(name + "_gate_exped")
    with nc.Block() as block:

        @block.vector
        def _(dve):
            after = Chain(dve, m)
            after(nc.vector.tensor_tensor(m.logits[:, :, 0:8], m.logits[:, :, 0:8], bg[:].unsqueeze(1).to_broadcast(shape), ALU.add))
            after(nc.vector.tensor_reduce(m.first[:], m.logits[:, :, 0:8], AX_X, ALU.max))
            nc.vector.tensor_tensor(m.score[:], m.logits[:, :, 0:8], m.first[:].to_broadcast(shape), ALU.subtract).then_inc(shifted, 1)
            dve.wait_ge(exped, 1)
            after(nc.vector.tensor_reduce(m.total[:], m.score[:], AX_X, ALU.add))
            after(nc.vector.reciprocal(m.total[:], m.total[:]))
            after(nc.vector.tensor_tensor(m.score[:], m.score[:], m.total[:].to_broadcast(shape), ALU.mult))
            pick_two(nc, m, after, m.score)
            after(nc.vector.tensor_tensor(m.cand[:], m.chosen[:, :, 0, 0, :], m.chosen[:, :, 0, 1, :], ALU.add))
            after(nc.vector.scalar_tensor_tensor(out=m.combine[:], in0=m.cand[:], scalar=2.0, in1=m.score[:],
                                                 op0=ALU.mult, op1=ALU.mult))

        @block.scalar
        def _(act):
            act.wait_ge(shifted, 1)
            nc.scalar.activation(m.score[:], m.score[:], ACT.Exp).then_inc(exped, 1)


def token_choice_rows(tw, m, name, ps):
    nc = tw.nc
    shifted, exped = tw.sem(name + "_pair_shifted"), tw.sem(name + "_pair_exped")
    turned, picked = tw.sem(name + "_turned"), tw.sem(name + "_picked")
    shape = [P, TILES, 8]
    with nc.Block() as block:

        @block.vector
        def _(dve):
            after = Chain(dve, m)
            pick_two(nc, m, after, m.logits)
            nc.vector.tensor_tensor(m.first[:], m.best[:, 1], m.best[:, 0], ALU.subtract).then_inc(shifted, 1)
            dve.wait_ge(exped, 1)
            after(nc.vector.tensor_scalar(m.total[:], m.first[:], 1.0, None, ALU.add))
            after(nc.vector.reciprocal(m.total[:], m.total[:]))
            after(nc.vector.tensor_tensor(m.first[:], m.first[:], m.total[:], ALU.mult))
            after(nc.vector.tensor_tensor(m.chosen[:, :, 1, 0, :], m.chosen[:, :, 0, 0, :], m.total[:].to_broadcast(shape), ALU.mult))
            nc.vector.tensor_tensor(m.chosen[:, :, 1, 1, :], m.chosen[:, :, 0, 1, :], m.first[:].to_broadcast(shape), ALU.mult).then_inc(picked, 1)
            dve.wait_ge(turned, 1)
            rows_in = ps[0:32, :, 0:4 * P].rearrange("r b (i n) -> r b i n", n=QUAD)
            for c in range(2):
                half = slice(IMAGES // 2 * c, IMAGES // 2 * (c + 1))
                after(nc.vector.tensor_copy(m.rows[:, half, :], rows_in[:, c, :, 0:TOKENS]))
                after(nc.vector.tensor_copy(m.weight_rows[:, half, :], rows_in[:, c, :, :]))
            sel = m.rows[0:16].rearrange("r i n -> r (i n)")
            after(nc.vector.tensor_tensor_scan(m.cum[:], m.ones[:], sel, 0.0, ALU.mult, ALU.add))
            after(nc.vector.tensor_tensor(m.cum[:], m.cum[:], sel, ALU.mult))
            after(nc.vector.tensor_scalar(m.slot_rows[:, :, 0:TOKENS], m.cum[:].rearrange("r (i n) -> r i n", n=TOKENS), 1.0, None, ALU.subtract))

        @block.scalar
        def _(act):
            act.wait_ge(shifted, 1)
            nc.scalar.activation(m.first[:], m.first[:], ACT.Exp).then_inc(exped, 1)

        @block.tensor
        def _(pe):
            pe.wait_ge(picked, 1)
            for t in range(TILES):
                mm = nc.tensor.transpose(ps[0:32, t // 4, (t % 4) * P:(t % 4 + 1) * P], m.chosen[:, t, :, :, :], tw.identity[:])
            mm.then_inc(turned, 1)


def expert_choice_rows(tw, m, name, ps, capacity):
    nc = tw.nc
    sigmoided, turned = tw.sem(name + "_sigmoided"), tw.sem(name + "_turned")
    with nc.Block() as block:

        @block.scalar
        def _(act):
            nc.scalar.activation(m.logits[:], m.logits[:], ACT.Sigmoid).then_inc(sigmoided, 1)

        @block.tensor
        def _(pe):
            pe.wait_ge(sigmoided, 1)
            for t in range(TILES):
                mm = nc.tensor.transpose(ps[0:16, t // 4, (t % 4) * P:(t % 4 + 1) * P], m.logits[:, t, :], tw.identity[:])
            mm.then_inc(turned, 1)

        @block.vector
        def _(dve):
            after = Chain(dve, m)
            dve.wait_ge(turned, 1)
            rows_in = ps[0:16, :, 0:4 * P].rearrange("r b (i n) -> r b i n", n=QUAD)
            for c in range(2):
                half = slice(IMAGES // 2 * c, IMAGES // 2 * (c + 1))
                after(nc.vector.tensor_copy(m.rows[0:16, half, :], rows_in[:, c, :, 0:TOKENS]))
                after(nc.vector.tensor_copy(m.weight_rows[0:16, half, :], rows_in[:, c, :, :]))
            score = m.rows[0:16].rearrange("r i n -> r (i n)")
            rounds = -(-capacity // 8)
            x = score
            for r in range(rounds):
                after(nc.vector.max(m.top[:, r, :], x))
                if r < rounds - 1:
                    after(nc.vector.match_replace(m.work[:, r % 2, :], m.top[:, r, :], x, -1.0))
                    x = m.work[:, r % 2, :]
            least = m.top[:, rounds - 1, (capacity - 1) % 8:(capacity - 1) % 8 + 1]
            after(nc.vector.tensor_scalar(m.gt[:], score, least, None, ALU.is_gt))
            after(nc.vector.tensor_reduce(m.count[:, 0:1], m.gt[:], AX_X, ALU.add))
            after(nc.vector.tensor_scalar(m.count[:, 1:2], m.count[:, 0:1], -1.0, float(capacity), ALU.mult, ALU.add))
            after(nc.vector.tensor_scalar(m.eq[:], score, least, None, ALU.is_equal))
            after(nc.vector.tensor_tensor_scan(m.cum[:], m.ones[:], m.eq[:], 0.0, ALU.mult, ALU.add))
            after(nc.vector.scalar_tensor_tensor(out=m.eq[:], in0=m.cum[:], scalar=m.count[:, 1:2], in1=m.eq[:],
                                                 op0=ALU.is_le, op1=ALU.mult))
            after(nc.vector.tensor_tensor(m.gt[:], m.gt[:], m.eq[:], ALU.add))
            after(nc.vector.tensor_tensor_scan(m.cum[:], m.ones[:], m.gt[:], 0.0, ALU.mult, ALU.add))
            after(nc.vector.tensor_tensor(m.cum[:], m.cum[:], m.gt[:], ALU.mult))
            after(nc.vector.tensor_scalar(m.slot_rows[:, :, 0:TOKENS], m.cum[:].rearrange("r (i n) -> r i n", n=TOKENS), 1.0, None, ALU.subtract))


def experts(tw, m, name, which, lists, capacity, hidden, w_in, w_out, weight_row, onto):
    nc = tw.nc
    n_exp = w_in.shape[0]
    ft = hidden // P
    fb = ft // 2
    C = capacity
    names = ("slots_in_psum slots_ready saved onehot gathered xT_ready up_in_psum silu gated "
             "down_in_psum down_ready returned back closed added").split()
    s = {k: tw.sem(name + "_" + k) for k in names}
    loaded = {k: [tw.sem(f"{name}_{k}_loaded_{p}") for p in range(2)] for k in ("win", "wout", "rows")}
    with ExitStack() as ctx:
        def sb(nm, shape):
            return ctx.enter_context(nc.sbuf_tensor(name + nm, shape, F32))

        def pb(nm, shape):
            return ctx.enter_context(nc.psum_tensor(name + nm, shape, F32))

        win = sb("win", [HALF, 2, HALVES, 2 * hidden])
        wout = sb("wout", [P, 2, ft, DIM])
        slot_b = sb("slot_b", [C, 2, lists, TILES * P])
        weight_b = sb("weight_b", [C, 2, lists, TILES * P])
        gather = sb("gather", [P, 2, TILES, lists * C])
        xT = sb("xT", [HALF, 2, HALVES, lists * C])
        act_gate = sb("act_gate", [P, 2, fb, lists * C])
        hid = sb("hid", [P, ft, lists * C])
        down = sb("down", [C, 2, lists, DIM])
        zeros = sb("zeros", [P, P])

        acc = pb("acc", [P, 4, 512])
        ps_x = pb("ps_x", [HALF, HALVES, lists * C])
        bank_g, bank_u = pb("bank_g", [P, 512]), pb("bank_u", [P, 512])
        ps_g = bank_g[:, 0:fb * lists * C].rearrange("p (f c) -> p f c", f=fb)
        ps_u = bank_u[:, 0:fb * lists * C].rearrange("p (f c) -> p f c", f=fb)
        ps_slots = bank_g[:, 0:TILES * 16].rearrange("p (t r) -> p t r", r=16)
        ps_d = pb("ps_d", [C, lists, DIM])
        block = ctx.enter_context(nc.Block())
        B = 4

        def n(e):
            return B + e + 1

        def experts_loop(eng, step):
            with eng.Fori(0, n_exp // 2) as pair:
                step(2 * pair, 0, pair)
                step(2 * pair + 1, 1, pair)

        @block.sync
        def _(sp):
            sp.dma_start(m.slot_scratch[which], m.slot_rows[:].rearrange("r i n -> r (i n)")).then_inc(s["saved"], 16)
            sp.dma_start(m.weight_scratch[which], m.weight_rows[weight_row:weight_row + 16].rearrange("r i n -> r (i n)")).then_inc(s["saved"], 16)
            sp.wait_ge(s["saved"], 32)

            def step(e, p, pair):
                sp.wait_ge(s["up_in_psum"], B + 2 * e - 2)
                sp.dma_start(win[:, p], w_in[e].rearrange("(k q) n -> q k n", q=HALF)).then_inc(loaded["win"][p], 16)
                sp.wait_ge(s["down_in_psum"], n(e) - 2)
                sp.dma_start(wout[:, p], w_out[e].rearrange("(f q) n -> q f n", q=P)).then_inc(loaded["wout"][p], 16)
                sp.wait_ge(s["returned"], n(e) - 2)
                for g in range(lists):
                    for scratch, dst in ((m.slot_scratch, slot_b), (m.weight_scratch, weight_b)):
                        row = scratch[which].rearrange("(g e) n -> e g n", g=lists)[e][g:g + 1, :]
                        sp.dma_start(dst[:, p, g, :], row.to_broadcast([C, TILES * P])).then_inc(loaded["rows"][p], 16)

            experts_loop(sp, step)

        @block.gpsimd
        def _(pool):
            nc.gpsimd.memset(zeros[:], 0.0).then_inc(s["slots_ready"], 1)

        @block.vector
        def _(dve):
            for x in ("gated", "down_in_psum", "back", "onehot", "gathered", "xT_ready", "returned", "down_ready", "silu", "up_in_psum"):
                dve.sem_inc(s[x], B)
            dve.wait_ge(s["slots_in_psum"], 1)
            nc.vector.tensor_copy(m.slot[:], ps_slots).then_inc(s["slots_ready"], 1)
            dve.wait_ge(s["slots_ready"], 2)

            def step(e, p, pair):
                dve.wait_ge(s["gathered"], n(e) - 2)
                for t in range(TILES):
                    for g in range(lists):
                        col = e + g * n_exp
                        ins = nc.vector.tensor_scalar(gather[:, p, t, g * C:(g + 1) * C], m.slot_iota[:, 0:C],
                                                      m.slot[:, t, bass.ds(col, 1)], None, ALU.is_equal)
                ins.then_inc(s["onehot"], 1)
                dve.wait_ge(loaded["rows"][p], 32 * lists * (pair + 1))
                for g in range(lists):
                    ins = nc.vector.scalar_tensor_tensor(out=weight_b[:, p, g, :], in0=slot_b[:, p, g, :], scalar=m.row_iota[0:C, :],
                                                         in1=weight_b[:, p, g, :], op0=ALU.is_equal, op1=ALU.mult)
                ins.then_inc(s["back"], 1)
                for c in range(2):
                    dve.wait_ge(s["silu"], B + 2 * e + c + 1)
                    if c == 0:
                        dve.wait_ge(s["down_in_psum"], n(e) - 1)
                    nc.vector.tensor_tensor(hid[:, c * fb:(c + 1) * fb, :], act_gate[:, c, :, :], ps_u, ALU.mult).then_inc(s["gated"], 1)

            experts_loop(dve, step)
            dve.wait_ge(s["closed"], 1)
            for t in range(TILES):
                nc.vector.tensor_tensor(tw.y[:, t, :], acc[:, t // 2, (t % 2) * DIM:(t % 2 + 1) * DIM], onto[:, t, :], ALU.add).then_inc(s["added"], 1)
                dve.wait_ge(s["added"], t + 1)
                nc.vector.bn_stats(tw.moments[:, t, :], tw.y[:, t, :])

        @block.scalar
        def _(act):
            def step(e, p, pair):
                act.wait_ge(s["gathered"], n(e))
                act.wait_ge(s["up_in_psum"], B + 2 * e - 2)
                nc.scalar.copy(xT[:, p], ps_x[:]).then_inc(s["xT_ready"], 1)
                for c in range(2):
                    act.wait_ge(s["up_in_psum"], B + 2 * e + c + 1)
                    act.wait_ge(s["gated"], B + 2 * e + c - 1)
                    nc.scalar.activation(act_gate[:, c, :, :], ps_g, ACT.Silu).then_inc(s["silu"], 1)
                act.wait_ge(s["down_in_psum"], n(e))
                act.wait_ge(s["returned"], n(e) - 2)
                nc.scalar.copy(down[:, p], ps_d[:]).then_inc(s["down_ready"], 1)

            experts_loop(act, step)

        @block.tensor
        def _(pe):
            for t in range(TILES):
                mm = nc.tensor.transpose(ps_slots[:, t, :], m.slot_rows[:, 4 * t:4 * t + 4, :], tw.identity[0:16, 0:16])
            mm.then_inc(s["slots_in_psum"], 1)
            pe.wait_ge(s["slots_ready"], 2)
            for c in range(4):
                nc.tensor.matmul(acc[:, c, 0:2 * DIM], zeros[:], m.h[:, 2 * c:2 * c + 2, :].rearrange("p t n -> p (t n)"), start=True, stop=False)

            def step(e, p, pair):
                pe.wait_ge(s["onehot"], n(e))
                pe.wait_ge(s["xT_ready"], n(e) - 1)
                for k in range(HALVES):
                    for t in range(TILES):
                        mm = nc.tensor.matmul(ps_x[:, k, :], m.h[:, t, k * HALF:(k + 1) * HALF], gather[:, p, t, :],
                                              start=(t == 0), stop=(t == TILES - 1))
                mm.then_inc(s["gathered"], 1)
                pe.wait_ge(loaded["win"][p], 16 * (pair + 1))
                pe.wait_ge(s["xT_ready"], n(e))
                for c in range(2):
                    pe.wait_ge(s["gated"], B + 2 * e + c)
                    for f in range(fb):
                        for ps, at in ((ps_g, 0), (ps_u, hidden)):
                            o = at + (c * fb + f) * P
                            for k in range(HALVES):
                                mm = nc.tensor.matmul(ps[:, f, :], win[:, p, k, o:o + P], xT[:, p, k, :], start=(k == 0), stop=(k == 1))
                    mm.then_inc(s["up_in_psum"], 1)
                pe.wait_ge(loaded["wout"][p], 16 * (pair + 1))
                pe.wait_ge(s["gated"], B + 2 * e + 2)
                pe.wait_ge(s["down_ready"], n(e) - 1)
                for g in range(lists):
                    for f in range(ft):
                        mm = nc.tensor.matmul(ps_d[:, g, :], hid[:, f, g * C:(g + 1) * C], wout[:, p, f, :], start=(f == 0), stop=(f == ft - 1))
                mm.then_inc(s["down_in_psum"], 1)
                pe.wait_ge(s["down_ready"], n(e))
                pe.wait_ge(s["back"], n(e))
                for t in range(TILES):
                    for g in range(lists):
                        mm = nc.tensor.matmul(acc[:, t // 2, (t % 2) * DIM:(t % 2 + 1) * DIM], weight_b[:, p, g, t * P:(t + 1) * P],
                                              down[:, p, g, :], start=False, stop=False, skip_group_check=True)
                mm.then_inc(s["returned"], 1)

            experts_loop(pe, step)
            for c in range(4):
                mm = nc.tensor.matmul(acc[:, c, 0:2 * DIM], zeros[:], m.h[:, 2 * c:2 * c + 2, :].rearrange("p t n -> p (t n)"),
                                      start=False, stop=True)
            mm.then_inc(s["closed"], 1)


def shared_ffn(tw, m, name, win, wout, hidden):
    nc = tw.nc
    ft = hidden // P
    names = "cleared up silu gated down added".split()
    s = {k: tw.sem(name + "_" + k) for k in names}
    half_cols = IMAGES // 2 * TOKENS
    with ExitStack() as ctx:
        hid = ctx.enter_context(nc.sbuf_tensor(name + "hid", [P, ft, IMAGES, QUAD], F32))
        act_gate = ctx.enter_context(nc.sbuf_tensor(name + "act_gate", [P, 2, IMAGES // 2, TOKENS], F32))
        ps_g = ctx.enter_context(nc.psum_tensor(name + "ps_g", [P, 2, 512], F32))
        ps_u = ctx.enter_context(nc.psum_tensor(name + "ps_u", [P, 2, 512], F32))
        ps_d = ctx.enter_context(nc.psum_tensor(name + "ps_d", [P, 4, 512], F32))
        block = ctx.enter_context(nc.Block())
        parts = [(f, c) for f in range(ft) for c in range(2)]

        @block.gpsimd
        def _(pool):
            nc.gpsimd.memset(hid[:], 0.0).then_inc(s["cleared"], 1)

        @block.tensor
        def _(pe):
            for i, (f, c) in enumerate(parts):
                if i >= 2:
                    pe.wait_ge(s["gated"], i - 1)
                for ps, at in ((ps_g, 0), (ps_u, hidden)):
                    for k in range(HALVES):
                        x = m.hT[:, k, :, :].rearrange("q t (j n) -> q (t j) n", n=QUAD)[:, IMAGES // 2 * c:IMAGES // 2 * (c + 1), 0:TOKENS]
                        mm = nc.tensor.matmul(ps[:, i % 2, 0:half_cols], win[:, k, at + f * P:at + (f + 1) * P], x, start=(k == 0), stop=(k == 1))
                mm.then_inc(s["up"], 1)
            pe.wait_ge(s["gated"], len(parts))
            for t in range(TILES):
                for f in range(ft):
                    mm = nc.tensor.matmul(ps_d[:, t // 2, (t % 2) * DIM:(t % 2 + 1) * DIM], hid[:, f, 4 * t:4 * t + 4, :], wout[:, f, :],
                                          start=(f == 0), stop=(f == ft - 1))
                mm.then_inc(s["down"], 1)

        @block.scalar
        def _(act):
            for i in range(len(parts)):
                act.wait_ge(s["up"], i + 1)
                if i >= 2:
                    act.wait_ge(s["gated"], i - 1)
                nc.scalar.activation(act_gate[:, i % 2].rearrange("p i n -> p (i n)"), ps_g[:, i % 2, 0:half_cols], ACT.Silu).then_inc(s["silu"], 1)

        @block.vector
        def _(dve):
            dve.wait_ge(s["cleared"], 1)
            for i, (f, c) in enumerate(parts):
                dve.wait_ge(s["silu"], i + 1)
                nc.vector.tensor_tensor(hid[:, f, IMAGES // 2 * c:IMAGES // 2 * (c + 1), 0:TOKENS], act_gate[:, i % 2],
                                        ps_u[:, i % 2, 0:half_cols].rearrange("p (i n) -> p i n", n=TOKENS), ALU.mult).then_inc(s["gated"], 1)
            for t in range(TILES):
                dve.wait_ge(s["down"], 2 * (t // 2) + 2)
                nc.vector.tensor_tensor(tw.y[:, t, :], ps_d[:, t // 2, (t % 2) * DIM:(t % 2 + 1) * DIM], m.h[:, t, :], ALU.add).then_inc(s["added"], 1)
            dve.wait_ge(s["added"], TILES)


def build(nc, ins, out, first, last):
    with ExitStack() as ctx:
        tw = Tower(nc, ctx, ins)
        setup(tw)
        loaded = tw.sem("weights_loaded")
        pending = []

        def weight(nm, src, shape):
            t = tw.sb(nm, shape)
            pending.append((t[:], src))
            return t

        def halves(nm):
            a = ins[nm]
            return weight("w_" + nm, a.rearrange("(k p) n -> p k n", p=HALF), [HALF, HALVES, a.shape[1]])

        def spread(nm):
            a = ins[nm]
            return weight("w_" + nm, a.rearrange("(o n) -> o n", o=1).to_broadcast([P, a.shape[0]]), [P, a.shape[0]])

        plan = {}
        if first == 0:
            def stage_0(tw):
                load = []

                def bring(nm, src, shape):
                    t = tw.sb("w_" + nm, shape)
                    load.append((t[:], src))
                    return t

                w = {"offset_w": bring("offset_w", ins["offset_wT"].rearrange("(s q) n -> q s n", q=P), [P, SLABS, 2 * KPOINTS]),
                     "offset_b": bring("offset_b", ins["offset_b"].rearrange("(o n) -> o n", o=1).to_broadcast([P, 2 * KPOINTS]), [P, 2 * KPOINTS]),
                     "base": bring("base", ins["base"], [TILE_TOKENS, 2 * KPOINTS]), "origin": bring("origin", ins["origin"], [TILE_TOKENS, 2]),
                     "minus_row": bring("minus_row", ins["minus_row"], [P, 1]),
                     "window_x": bring("window_x", ins["window_x"], [P, GRID, WINDOW]), "cover_x": bring("cover_x", ins["cover_x"], [P, COVER, WINDOW]),
                     "dconv": bring("dconv", ins["dconv"], [P, CHANNELS, KHALVES, DIM]),
                     "gamma": bring("gamma", ins["gamma"], [HALF, HALVES]), "beta": bring("beta", ins["beta"], [HALF, HALVES])}
                arrived = tw.sem("tok_weights")
                with nc.Block() as block:
                    @block.sync
                    def _(sp):
                        for dst, src in load:
                            sp.dma_start(dst, src).then_inc(arrived, 16)
                        sp.wait_ge(arrived, 16 * len(load))
                tokenizer(tw, w)

            plan[0] = stage_0
        if first <= 2 <= last:
            w2 = halves("L0_ffn_Wg")

            def stage_2(tw):
                m = MoeBuffers(tw)
                front(tw, m, "L0_ffn", w2, 8)
                with nc.psum_tensor("L0_ffn_rows", [P, 2, 512], F32) as ps, tw.scratch():
                    RowScratch(tw, m)
                    token_choice_rows(tw, m, "L0_ffn", ps)
                experts(tw, m, "L0_ffn", 0, 2, 120, 512, ins["L0_ffn_Win"], ins["L0_ffn_W2"], 16, m.h)
                finish_norm(tw, "L0_ffn")

            plan[2] = stage_2
        if first <= 6 <= last:
            w6 = halves("L2_ffn_gate"), halves("L2_ffn_shared_in"), weight("w_shared_out", ins["L2_ffn_shared_out"].rearrange("(f q) n -> q f n", q=P), [P, 3, DIM])

            def stage_6(tw):
                m = MoeBuffers(tw)
                front(tw, m, "L2_ffn", w6[0], 16)
                shared_ffn(tw, m, "L2_shared", w6[1], w6[2], 384)
                with nc.psum_tensor("L2_ffn_rows", [P, 2, 512], F32) as ps, tw.scratch():
                    RowScratch(tw, m)
                    expert_choice_rows(tw, m, "L2_ffn", ps, 100)
                experts(tw, m, "L2_ffn", 1, 1, 100, 768, ins["L2_ffn_Win"], ins["L2_ffn_Wout"], 0, tw.y)
                finish_norm(tw, "L2_ffn")

            plan[6] = stage_6
        if first <= 1 <= last:
            w1 = halves("L0_attn_Wqkv"), halves("L0_attn_Wo"), tw.sb("w_L0_attn_bo", [P, DIM])
            rope = {"cos": tw.sb("rope_cos", [P, HEAD_DIM]), "sin": tw.sb("rope_sin", [P, HEAD_DIM]), "mask": tw.sb("rope_mask", [P, TOKENS]),
                    "context": tw.sb("is_context", [P, 1]), "latent": tw.sb("is_latent", [P, 1]),
                    "gain": spread("L0_attn_ln_g"), "shift": spread("L0_attn_ln_b")}
            for key, src in (("cos", "rope_cos"), ("sin", "rope_sin"), ("mask", "rope_mask"), ("context", "is_context"), ("latent", "is_latent")):
                pending.append((rope[key][:], ins[src]))
            pending.append((w1[2][:], ins["L0_attn_bo"]))

            def stage_1(tw):
                b = AttentionBuffers(tw)
                softmax_attention(tw, b, "L0_attn", "rope", *w1, rope=rope)
                finish_norm(tw, "L0_attn")

            plan[1] = stage_1
        if first <= 3 <= last:
            w3 = {"Wq": weight("w_L1_attn_Wq", ins["L1_attn_Wq"].rearrange("(g p) n -> p g n", p=P), [P, 6, DIM]),
                  "bq": weight("w_L1_attn_bq", ins["L1_attn_bq"], [P, 6]),
                  "Wkv": halves("L1_attn_Wkv"), "bk": spread("L1_attn_bk"), "bv": spread("L1_attn_bv"),
                  "A": weight("w_L1_attn_A", ins["L1_attn_A"], [P, P]), "AT": weight("w_L1_attn_AT", ins["L1_attn_AT"], [P, P]),
                  "diagonal": weight("w_L1_attn_diagonal", ins["L1_attn_diagonal"], [P, 6]),
                  "sink": spread("L1_attn_sink"), "v_null": spread("L1_attn_v_null"), "bo": spread("L1_attn_bo"),
                  "Wo": weight("w_L1_attn_Wo", ins["L1_attn_Wo"].rearrange("c (k p) n -> p c k n", p=HALF), [HALF, BRANCHES, HALVES, DIM]),
                  "cos": weight("w_cheb_cos", ins["cheb_cos"], [P, HEAD_DIM]), "sin": weight("w_cheb_sin", ins["cheb_sin"], [P, HEAD_DIM]),
                  "causal": weight("w_causal", ins["causal"], [P, TOKENS])}

            def stage_3(tw):
                branch_attention(tw, "L1_attn", w3)
                finish_norm(tw, "L1_attn")

            plan[3] = stage_3
        for i, l in ((4, "L1_ffn"), (8, "L3_ffn")):
            if first <= i <= last:
                w = halves(l + "_gate"), spread(l + "_bg"), halves(l + "_Wqkv"), halves(l + "_Wproj"), spread(l + "_bproj"), spread(l + "_bqkv")
                adapter = {"down": halves(l + "_down"), "up": weight(l + "_up", ins[l + "_up"], [P, 3 * DIM])}
                if l == "L1_ffn":
                    adapter["down_bias"] = spread(l + "_down_bias")
                    adapter["up_bias"] = weight(l + "_up_bias", ins[l + "_up_bias"], [8, 3 * DIM])

                def stage(tw, l=l, w=w, adapter=adapter):
                    m, b = MoeBuffers(tw), AttentionBuffers(tw)
                    front(tw, m, l, w[0], 8)
                    lora_gate(tw, m, l, w[1])
                    softmax_attention(tw, b, l, "adapted", w[2], w[3], w[4], bqkv=w[5], adapter={**adapter, "combine": m.combine})
                    finish_norm(tw, l)

                plan[i] = stage
        if first <= 5 <= last:
            w5 = halves("L2_attn_qkv"), halves("L2_attn_proj"), spread("L2_attn_proj_b")

            def stage_5(tw):
                b = AttentionBuffers(tw)
                softmax_attention(tw, b, "L2_attn", "unit", *w5)
                finish_norm(tw, "L2_attn")

            plan[5] = stage_5
        if first <= 7 <= last:
            w7 = (halves("L3_attn_Wqkv"), spread("L3_attn_bqkv"), halves("L3_attn_Wp"), spread("L3_attn_bp"))

            def stage_7(tw):
                b = AttentionBuffers(tw)
                softmax_attention(tw, b, "L3_attn", "biased", w7[0], w7[2], w7[3], bqkv=w7[1])
                finish_norm(tw, "L3_attn")

            plan[7] = stage_7
        pending.append((tw.is_pad[:], ins["is_pad"]))
        with nc.Block() as block:
            @block.sync
            def _(sp):
                for dst, src in pending:
                    sp.dma_start(dst, src).then_inc(loaded, 16)
                sp.wait_ge(loaded, 16 * len(pending))

        if first > 0:
            y_loaded, y_cleared = tw.sem("y_loaded"), tw.sem("y_cleared")
            with nc.Block() as block:
                @block.gpsimd
                def _(pool):
                    nc.gpsimd.memset(tw.mean[:], 0.0)
                    nc.gpsimd.memset(tw.rstd[:], 1.0)
                    nc.gpsimd.memset(tw.y[:], 0.0).then_inc(y_cleared, 1)

                @block.sync
                def _(sp):
                    sp.wait_ge(y_cleared, 1)
                    for j in range(IMG_PER_TILE):
                        sp.dma_start(tw.y[QUAD * j:QUAD * j + TOKENS, :, :],
                                     ins["dbg_h"].rearrange("(i j) n c -> j n i c", j=IMG_PER_TILE)[j]).then_inc(y_loaded, 16)
                    sp.wait_ge(y_loaded, 64)
        for i, stage in sorted(plan.items()):
            with tw.stage(f"stage{i}_"):
                stage(tw)

        normed, stored = tw.sem("result_normed"), tw.sem("result_stored")
        with nc.Block() as block:
            @block.vector
            def _(dve):
                for t in range(TILES):
                    nc.vector.tensor_scalar(tw.y[:, t, :], tw.y[:, t, :], tw.mean[:, t, :], tw.rstd[:, t, :],
                                            ALU.subtract, ALU.mult).then_inc(normed, 1)

            @block.sync
            def _(sp):
                sp.wait_ge(normed, TILES)
                for j in range(IMG_PER_TILE):
                    sp.dma_start(out.rearrange("(i j) n c -> j n i c", j=IMG_PER_TILE)[j],
                                 tw.y[QUAD * j:QUAD * j + TOKENS, :, :]).then_inc(stored, 16)
                sp.wait_ge(stored, 16 * IMG_PER_TILE)


_DEBUG = (0, 8)


def layout(x):
    a = {k: np.asarray(v) for k, v in x.items()}
    o = {}
    x = a["x"]
    p = x[:, :, :GRID * PATCH, :GRID * PATCH].reshape(IMAGES, CHANNELS, GRID, PATCH, GRID, PATCH)
    o["patchesT"] = p.transpose(1, 3, 5, 0, 2, 4).reshape(CHANNELS * KPOINTS, IMAGES * TOKENS)
    o["offset_wT"] = a["L0_tok_offset_w"].reshape(KPOINTS, 2, -1).transpose(2, 1, 0).reshape(-1, 2 * KPOINTS)
    o["offset_b"] = a["L0_tok_offset_b"].reshape(KPOINTS, 2).T.reshape(-1)
    padded = np.zeros((IMAGES, CHANNELS, PADDED, PADDED), x.dtype)
    padded[:, :, MARGIN:MARGIN + IMAGE, MARGIN:MARGIN + IMAGE] = x
    rows = padded.transpose(0, 2, 1, 3).reshape(TILES, IMG_PER_TILE, PADDED, CHANNELS, PADDED)
    o["strips"] = np.stack([rows[:, :, PATCH * g:PATCH * g + WINDOW] for g in range(GRID)])
    at = lambda i: slice(MARGIN + WINDOW * i, MARGIN + WINDOW * (i + 1))
    o["windows"] = np.stack([np.stack([rows[:, :, at(i), :, at(j)] for j in range(COVER)]) for i in range(COVER)])
    o["dconv"] = a["L0_tok_dconv_w"].reshape(DIM, CHANNELS, KHALVES, P).transpose(3, 1, 2, 0)
    o["gamma"], o["beta"] = a["L0_tok_bn_gamma"].reshape(HALVES, HALF).T, a["L0_tok_bn_beta"].reshape(HALVES, HALF).T
    g, k = np.arange(GRID), np.arange(PATCH)
    place = np.zeros((IMG_PER_TILE, GRID, GRID, 2, PATCH, PATCH), np.float32)
    place[:, :, :, 0] = (PATCH * g)[None, :, None, None, None] + k[None, None, None, :, None]
    place[:, :, :, 1] = (PATCH * g)[None, None, :, None, None] + k[None, None, None, None, :]
    o["base"] = place.reshape(TILE_TOKENS, 2 * KPOINTS)
    o["origin"] = o["base"].reshape(TILE_TOKENS, 2, KPOINTS)[:, :, 0] - MARGIN
    o["minus_row"] = -np.tile(np.arange(QUAD, dtype=np.float32), IMG_PER_TILE)[:, None]
    column = np.arange(WINDOW, dtype=np.float32)
    o["window_x"] = np.tile(PATCH * g[:, None] - MARGIN + column, (P, 1, 1)).astype(np.float32)
    o["cover_x"] = np.tile(WINDOW * np.arange(COVER)[:, None] + column, (P, 1, 1)).astype(np.float32)
    o["L3_attn_Wqkv"] = np.concatenate([a["L3_attn_Wq"], a["L3_attn_Wk"], a["L3_attn_Wv"]], 1)
    o["L3_attn_bqkv"] = np.concatenate([a["L3_attn_bq"], a["L3_attn_bk"], a["L3_attn_bv"]])
    o["L0_attn_Wqkv"] = np.concatenate([a["L0_attn_Wq"], a["L0_attn_Wkv"]], 1)
    o["L0_attn_Wo"] = np.concatenate([a["L0_attn_Wo_ctx"], a["L0_attn_Wo_lat"]], 1)
    context = TOKENS + (TOKENS - LATENT)
    bo = np.zeros((IMG_PER_TILE, QUAD, DIM), np.float32)
    bo[:, :context], bo[:, context:TOKENS] = a["L0_attn_bo_ctx"], a["L0_attn_bo_lat"]
    o["L0_attn_bo"] = bo.reshape(P, DIM)
    o["L0_attn_ln_g"], o["L0_attn_ln_b"] = a["L0_attn_ln_g"], a["L0_attn_ln_b"]
    inv = 1.0 / 10000.0 ** (np.arange(0, HEAD_DIM, 2, dtype=np.float32) / HEAD_DIM)
    angle = np.arange(TOKENS, dtype=np.float32)[:, None] * inv[None, :].astype(np.float32)
    quads = lambda x: np.tile(np.concatenate([x, np.zeros((QUAD - TOKENS, x.shape[1]), x.dtype)]).astype(np.float32), (IMG_PER_TILE, 1))
    o["rope_cos"] = quads(np.concatenate([np.cos(angle), np.cos(angle)], 1))
    o["rope_sin"] = quads(np.concatenate([-np.sin(angle), np.sin(angle)], 1))
    token = np.arange(TOKENS)
    o["rope_mask"] = quads(np.where((token[:, None] < context) & (token[None, :] >= context), -1e30, 0.0))
    o["is_pad"] = 1 - quads(np.ones((TOKENS, 1)))
    o["is_context"] = quads((token < context)[:, None])
    o["is_latent"] = quads((token >= context)[:, None])
    o["L1_attn_Wq"] = a["L1_attn_Wq"]
    o["L1_attn_bq"] = a["L1_attn_bq"].reshape(-1, P).T
    o["L1_attn_Wkv"] = np.concatenate([a["L1_attn_Wk"].T, a["L1_attn_Wv"].T], 1)
    o["L1_attn_bk"], o["L1_attn_bv"] = a["L1_attn_bk"], a["L1_attn_bv"]
    blocks = lambda x: np.block([[x if i == j else np.zeros_like(x) for j in range(P // HEAD_DIM)] for i in range(P // HEAD_DIM)])
    o["L1_attn_A"], o["L1_attn_AT"] = blocks(a["L1_attn_A"]), blocks(a["L1_attn_A"].T)
    o["L1_attn_diagonal"] = a["L1_attn_id_bias"].reshape(-1, P).T
    o["L1_attn_sink"], o["L1_attn_v_null"], o["L1_attn_bo"] = (a["L1_attn_" + k].reshape(-1) for k in ("sink_scalars", "v_nulls", "bo"))
    o["L1_attn_Wo"] = a["L1_attn_Wo"]
    half = HEAD_DIM // 2
    pos = (np.float32(2) * np.arange(TOKENS, dtype=np.float32) / np.float32(TOKENS - 1) - np.float32(1)).astype(np.float32)
    cheb = [np.ones_like(pos), pos]
    for _ in range(2, HEAD_DIM + 1):
        cheb.append((np.float32(2) * pos * cheb[-1] - cheb[-2]).astype(np.float32))
    cheb = np.stack(cheb, 1)
    degree = np.clip(1 + np.round(np.arange(half, dtype=np.float32) / (half - 1) * (HEAD_DIM - 2)).astype(np.int32), 1, HEAD_DIM - 1)
    raw1, raw2 = cheb[:, degree], cheb[:, degree + 1]
    length = np.sqrt(raw1 * raw1 + raw2 * raw2 + np.float32(1e-8))
    o["cheb_cos"] = quads(np.concatenate([raw1 / length, raw1 / length], 1))
    o["cheb_sin"] = quads(np.concatenate([-raw2 / length, raw2 / length], 1))
    o["causal"] = quads(token[None, :] <= token[:, None])
    for l, g, bg, wqkv, bqkv, wp, bp, down, up in (
            ("L1_ffn", "Wg", "bg", "Wqkv", "bqkv", "Wproj", "bproj", "A", "Bm"),
            ("L3_ffn", "W_gate", "b_gate", "W_qkv", "b_qkv", "W_proj", "b_proj", "A", "B_lora")):
        x = lambda nm: a[l + "_" + nm]
        o[l + "_gate"], o[l + "_bg"] = x(g).T, x(bg)
        o[l + "_Wqkv"], o[l + "_bqkv"] = x(wqkv).T, x(bqkv)
        o[l + "_Wproj"], o[l + "_bproj"] = x(wp).T, x(bp)
        o[l + "_down"] = x(down).reshape(-1, DIM).T
        o[l + "_up"] = x(up).transpose(0, 2, 1).reshape(-1, 3 * DIM)
    o["L1_ffn_down_bias"], o["L1_ffn_up_bias"] = a["L1_ffn_ba"].reshape(-1), a["L1_ffn_bb"]
    o["L2_attn_qkv"], o["L2_attn_proj"], o["L2_attn_proj_b"] = a["L2_attn_qkv_w"].T, a["L2_attn_proj_w"].T, a["L2_attn_proj_b"]
    h = a["L0_ffn_W2"].shape[1]
    o["L0_ffn_Wg"] = a["L0_ffn_Wg"]
    o["L0_ffn_Win"] = np.concatenate([a["L0_ffn_W1"][..., h:], a["L0_ffn_W1"][..., :h]], 2)
    o["L0_ffn_W2"] = a["L0_ffn_W2"]
    o["L2_ffn_gate"] = a["L2_ffn_gate_weight"].T
    o["L2_ffn_Win"] = np.concatenate([a["L2_ffn_Wg"].transpose(0, 2, 1), a["L2_ffn_Wu"].transpose(0, 2, 1)], 2)
    o["L2_ffn_Wout"] = a["L2_ffn_Wd"].transpose(0, 2, 1)
    o["L2_ffn_shared_in"] = np.concatenate([a["L2_ffn_Ws_g"].T, a["L2_ffn_Ws_u"].T], 1)
    o["L2_ffn_shared_out"] = a["L2_ffn_Ws_d"].T
    o["L3_attn_Wp"], o["L3_attn_bp"] = a["L3_attn_Wp"], a["L3_attn_bp"]
    if "dbg_h" in a:
        o["dbg_h"] = a["dbg_h"]
    return {k: np.ascontiguousarray(v) for k, v in o.items()}


def kernel(**inputs):
    import concourse.bacc as bacc
    from concourse.bass_utils import run_bass_kernel_spmd

    nc = bacc.Bacc("TRN2", target_bir_lowering=False, num_devices=1)
    arrays = layout(inputs)
    ins = {k: nc.dram_tensor("in_" + k, v.shape, mybir.dt.from_np(v.dtype), kind="ExternalInput").ap() for k, v in arrays.items()}
    out = nc.dram_tensor("result", (IMAGES, TOKENS, DIM), F32, kind="ExternalOutput").ap()
    build(nc, ins, out, *_DEBUG)
    r = run_bass_kernel_spmd(nc, [{"in_" + k: v for k, v in arrays.items()}], core_ids=[0])
    return r.results[0]["result"]
```

```python
from contextlib import ExitStack, contextmanager

import numpy as np
import concourse.bass as bass
from concourse import mybir

F32 = mybir.dt.float32
ALU = mybir.AluOpType
ACT = mybir.ActivationFunctionType
AX_X = mybir.AxisListType.X

IMAGES, TOKENS, DIM = 32, 25, 192
HEADS, HEAD_DIM = 12, 16
QUAD = 32
IMG_PER_TILE = 4
P = QUAD * IMG_PER_TILE
TILES = IMAGES // IMG_PER_TILE
HALVES = 2
HALF = DIM // HALVES
GROUPS = HEADS // 4
LN_EPS = 1e-5
LATENT = 32


class Tower:

    def __init__(self, nc, ctx, ins):
        self.nc, self.ctx, self.ins = nc, ctx, ins
        self.scope, self.prefix = ctx, ""
        self.kept = {}
        self.sems = []
        self.y = self.sb("y", [P, TILES, DIM])
        self.moments = self.sb("moments", [P, TILES, 6])
        self.mean_var = self.sb("mean_var", [P, TILES, 2])
        self.rstd = self.sb("rstd", [P, TILES, 1])
        self.mean = self.sb("mean", [P, TILES, 1])
        self.identity = self.sb("identity", [P, P])
        self.eps = self.sb("eps", [P, 1])
        self.is_pad = self.sb("is_pad", [P, 1])
        self.minus_half = self.sb("minus_half", [P, 1])

    def sb(self, name, shape):
        return self.scope.enter_context(self.nc.sbuf_tensor(self.prefix + name, shape, F32))

    @contextmanager
    def scratch(self):
        outer = self.scope
        with ExitStack() as self.scope:
            yield
        self.scope = outer

    def keep(self, name, make):
        if name not in self.kept:
            self.kept[name] = make()
        return self.kept[name]

    def sem(self, name):
        s = self.nc.alloc_semaphore(name=self.prefix + name)
        self.sems.append(s)
        return s

    @contextmanager
    def stage(self, name):
        outer, self.sems = self.sems, []
        self.prefix = name
        with self.scratch():
            yield
        self.nc.clear_and_free_semaphores(self.sems)
        self.nc.all_engine_barrier()
        self.prefix, self.sems = "", outer


def setup(tw):
    nc = tw.nc
    zeroed, ready = tw.sem("identity_zeroed"), tw.sem("identity_ready")
    with nc.Block() as block:

        @block.gpsimd
        def _(pool):
            nc.gpsimd.memset(tw.identity[:], 0.0).then_inc(zeroed, 1)
            nc.gpsimd.memset(tw.eps[:], LN_EPS)
            nc.gpsimd.memset(tw.minus_half[:], -0.5)
            pool.wait_ge(zeroed, 1)
            nc.gpsimd.affine_select(out=tw.identity[:], in_=tw.identity[:], compare_op=ALU.not_equal, fill=1.0,
                                    base=0, pattern=[[-1, P]], channel_multiplier=1).then_inc(ready, 1)
            pool.wait_ge(ready, 1)


def finish_norm(tw, name):
    nc = tw.nc
    aggregated, rooted = tw.sem(name + "_aggregated"), tw.sem(name + "_rooted")
    done = tw.sem(name + "_norm_done")
    with nc.Block() as block:

        @block.vector
        def _(dve):
            for t in range(TILES):
                nc.vector.bn_aggr(tw.mean_var[:, t, :], tw.moments[:, t, :]).then_inc(aggregated, 1)
            dve.wait_ge(aggregated, TILES)
            nc.vector.tensor_copy(tw.mean[:], tw.mean_var[:, :, 0:1])
            dve.wait_ge(rooted, 1)
            nc.vector.reciprocal(tw.rstd[:], tw.rstd[:]).then_inc(done, 1)
            dve.wait_ge(done, 1)

        @block.scalar
        def _(act):
            act.wait_ge(aggregated, TILES)
            nc.scalar.activation(tw.rstd[:], tw.mean_var[:, :, 1:2], ACT.Sqrt, bias=tw.eps[:]).then_inc(rooted, 1)


class AttentionBuffers:

    NAMES = ("normed hT_in_psum hT_ready resid_ready qkv_in_psum qk_padded v_ready heads_in_psum qT_ready "
             "kT_act kT_dve scores_in_psum row_max shifted probs probs_in_psum probs_T v_spread inv_sum out_in_psum out_normed "
             "outT_in_psum outT_ready proj_in_psum y_ready adapter_in_psum adapter_mixed mixT_in_psum mixT_ready masked "
             "y_part v_normed v_scaled head_var head_rstd").split()

    def __init__(self, tw):
        sb = tw.sb
        nc, ctx = tw.nc, tw.ctx
        self.h = sb("h", [P, 2, DIM])
        self.resid = sb("resid", [P, 2, DIM])
        self.hT = sb("hT", [HALF, 2, HALVES, P])
        self.qk = sb("qk", [P, 2, 2 * HEADS, QUAD])
        self.v = sb("v", [P, 2, DIM])
        self.qT = sb("qT", [P, 2, GROUPS, P])
        self.kT = sb("kT", [P, 2, GROUPS, IMG_PER_TILE, 4, TOKENS])
        self.probs = sb("probs", [P, 2, HEADS, QUAD])
        self.pT = sb("pT", [P, 2, GROUPS, P])
        self.v_heads = sb("v_heads", [P, 2, IMG_PER_TILE, GROUPS, 4, HEAD_DIM + 1])
        self.row_max = sb("row_max", [P, 2, HEADS])
        self.inv_sum = sb("inv_sum", [P, 2, HEADS])
        self.out = sb("out", [P, 2, DIM])
        self.outT = sb("outT", [HALF, 2, HALVES, P])
        self.mix = sb("mix", [P, 2, P])
        self.mixT = sb("mixT", [P, 2, 2, P])
        self.weights = sb("mix_weights", [P, 2, 8])
        self.rotated = sb("rotated", [P, 2 * HEADS, HEAD_DIM])
        self.centred = sb("centred", [P, 2 * HEADS, HEAD_DIM])
        self.square = sb("square", [P, 2 * HEADS, HEAD_DIM])
        self.head_sum = sb("head_sum", [P, 2 * HEADS])
        self.head_var = sb("head_var", [P, 2, 2 * HEADS])
        self.head_rstd = sb("head_rstd", [P, 2, 2 * HEADS])
        self.sem = {n: tw.sem("attn_" + n) for n in self.NAMES}
        self.cleared, v_cleared = tw.sem("attn_cleared"), tw.sem("attn_v_cleared")
        self.base = 2

        with nc.Block() as block:

            @block.vector
            def _(dve):
                for s in self.sem.values():
                    dve.sem_inc(s, 2)
                nc.vector.memset(self.qk[:], 0.0).then_inc(self.cleared, 1)
                nc.vector.memset(self.probs[:], 0.0).then_inc(self.cleared, 1)
                dve.wait_ge(v_cleared, 1)
                for a in range(4):
                    q = slice(QUAD * a, QUAD * (a + 1))
                    last = nc.vector.memset(self.v_heads[q, :, :, :, a, HEAD_DIM:HEAD_DIM + 1].rearrange("q b j g o -> q (b j g) o"), 1.0)
                last.then_inc(self.cleared, 1)
                dve.wait_ge(self.cleared, 4)

            @block.gpsimd
            def _(pool):
                nc.gpsimd.memset(self.v_heads[:], 0.0).then_inc(v_cleared, 1)
                nc.gpsimd.memset(self.kT[:], 0.0).then_inc(self.cleared, 1)


def softmax_attention(tw, b, name, kind, wqkv, wproj, bproj, bqkv=None, adapter=None, rope=None):
    nc, base = tw.nc, b.base
    s = b.sem
    scale = HEAD_DIM ** -0.5
    head_step = tw.sem(name + "_head_step")
    steps = {"biased": 0, "adapted": 0, "rope": 8, "unit": 4}[kind]
    proj_cols = wproj.shape[2]

    def n(t):
        return base + t + 1

    with ExitStack() as ctx:
        def pb(nm, shape):
            return ctx.enter_context(nc.psum_tensor(name + nm, shape, F32))

        bank_h, bank_o = pb("bank_h", [P, 512]), pb("bank_o", [P, 512])
        ps_hT = bank_h[0:HALF, 0:HALVES * P].rearrange("q (k n) -> q k n", k=HALVES)
        ps_adapter = bank_h[:, 2 * P:3 * P]
        ps_outT = bank_o[0:HALF, 0:HALVES * P].rearrange("q (k n) -> q k n", k=HALVES)
        ps_mixT = bank_o[:, 2 * P:4 * P].rearrange("q (k n) -> q k n", k=2)
        ps_qk = pb("ps_qk", [P, 2 * HEADS, HEAD_DIM])
        bank_v = pb("bank_v", [P, 512])
        ps_v, ps_y = bank_v[:, 0:DIM], bank_v[:, 0:proj_cols]
        ps_qT = pb("ps_qT", [P, GROUPS, P])
        ps_kT = pb("ps_kT", [P, GROUPS, P])
        ps_s = pb("ps_s", [P, HEADS, TOKENS])
        ps_o = pb("ps_o", [P, GROUPS, 4, HEAD_DIM + 1])

        def tiles(eng, step):
            step(0, None, None, 0)
            step(1, 0, None, 1)
            with eng.Fori(0, TILES - 3, 2) as i:
                step(i + 2, i + 1, i, 0)
                step(i + 3, i + 2, i + 1, 1)
            step(None, TILES - 1, TILES - 2, 0)
            step(None, None, TILES - 1, 1)

        block = ctx.enter_context(nc.Block())

        @block.tensor
        def _(pe):
            def step(a, t, u, p):
                q = 1 - p
                if u is not None:
                    pe.wait_ge(s["probs"], n(u))
                    for g in range(GROUPS):
                        mm = nc.tensor.transpose(ps_kT[:, g, :], b.probs[:, p, 4 * g:4 * g + 4, :], tw.identity[:])
                    mm.then_inc(s["probs_in_psum"], 1)
                if a is not None:
                    pe.wait_ge(s["normed"], n(a))
                    pe.wait_ge(s["hT_ready"], n(a) - 1)
                    if kind == "adapted":
                        pe.wait_ge(s["adapter_mixed"], n(a) - 1)
                    for k in range(HALVES):
                        mm = nc.tensor.transpose(ps_hT[:, k, :], b.h[:, p, k * HALF:(k + 1) * HALF], tw.identity[:])
                    mm.then_inc(s["hT_in_psum"], 1)
                    if kind == "adapted":
                        pe.wait_ge(s["hT_ready"], n(a))
                        for k in range(HALVES):
                            mm = nc.tensor.matmul(ps_adapter, b.hT[:, p, k, :], adapter["down"][:, k, :], start=(k == 0), stop=(k == 1))
                        mm.then_inc(s["adapter_in_psum"], 1)
                if t is not None:
                    pe.wait_ge(s["qk_padded"], n(t))
                    pe.wait_ge(s["qT_ready"], n(t) - 1)
                    pe.wait_ge(s["kT_act"], n(t) - 1)
                    pe.wait_ge(s["kT_dve"], n(t) - 1)
                    pe.wait_ge(s["probs_T"], n(t) - 1)
                    for g in range(GROUPS):
                        nc.tensor.transpose(ps_qT[:, g, :], b.qk[:, q, 4 * g:4 * g + 4, :], tw.identity[:])
                    for g in range(GROUPS):
                        mm = nc.tensor.transpose(ps_kT[:, g, :], b.qk[:, q, HEADS + 4 * g:HEADS + 4 * g + 4, :], tw.identity[:])
                    mm.then_inc(s["heads_in_psum"], 1)
                if a is not None and kind == "adapted":
                    pe.wait_ge(s["adapter_mixed"], n(a))
                    nc.tensor.transpose(ps_mixT[:, 0, :], b.mix[:, p, :], tw.identity[:])
                    nc.tensor.transpose(ps_mixT[0:8, 1, :], b.weights[:, p, :], tw.identity[:]).then_inc(s["mixT_in_psum"], 1)
                if u is not None:
                    pe.wait_ge(s["probs_T"], n(u))
                    pe.wait_ge(s["v_spread"], n(u))
                    pe.wait_ge(s["out_normed"], n(u) - 1)
                    for g in range(GROUPS):
                        for j in range(IMG_PER_TILE):
                            rows = slice(QUAD * j, QUAD * (j + 1))
                            mm = nc.tensor.matmul(ps_o[rows, g, :, :], b.pT[:, p, g, rows], b.v_heads[:, p, j, g, :, :], start=True, stop=True)
                    mm.then_inc(s["out_in_psum"], 1)
                if a is not None:
                    pe.wait_ge(s["hT_ready"], n(a))
                    if kind == "adapted":
                        pe.wait_ge(s["mixT_ready"], n(a))
                    pe.wait_ge(s["qk_padded"], n(a) - 1)
                    if kind != "rope":
                        pe.wait_ge(s["v_ready"], n(a) - 1)
                        if u is not None:
                            pe.wait_ge(s["y_ready"], n(u) - 1)
                    for at, ps in ((0, ps_qk[:]), (2 * DIM, ps_v)):
                        if at == 2 * DIM and kind == "rope":
                            continue
                        cols = slice(at, 2 * DIM if at == 0 else 3 * DIM)
                        adapted = kind == "adapted"
                        for k in range(HALVES):
                            mm = nc.tensor.matmul(ps, b.hT[:, p, k, :], wqkv[:, k, cols], start=(k == 0), stop=(k == 1 and not adapted))
                        if adapted:
                            mm = nc.tensor.matmul(ps, b.mixT[:, p, 0, :], adapter["up"][:, cols], start=False, stop="up_bias" not in adapter)
                            if "up_bias" in adapter:
                                mm = nc.tensor.matmul(ps, b.mixT[0:8, p, 1, :], adapter["up_bias"][:, cols], start=False, stop=True)
                    mm.then_inc(s["qkv_in_psum"], 1)
                if t is not None:
                    pe.wait_ge(s["qT_ready"], n(t))
                    pe.wait_ge(s["kT_act"], n(t))
                    pe.wait_ge(s["kT_dve"], n(t))
                    pe.wait_ge(s["masked" if kind == "rope" else "shifted"], n(t) - 1)
                    for g in range(GROUPS):
                        for j in range(IMG_PER_TILE):
                            rows = slice(QUAD * j, QUAD * (j + 1))
                            mm = nc.tensor.matmul(ps_s[rows, 4 * g:4 * g + 4, :], b.qT[:, q, g, rows], b.kT[:, q, g, j, :, :],
                                                  start=True, stop=True)
                    mm.then_inc(s["scores_in_psum"], 1)
                if u is not None:
                    pe.wait_ge(s["out_normed"], n(u))
                    pe.wait_ge(s["outT_ready"], n(u) - 1)
                    for k in range(HALVES):
                        mm = nc.tensor.transpose(ps_outT[:, k, :], b.out[:, p, k * HALF:(k + 1) * HALF], tw.identity[:])
                    mm.then_inc(s["outT_in_psum"], 1)
                    pe.wait_ge(s["outT_ready"], n(u))
                    pe.wait_ge(s["y_ready"], n(u) - 1)
                    if a is not None and kind != "rope":
                        pe.wait_ge(s["v_ready"], n(a))
                    for k in range(HALVES):
                        mm = nc.tensor.matmul(ps_y, b.outT[:, p, k, :], wproj[:, k, :], start=(k == 0), stop=(k == 1))
                    mm.then_inc(s["proj_in_psum"], 1)

            tiles(pe, step)

        def spread(x, heads):
            return x.unsqueeze(2).to_broadcast([P, heads, HEAD_DIM])

        def rotate_heads(dve, t, p, qk):
            def after(ins, k):
                ins.then_inc(head_step, 1)
                dve.wait_ge(head_step, steps * t + k)

            half = HEAD_DIM // 2
            turn = lambda x, heads, cols: x[:, cols].unsqueeze(1).to_broadcast([P, heads, len(range(HEAD_DIM)[cols])])
            low, high, both = slice(0, half), slice(half, HEAD_DIM), slice(0, HEAD_DIM)
            after(nc.vector.tensor_tensor(b.rotated[:, :, low], ps_qk[:, :, high], turn(rope["sin"], 2 * HEADS, low), ALU.mult), 1)
            after(nc.vector.tensor_tensor(b.rotated[:, :, high], ps_qk[:, :, low], turn(rope["sin"], 2 * HEADS, high), ALU.mult), 2)
            after(nc.vector.tensor_tensor(qk, ps_qk[:], turn(rope["cos"], 2 * HEADS, both), ALU.mult), 3)
            nc.vector.tensor_tensor(qk, qk, b.rotated[:], ALU.add).then_inc(s["qk_padded"], 1)
            dve.wait_ge(s["qk_padded"], n(t))
            kv, c, sq = qk[:, HEADS:], b.centred[:, 0:HEADS], b.square[:, 0:HEADS]
            after(nc.vector.tensor_reduce(b.head_sum[:, 0:HEADS], kv, AX_X, ALU.add), 4)
            after(nc.vector.tensor_scalar(b.head_sum[:, 0:HEADS], b.head_sum[:, 0:HEADS], 1.0 / HEAD_DIM, None, ALU.mult), 5)
            after(nc.vector.tensor_tensor(c, kv, spread(b.head_sum[:, 0:HEADS], HEADS), ALU.subtract), 6)
            after(nc.vector.tensor_tensor(sq, c, c, ALU.mult), 7)
            after(nc.vector.tensor_reduce(b.head_sum[:, 0:HEADS], sq, AX_X, ALU.add), 8)
            nc.vector.tensor_scalar(b.head_var[:, p, 0:HEADS], b.head_sum[:, 0:HEADS], 1.0 / HEAD_DIM, LN_EPS,
                                    ALU.mult, ALU.add).then_inc(s["head_var"], 1)

        def finish_rotated(dve, t, p):
            dve.wait_ge(s["head_rstd"], n(t))
            c = b.centred[:, 0:HEADS]
            v = b.v[:, p, :].rearrange("p (h d) -> p h d", d=HEAD_DIM)
            dve.wait_ge(s["v_spread"], n(t) - 2)
            nc.vector.tensor_tensor(v, c, spread(b.head_rstd[:, p, 0:HEADS], HEADS), ALU.mult).then_inc(s["v_normed"], 1)
            dve.wait_ge(s["v_normed"], n(t))
            nc.vector.tensor_tensor(v, v, rope["gain"][:].unsqueeze(1).to_broadcast([P, HEADS, HEAD_DIM]), ALU.mult).then_inc(s["v_scaled"], 1)
            dve.wait_ge(s["v_scaled"], n(t))
            nc.vector.tensor_tensor(v, v, rope["shift"][:].unsqueeze(1).to_broadcast([P, HEADS, HEAD_DIM]), ALU.add).then_inc(s["v_ready"], 1)

        def unit_heads(dve, t, p, qk):
            def after(ins, k):
                ins.then_inc(head_step, 1)
                dve.wait_ge(head_step, steps * t + k)

            dve.wait_ge(s["v_spread"], n(t) - 2)
            nc.vector.tensor_copy(b.v[:, p, :], ps_v).then_inc(s["v_ready"], 1)
            after(nc.vector.tensor_reduce(b.head_sum[:], ps_qk[:], AX_X, ALU.add), 1)
            after(nc.vector.tensor_scalar(b.head_sum[:], b.head_sum[:], 1.0 / HEAD_DIM, None, ALU.mult), 2)
            nc.vector.tensor_tensor(b.centred[:], ps_qk[:], spread(b.head_sum[:], 2 * HEADS), ALU.subtract).then_inc(s["masked"], 1)
            dve.wait_ge(s["masked"], n(t))
            after(nc.vector.tensor_tensor(b.square[:], b.centred[:], b.centred[:], ALU.mult), 3)
            after(nc.vector.tensor_reduce(b.head_sum[:], b.square[:], AX_X, ALU.add), 4)
            nc.vector.tensor_scalar(b.head_var[:, p, :], b.head_sum[:], 1.0 / (HEAD_DIM - 1), tw.is_pad[:],
                                    ALU.mult, ALU.add).then_inc(s["head_var"], 1)

        def finish_unit(dve, t, t_parity, qk):
            dve.wait_ge(s["head_rstd"], n(t))
            nc.vector.tensor_tensor(qk, b.centred[:], spread(b.head_rstd[:, t_parity, :], 2 * HEADS), ALU.mult).then_inc(s["qk_padded"], 1)

        @block.vector
        def _(dve):
            def step(a, t, u, p):
                q = 1 - p
                if a is not None:
                    dve.wait_ge(s["hT_in_psum"], n(a) - 2)
                    dve.wait_ge(s["resid_ready"], n(a) - 2)
                    nc.vector.tensor_scalar(b.h[:, p, :], tw.y[:, a, :], tw.mean[:, a, :], tw.rstd[:, a, :],
                                            ALU.subtract, ALU.mult).then_inc(s["normed"], 1)
                    if kind == "adapted":
                        dve.wait_ge(s["adapter_in_psum"], n(a))
                        dve.wait_ge(s["mixT_in_psum"], n(a) - 2)
                        mix, source = b.mix[:, p, :], ps_adapter
                        if "down_bias" in adapter:
                            nc.vector.tensor_tensor(mix, source, adapter["down_bias"][:], ALU.add).then_inc(s["masked"], 1)
                            dve.wait_ge(s["masked"], n(a))
                            source = mix
                        nc.vector.tensor_copy(b.weights[:, p, :], adapter["combine"][:, a, :])
                        nc.vector.tensor_tensor(mix.rearrange("p (e r) -> p e r", e=8), source.rearrange("p (e r) -> p e r", e=8),
                                                adapter["combine"][:, a, :].unsqueeze(2).to_broadcast([P, 8, P // 8]),
                                                ALU.mult).then_inc(s["adapter_mixed"], 1)
                if t is not None:
                    dve.wait_ge(s["heads_in_psum"], n(t))
                    dve.wait_ge(s["scores_in_psum"], n(t) - 2)
                    for head in (2, 3):
                        rows = slice(QUAD * head, QUAD * (head + 1))
                        ins = nc.vector.tensor_copy(b.kT[rows, q, :, :, head, :],
                                                    ps_kT[rows, :, :].rearrange("p g (j n) -> p g j n", n=QUAD)[:, :, :, 0:TOKENS])
                    ins.then_inc(s["kT_dve"], 1)
                    dve.wait_ge(s["v_ready"], n(t))
                    dve.wait_ge(s["out_in_psum"], n(t) - 2)
                    for j in range(IMG_PER_TILE):
                        for head in range(4):
                            v = b.v[QUAD * j:QUAD * (j + 1), q, :].rearrange("n (g a d) -> n g a d", g=GROUPS, a=4)[:, :, head, :]
                            ins = nc.vector.tensor_copy(b.v_heads[QUAD * head:QUAD * (head + 1), q, j, :, head, 0:HEAD_DIM], v)
                    ins.then_inc(s["v_spread"], 1)
                if u is not None:
                    dve.wait_ge(s["out_in_psum"], n(u))
                    dve.wait_ge(s["outT_in_psum"], n(u) - 2)
                    by_head = ps_o[:].rearrange("p g a d -> p (g a) d")
                    nc.vector.reciprocal(b.inv_sum[:, p, :].unsqueeze(2), by_head[:, :, HEAD_DIM:HEAD_DIM + 1]).then_inc(s["inv_sum"], 1)
                    dve.wait_ge(s["inv_sum"], n(u))
                    nc.vector.tensor_tensor(b.out[:, p, :].rearrange("p (h d) -> p h d", d=HEAD_DIM), by_head[:, :, 0:HEAD_DIM],
                                            b.inv_sum[:, p, :].unsqueeze(2).to_broadcast([P, HEADS, HEAD_DIM]),
                                            ALU.mult).then_inc(s["out_normed"], 1)
                if a is not None:
                    dve.wait_ge(s["qkv_in_psum"], n(a))
                    dve.wait_ge(s["heads_in_psum"], n(a) - 2)
                    heads_of = lambda x: x.rearrange("p (h d) -> p h d", d=HEAD_DIM)
                    qk = b.qk[:, p, :, 0:HEAD_DIM]
                    if bqkv is not None:
                        nc.vector.tensor_tensor(qk, ps_qk[:], heads_of(bqkv[:, 0:2 * DIM]), ALU.add).then_inc(s["qk_padded"], 1)
                        dve.wait_ge(s["v_spread"], n(a) - 2)
                        nc.vector.tensor_tensor(b.v[:, p, :], ps_v, bqkv[:, 2 * DIM:3 * DIM], ALU.add).then_inc(s["v_ready"], 1)
                    if kind == "rope":
                        rotate_heads(dve, a, p, qk)
                    if kind == "unit":
                        unit_heads(dve, a, p, qk)
                if t is not None:
                    dve.wait_ge(s["scores_in_psum"], n(t))
                    dve.wait_ge(s["probs_in_psum"], n(t) - 2)
                    scores = ps_s[:]
                    if kind == "rope":
                        scores = b.probs[:, q, :, 0:TOKENS]
                        nc.vector.tensor_tensor(scores, ps_s[:], rope["mask"][:].unsqueeze(1).to_broadcast([P, HEADS, TOKENS]),
                                                ALU.add).then_inc(s["masked"], 1)
                        dve.wait_ge(s["masked"], n(t))
                    nc.vector.tensor_reduce(b.row_max[:, q, :], scores, AX_X, ALU.max).then_inc(s["row_max"], 1)
                    dve.wait_ge(s["row_max"], n(t))
                    nc.vector.tensor_tensor(b.probs[:, q, :, 0:TOKENS], scores,
                                            b.row_max[:, q, :].unsqueeze(2).to_broadcast([P, HEADS, TOKENS]),
                                            ALU.subtract).then_inc(s["shifted"], 1)
                if a is not None:
                    if kind == "rope":
                        finish_rotated(dve, a, p)
                    if kind == "unit":
                        finish_unit(dve, a, p, qk)
                if u is not None:
                    dve.wait_ge(s["proj_in_psum"], n(u))
                    dve.wait_ge(s["resid_ready"], n(u))
                    if kind == "rope":
                        nc.vector.scalar_tensor_tensor(out=b.resid[:, p, :], in0=ps_y[:, 0:DIM], scalar=rope["context"][:], in1=b.resid[:, p, :],
                                                       op0=ALU.mult, op1=ALU.add).then_inc(s["y_part"], 1)
                        dve.wait_ge(s["y_part"], n(u))
                        nc.vector.scalar_tensor_tensor(out=tw.y[:, u, :], in0=ps_y[:, DIM:2 * DIM], scalar=rope["latent"][:], in1=b.resid[:, p, :],
                                                       op0=ALU.mult, op1=ALU.add).then_inc(s["y_ready"], 1)
                    else:
                        nc.vector.tensor_tensor(tw.y[:, u, :], ps_y, b.resid[:, p, :], ALU.add).then_inc(s["y_ready"], 1)
                    dve.wait_ge(s["y_ready"], n(u))
                    nc.vector.bn_stats(tw.moments[:, u, :], tw.y[:, u, :])

            tiles(dve, step)

        @block.scalar
        def _(act):
            def step(a, t, u, p):
                q = 1 - p
                if u is not None:
                    act.wait_ge(s["probs_in_psum"], n(u))
                    act.wait_ge(s["out_in_psum"], n(u) - 2)
                    nc.scalar.copy(b.pT[:, p, :, :], ps_kT[:]).then_inc(s["probs_T"], 1)
                if a is not None:
                    act.wait_ge(s["hT_in_psum"], n(a))
                    act.wait_ge(s["qkv_in_psum"], n(a) - 2)
                    nc.scalar.copy(b.hT[:, p, :, :], ps_hT[:]).then_inc(s["hT_ready"], 1)
                if t is not None:
                    act.wait_ge(s["heads_in_psum"], n(t))
                    act.wait_ge(s["scores_in_psum"], n(t) - 2)
                    nc.scalar.copy(b.qT[:, q, :, :], ps_qT[:]).then_inc(s["qT_ready"], 1)
                    for head in (0, 1):
                        rows = slice(QUAD * head, QUAD * (head + 1))
                        ins = nc.scalar.copy(b.kT[rows, q, :, :, head, :],
                                             ps_kT[rows, :, :].rearrange("p g (j n) -> p g j n", n=QUAD)[:, :, :, 0:TOKENS])
                    ins.then_inc(s["kT_act"], 1)
                if a is not None and kind == "adapted":
                    act.wait_ge(s["mixT_in_psum"], n(a))
                    nc.scalar.copy(b.mixT[:, p, 0, :], ps_mixT[:, 0, :])
                    nc.scalar.copy(b.mixT[0:8, p, 1, :], ps_mixT[0:8, 1, :]).then_inc(s["mixT_ready"], 1)
                if u is not None:
                    act.wait_ge(s["outT_in_psum"], n(u))
                    act.wait_ge(s["proj_in_psum"], n(u) - 2)
                    nc.scalar.copy(b.outT[:, p, :, :], ps_outT[:]).then_inc(s["outT_ready"], 1)
                if t is not None:
                    act.wait_ge(s["shifted"], n(t))
                    nc.scalar.activation(b.probs[:, q, :, 0:TOKENS], b.probs[:, q, :, 0:TOKENS], ACT.Exp,
                                         scale=scale).then_inc(s["probs"], 1)

            tiles(act, step)

        @block.gpsimd
        def _(pool):
            def step(a, t, u, p):
                q = 1 - p
                if t is not None:
                    pool.wait_ge(s["normed"], n(t))
                    pool.wait_ge(s["y_ready"], n(t) - 2)
                    nc.gpsimd.tensor_tensor(b.resid[:, q, :], b.h[:, q, :], bproj[:], ALU.add).then_inc(s["resid_ready"], 1)
                if a is not None and kind in ("rope", "unit"):
                    heads = HEADS if kind == "rope" else 2 * HEADS
                    pool.wait_ge(s["head_var"], n(a))
                    nc.gpsimd.tensor_tensor(b.head_rstd[:, p, 0:heads], b.head_var[:, p, 0:heads], tw.minus_half[:].to_broadcast([P, heads]),
                                            ALU.pow).then_inc(s["head_rstd"], 1)

            tiles(pool, step)


BRANCHES = 4
ALL_HEADS = BRANCHES * HEADS


def branch_attention(tw, name, w):
    nc = tw.nc
    names = ("prep_s prep_m prep_w prep_b prep_done normed hT_in_psum hT_ready resid_ready proj_in_psum queries_ready key_var key_rstd key_scale "
             "qk_ready v_ready v_spread heads_in_psum qT_ready kT_ready scores_in_psum magnitude exp log softplus masked gate_exp "
             "gate_log gate weights wT_in_psum wT_ready out_in_psum sunk inv_sum out_part out_ready outT_in_psum outT_ready "
             "y_in_psum y_ready cleared cleared_pool v_cleared").split()
    s = {k: tw.sem(name + "_" + k) for k in names}
    rotate_step, ROTATE_STEPS = tw.sem(name + "_rotate_step"), 11
    QK = ALL_HEADS + HEADS
    KG = ALL_HEADS // 4
    PREP = ALL_HEADS * HEAD_DIM // P
    gate_scale = float(np.pi / np.sqrt(3.0))

    def n(t):
        return 2 + t + 1

    def tiles(eng, step):
        step(0, None, None, 0)
        step(1, 0, None, 1)
        with eng.Fori(0, TILES - 3, 2) as i:
            step(i + 2, i + 1, i, 0)
            step(i + 3, i + 2, i + 1, 1)
        step(None, TILES - 1, TILES - 2, 0)
        step(None, None, TILES - 1, 1)

    def per_head(x):
        return x.rearrange("p (h d) -> p h d", d=HEAD_DIM)

    with ExitStack() as ctx:
        def sb(nm, shape):
            return ctx.enter_context(nc.sbuf_tensor(name + nm, shape, F32))

        def pb(nm, shape):
            return ctx.enter_context(nc.psum_tensor(name + nm, shape, F32))

        mix = sb("mix", [P, PREP, P])
        eye_a = sb("eye_a", [P, P])
        wq = sb("wq", [HALF, HALVES, ALL_HEADS * HEAD_DIM])
        bias = sb("bias", [P, QK * HEAD_DIM])
        bo = sb("bo", [P, DIM])
        sink_v = sb("sink_v", [P, DIM])
        h = sb("h", [P, 2, DIM])
        resid = sb("resid", [P, 2, DIM])
        hT = sb("hT", [HALF, 2, HALVES, P])
        flat = sb("flat", [P, QK, HEAD_DIM])
        swapped = sb("swapped", [P, QK, HEAD_DIM])
        key_sq = sb("key_sq", [P, HEADS, HEAD_DIM])
        key_var = sb("key_var", [P, HEADS])
        key_rstd = sb("key_rstd", [P, HEADS])
        qk = sb("qk", [P, QK, QUAD])
        v = sb("v", [P, 2, DIM])
        v_heads = sb("v_heads", [P, 2, IMG_PER_TILE, GROUPS, 4, HEAD_DIM + 1])
        qT = sb("qT", [P, GROUPS, IMG_PER_TILE, BRANCHES, QUAD])
        kT = sb("kT", [P, GROUPS, IMG_PER_TILE, 4, TOKENS])
        work = sb("work", [P, ALL_HEADS, TOKENS])
        weight = sb("weight", [P, ALL_HEADS, QUAD])
        wT = sb("wT", [P, IMG_PER_TILE * GROUPS, P])
        row_sum = sb("row_sum", [P, ALL_HEADS])
        inv_sum = sb("inv_sum", [P, ALL_HEADS])
        out = sb("out", [P, IMG_PER_TILE, DIM])
        outT = sb("outT", [HALF, BRANCHES, HALVES, IMG_PER_TILE, QUAD])

        turn_bank = pb("turn_bank", [P, 4, 512])
        bank_h = pb("bank_h", [P, 512])
        bank_t = pb("bank_t", [P, 512])
        bank_o = pb("bank_o", [P, 2, 512])
        ps_hT = bank_h[0:HALF, 0:HALVES * P].rearrange("q (k n) -> q k n", k=HALVES)
        ps_s = turn_bank[:, :, 0:HEADS * TOKENS]
        ps_kT = turn_bank[:, 0:GROUPS, GROUPS * P:(GROUPS + 1) * P]
        turned = (bank_t, bank_h)
        CHUNKS = IMG_PER_TILE * GROUPS // 4
        OUT_COLS = 4 * (HEAD_DIM + 1)

        def work_rows(x):
            return x[:].rearrange("p (j h) n -> p j (h n)", j=IMG_PER_TILE)

        block = ctx.enter_context(nc.Block())

        @block.tensor
        def _(pe):
            pe.wait_ge(s["prep_m"], PREP)
            for g in range(PREP):
                if g:
                    pe.wait_ge(s["prep_b"], g)
                for k in range(HALVES):
                    nc.tensor.matmul(turn_bank[0:HALF, 0, k * P:(k + 1) * P], w["Wq"][:, g, k * HALF:(k + 1) * HALF], mix[:, g, :],
                                     start=True, stop=True)
                nc.tensor.matmul(turn_bank[:, 0, 2 * P:3 * P], w["bq"][:, g:g + 1].to_broadcast([P, P]), mix[:, g, :],
                                 start=True, stop=True).then_inc(s["prep_w"], 1)
            pe.wait_ge(s["prep_b"], PREP)
            pe.wait_ge(s["prep_done"], 1)

            def step(a, t, u, p):
                if u is not None:
                    pe.wait_ge(s["weights"], n(u))
                    pe.wait_ge(s["outT_ready"], 2 * n(u) - 2)
                    for c in range(CHUNKS):
                        if c == 2:
                            pe.wait_ge(s["wT_ready"], 3 * n(u) - 2)
                        for i in range(4):
                            x = 4 * c + i
                            mm = nc.tensor.transpose(turned[c % 2][:, i * P:(i + 1) * P], weight[:, 4 * x:4 * x + 4, :], tw.identity[:])
                        mm.then_inc(s["wT_in_psum"], 1)
                if a is not None:
                    pe.wait_ge(s["normed"], n(a))
                    pe.wait_ge(s["hT_ready"], n(a) - 1)
                    if u is not None:
                        pe.wait_ge(s["wT_ready"], 3 * n(u) - 1)
                    for k in range(HALVES):
                        mm = nc.tensor.transpose(ps_hT[:, k, :], h[:, p, k * HALF:(k + 1) * HALF], tw.identity[:])
                    mm.then_inc(s["hT_in_psum"], 1)
                if u is not None:
                    pe.wait_ge(s["wT_ready"], 3 * n(u))
                    pe.wait_ge(s["v_spread"], n(u))
                    pe.wait_ge(s["y_ready"], n(u) - 1)
                    pe.wait_ge(s["out_part"], 2 * n(u) - 2)
                    for j in range(IMG_PER_TILE):
                        for g in range(GROUPS):
                            at = (j % 2 * GROUPS + g) * OUT_COLS
                            mm = nc.tensor.matmul(bank_o[:, j // 2, at:at + OUT_COLS], wT[:, j * GROUPS + g, :], v_heads[:, p, j, g, :, :],
                                                  start=True, stop=True)
                    mm.then_inc(s["out_in_psum"], 1)
                if a is not None:
                    pe.wait_ge(s["hT_ready"], n(a))
                    pe.wait_ge(s["softplus"], n(a) - 1)
                    pe.wait_ge(s["magnitude"], n(a) - 1)
                    for c in (2, 0, 1):
                        for k in range(HALVES):
                            rhs = wq[:, k, c * 2 * DIM:(c + 1) * 2 * DIM] if c < 2 else w["Wkv"][:, k, :]
                            mm = nc.tensor.matmul(turn_bank[:, c, 0:2 * DIM], hT[:, p, k, :], rhs, start=(k == 0), stop=(k == 1))
                    mm.then_inc(s["proj_in_psum"], 1)
                if u is not None:
                    pe.wait_ge(s["out_ready"], n(u))
                    for half in range(2):
                        for j in (2 * half, 2 * half + 1):
                            for k in range(HALVES):
                                at = ((j % 2) * HALVES + k) * P
                                mm = nc.tensor.transpose(turned[half][0:HALF, at:at + P], out[:, j, k * HALF:(k + 1) * HALF], tw.identity[:])
                        mm.then_inc(s["outT_in_psum"], 1)
                    pe.wait_ge(s["outT_ready"], 2 * n(u))
                    for c in range(BRANCHES):
                        for k in range(HALVES):
                            mm = nc.tensor.matmul(bank_o[:, 0, 0:DIM], outT[:, c, k].rearrange("q j n -> q (j n)"), w["Wo"][:, c, k, :],
                                                  start=(c == 0 and k == 0), stop=(c == BRANCHES - 1 and k == 1))
                    mm.then_inc(s["y_in_psum"], 1)
                if a is not None:
                    pe.wait_ge(s["qk_ready"], n(a))
                    pe.wait_ge(s["v_ready"], n(a))
                    for c in range(BRANCHES):
                        for g in range(GROUPS):
                            first = c * HEADS + 4 * g
                            mm = nc.tensor.transpose(turn_bank[:, c, g * P:(g + 1) * P], qk[:, first:first + 4, :], tw.identity[:])
                    for g in range(GROUPS):
                        first = ALL_HEADS + 4 * g
                        mm = nc.tensor.transpose(ps_kT[:, g, :], qk[:, first:first + 4, :], tw.identity[:])
                    mm.then_inc(s["heads_in_psum"], 1)
                    pe.wait_ge(s["qT_ready"], n(a))
                    pe.wait_ge(s["kT_ready"], n(a))
                    for j in range(IMG_PER_TILE):
                        for g in range(GROUPS):
                            mm = nc.tensor.matmul(ps_s[:, j, g * 4 * TOKENS:(g + 1) * 4 * TOKENS],
                                                  qT[:, g, j].rearrange("p c n -> p (c n)"), kT[:, g, j, :, :], start=True, stop=True)
                    mm.then_inc(s["scores_in_psum"], 1)

            tiles(pe, step)

        @block.vector
        def _(dve):
            for k in names[names.index("normed"):names.index("cleared")]:
                dve.sem_inc(s[k], 6 if k in ("wT_in_psum", "wT_ready") else 4 if k in ("out_part", "outT_ready", "outT_in_psum") else 2)
            nc.vector.tensor_tensor(eye_a[:], w["A"][:], w["AT"][:], ALU.subtract).then_inc(s["prep_s"], 1)
            dve.wait_ge(s["prep_s"], 1)
            nc.vector.tensor_tensor(eye_a[:], eye_a[:], tw.identity[:], ALU.add).then_inc(s["prep_s"], 1)
            dve.wait_ge(s["prep_s"], 2)
            for g in range(PREP):
                nc.vector.scalar_tensor_tensor(out=mix[:, g, :], in0=tw.identity[:], scalar=w["diagonal"][:, g:g + 1], in1=eye_a[:],
                                               op0=ALU.mult, op1=ALU.add).then_inc(s["prep_m"], 1)
            for g in range(PREP):
                dve.wait_ge(s["prep_w"], g + 1)
                nc.vector.tensor_copy(wq[:, :, g * P:(g + 1) * P], turn_bank[0:HALF, 0, 0:2 * P].rearrange("q (k n) -> q k n", k=HALVES))
                nc.vector.tensor_copy(bias[:, g * P:(g + 1) * P], turn_bank[:, 0, 2 * P:3 * P]).then_inc(s["prep_b"], 1)
            nc.vector.tensor_copy(bias[:, ALL_HEADS * HEAD_DIM:], w["bk"][:]).then_inc(s["prep_s"], 1)
            nc.vector.tensor_tensor(per_head(sink_v[:]), per_head(w["v_null"][:]), w["sink"][:].unsqueeze(2).to_broadcast([P, HEADS, HEAD_DIM]),
                                    ALU.mult).then_inc(s["prep_s"], 1)
            nc.vector.tensor_tensor(bo[:], w["bo"][:, 0:DIM], w["bo"][:, DIM:2 * DIM], ALU.add).then_inc(s["prep_s"], 1)
            for c in (2, 3):
                dve.wait_ge(s["prep_s"], 3 + c)
                nc.vector.tensor_tensor(bo[:], bo[:], w["bo"][:, c * DIM:(c + 1) * DIM], ALU.add).then_inc(s["prep_s"], 1)
            dve.wait_ge(s["prep_s"], 7)
            nc.vector.tensor_scalar(bo[:], bo[:], 1.0 / BRANCHES, None, ALU.mult).then_inc(s["prep_s"], 1)
            nc.vector.memset(weight[:], 0.0).then_inc(s["prep_s"], 1)
            dve.wait_ge(s["prep_s"], 9)
            dve.wait_ge(s["cleared"], 1)
            for head in range(4):
                rows = slice(QUAD * head, QUAD * (head + 1))
                ins = nc.vector.memset(v_heads[rows, :, :, :, head, HEAD_DIM:HEAD_DIM + 1].rearrange("q b j g o -> q (b j g) o"), 1.0)
            ins.then_inc(s["v_cleared"], 1)
            dve.wait_ge(s["v_cleared"], 1)
            dve.wait_ge(s["prep_b"], PREP)
            dve.sem_inc(s["prep_done"], 1)

            def rotate(at, a, k, heads_from, first):
                half = HEAD_DIM // 2
                lo, hi = slice(0, half), slice(half, HEAD_DIM)
                count = at.stop - at.start
                table = lambda x, cols: x[:, cols].unsqueeze(1).to_broadcast([P, count, len(range(HEAD_DIM)[cols])])
                for bank in heads_from:
                    heads = slice(at.start + 2 * HEADS * (bank - heads_from[0]), min(at.stop, at.start + 2 * HEADS * (bank - heads_from[0] + 1)))
                    ins = nc.vector.tensor_tensor(flat[:, heads, :], per_head(turn_bank[:, bank, 0:(heads.stop - heads.start) * HEAD_DIM]),
                                                  per_head(bias[:])[:, heads, :], ALU.add)
                after(ins, a, k)
                after(nc.vector.tensor_tensor(swapped[:, at, lo], flat[:, at, hi], table(w["sin"], lo), ALU.mult), a, k + 1)
                after(nc.vector.tensor_tensor(swapped[:, at, hi], flat[:, at, lo], table(w["sin"], hi), ALU.mult), a, k + 2)
                after(nc.vector.tensor_tensor(flat[:, at, :], flat[:, at, :], table(w["cos"], slice(0, HEAD_DIM)), ALU.mult), a, k + 3)
                if first:
                    dve.wait_ge(s["heads_in_psum"], n(a) - 1)
                return nc.vector.tensor_tensor(qk[:, at, 0:HEAD_DIM], flat[:, at, :], swapped[:, at, :], ALU.add)

            def after(ins, a, k):
                ins.then_inc(rotate_step, 1)
                dve.wait_ge(rotate_step, ROTATE_STEPS * a + k)

            def step(a, t, u, p):
                q = 1 - p
                if a is not None:
                    dve.wait_ge(s["hT_in_psum"], n(a) - 2)
                    dve.wait_ge(s["resid_ready"], n(a) - 2)
                    nc.vector.tensor_scalar(h[:, p, :], tw.y[:, a, :], tw.mean[:, a, :], tw.rstd[:, a, :],
                                            ALU.subtract, ALU.mult).then_inc(s["normed"], 1)
                if t is not None:
                    wts = weight[:, :, 0:TOKENS]
                    dve.wait_ge(s["log"], n(t))
                    nc.vector.scalar_tensor_tensor(out=work_rows(work), in0=ps_s, scalar=0.0, in1=work_rows(work),
                                                   op0=ALU.max, op1=ALU.add).then_inc(s["softplus"], 1)
                    dve.wait_ge(s["softplus"], n(t))
                    dve.wait_ge(s["wT_in_psum"], 3 * n(t) - 3)
                    nc.vector.tensor_tensor(wts, work[:], w["causal"][:].unsqueeze(1).to_broadcast([P, ALL_HEADS, TOKENS]),
                                            ALU.mult).then_inc(s["masked"], 1)
                    dve.wait_ge(s["v_ready"], n(t))
                    dve.wait_ge(s["out_in_psum"], n(t) - 2)
                    for j in range(IMG_PER_TILE):
                        for head in range(4):
                            values = v[QUAD * j:QUAD * (j + 1), q, :].rearrange("n (g a d) -> n g a d", g=GROUPS, a=4)[:, :, head, :]
                            ins = nc.vector.tensor_copy(v_heads[QUAD * head:QUAD * (head + 1), q, j, :, head, 0:HEAD_DIM], values)
                    ins.then_inc(s["v_spread"], 1)
                    dve.wait_ge(s["gate"], n(t))
                    dve.wait_ge(s["masked"], n(t))
                    nc.vector.tensor_tensor(wts, wts, work[:], ALU.mult).then_inc(s["weights"], 1)
                if u is not None:
                    dve.wait_ge(s["out_in_psum"], n(u))
                    for half in range(2):
                        images = slice(2 * half, 2 * half + 2)
                        x = bank_o[:, half, 0:2 * GROUPS * OUT_COLS].rearrange("p (j h d) -> p j h d", j=2, d=HEAD_DIM + 1)
                        nc.vector.scalar_tensor_tensor(out=row_sum[:, 2 * half * HEADS:2 * (half + 1) * HEADS].rearrange("p (j h) -> p j h", j=2),
                                                       in0=x[:, :, :, HEAD_DIM], scalar=1e-6,
                                                       in1=w["sink"][:].unsqueeze(1).to_broadcast([P, 2, HEADS]),
                                                       op0=ALU.add, op1=ALU.add).then_inc(s["sunk"], 1)
                        if half == 0:
                            dve.wait_ge(s["outT_in_psum"], 2 * n(u) - 2)
                        nc.vector.tensor_tensor(out[:, images, :].rearrange("p j (h d) -> p j h d", d=HEAD_DIM), x[:, :, :, 0:HEAD_DIM],
                                                per_head(sink_v[:]).unsqueeze(1).to_broadcast([P, 2, HEADS, HEAD_DIM]), ALU.add).then_inc(s["out_part"], 1)
                    dve.wait_ge(s["sunk"], 2 * n(u) - 2)
                    nc.vector.reciprocal(inv_sum[:], row_sum[:]).then_inc(s["inv_sum"], 1)
                    dve.wait_ge(s["inv_sum"], n(u))
                    dve.wait_ge(s["out_part"], 2 * n(u))
                    o = per_head(out[:].rearrange("p j n -> p (j n)"))
                    nc.vector.tensor_tensor(o, o, inv_sum[:].unsqueeze(2).to_broadcast([P, ALL_HEADS, HEAD_DIM]), ALU.mult).then_inc(s["out_ready"], 1)
                if a is not None:
                    dve.wait_ge(s["proj_in_psum"], n(a))
                    keys = qk[:, ALL_HEADS:, 0:HEAD_DIM]
                    after(rotate(slice(ALL_HEADS, QK), a, 1, (2,), True), a, 5)
                    nc.vector.tensor_tensor(v[:, p, :], turn_bank[:, 2, DIM:2 * DIM], w["bv"][:], ALU.add).then_inc(s["v_ready"], 1)
                    after(nc.vector.tensor_tensor(key_sq[:], keys, keys, ALU.mult), a, 6)
                    after(nc.vector.tensor_reduce(key_var[:], key_sq[:], AX_X, ALU.add), a, 7)
                    nc.vector.tensor_scalar(key_var[:], key_var[:], 1e-6, None, ALU.max).then_inc(s["key_var"], 1)
                    rotate(slice(0, ALL_HEADS), a, 8, (0, 1), False).then_inc(s["queries_ready"], 1)
                    dve.wait_ge(s["key_rstd"], n(a))
                    nc.vector.tensor_scalar(key_rstd[:], key_rstd[:], HEAD_DIM ** -0.5, None, ALU.mult).then_inc(s["key_scale"], 1)
                    dve.wait_ge(s["key_scale"], n(a))
                    dve.wait_ge(s["queries_ready"], n(a))
                    nc.vector.tensor_tensor(keys, keys, key_rstd[:].unsqueeze(2).to_broadcast([P, HEADS, HEAD_DIM]), ALU.mult).then_inc(s["qk_ready"], 1)
                if u is not None:
                    dve.wait_ge(s["y_in_psum"], n(u))
                    dve.wait_ge(s["resid_ready"], n(u))
                    nc.vector.scalar_tensor_tensor(out=tw.y[:, u, :], in0=bank_o[:, 0, 0:DIM], scalar=1.0 / BRANCHES, in1=resid[:, p, :],
                                                   op0=ALU.mult, op1=ALU.add).then_inc(s["y_ready"], 1)
                    dve.wait_ge(s["y_ready"], n(u))
                    nc.vector.bn_stats(tw.moments[:, u, :], tw.y[:, u, :])

            tiles(dve, step)

        @block.scalar
        def _(act):
            def copy_weights(u, c):
                act.wait_ge(s["wT_in_psum"], 3 * n(u) - 2 + c)
                nc.scalar.copy(wT[:, 4 * c:4 * c + 4, :].rearrange("p x n -> p (x n)"), turned[c % 2][:]).then_inc(s["wT_ready"], 1)

            def step(a, t, u, p):
                if t is not None:
                    act.wait_ge(s["scores_in_psum"], n(t))
                    act.wait_ge(s["weights"], n(t) - 1)
                    nc.scalar.activation(work_rows(work), ps_s, ACT.Abs).then_inc(s["magnitude"], 1)
                    act.wait_ge(s["magnitude"], n(t))
                    nc.scalar.activation(work[:], work[:], ACT.Exp, scale=-1.0).then_inc(s["exp"], 1)
                if u is not None:
                    act.wait_ge(s["out_in_psum"], n(u) - 1)
                    copy_weights(u, 0)
                    copy_weights(u, 1)
                if t is not None:
                    act.wait_ge(s["exp"], n(t))
                    nc.scalar.activation(work[:], work[:], ACT.Ln, bias=1.0).then_inc(s["log"], 1)
                if u is not None:
                    copy_weights(u, 2)
                if a is not None:
                    act.wait_ge(s["hT_in_psum"], n(a))
                    act.wait_ge(s["proj_in_psum"], n(a) - 2)
                    nc.scalar.copy(hT[:, p, :, :], ps_hT).then_inc(s["hT_ready"], 1)
                if t is not None:
                    act.wait_ge(s["masked"], n(t))
                    nc.scalar.activation(work[:], weight[:, :, 0:TOKENS], ACT.Exp, scale=-gate_scale).then_inc(s["gate_exp"], 1)
                    act.wait_ge(s["gate_exp"], n(t))
                    nc.scalar.activation(work[:], work[:], ACT.Ln, bias=1.0).then_inc(s["gate_log"], 1)
                    act.wait_ge(s["gate_log"], n(t))
                    nc.scalar.activation(work[:], work[:], ACT.Exp, scale=-1.0).then_inc(s["gate"], 1)
                if u is not None:
                    act.wait_ge(s["y_in_psum"], n(u) - 1)
                    for half in range(2):
                        act.wait_ge(s["outT_in_psum"], 2 * n(u) - 1 + half)
                        for j in (2 * half, 2 * half + 1):
                            at = (j % 2) * HALVES * P
                            ins = nc.scalar.copy(outT[:, :, :, j, :].rearrange("q c k n -> q k c n"),
                                                 turned[half][0:HALF, at:at + HALVES * P].rearrange("q (k c n) -> q k c n", k=HALVES, c=BRANCHES))
                        ins.then_inc(s["outT_ready"], 1)
                if a is not None:
                    act.wait_ge(s["heads_in_psum"], n(a))
                    act.wait_ge(s["scores_in_psum"], n(a) - 1)
                    for head in range(4):
                        rows = slice(QUAD * head, QUAD * (head + 1))
                        ins = nc.scalar.copy(kT[rows, :, :, head, :], ps_kT[rows].rearrange("p g (j n) -> p g j n", n=QUAD)[:, :, :, 0:TOKENS])
                    ins.then_inc(s["kT_ready"], 1)
                    for c in range(BRANCHES):
                        ins = nc.scalar.copy(qT[:, :, :, c, :], turn_bank[:, c, 0:GROUPS * P].rearrange("p (g j n) -> p g j n", g=GROUPS, n=QUAD))
                    ins.then_inc(s["qT_ready"], 1)

            tiles(act, step)

        @block.gpsimd
        def _(pool):
            nc.gpsimd.memset(kT[:], 0.0).then_inc(s["cleared_pool"], 1)
            nc.gpsimd.memset(qk[:], 0.0).then_inc(s["cleared_pool"], 1)
            nc.gpsimd.memset(v_heads[:], 0.0).then_inc(s["cleared_pool"], 1)
            pool.wait_ge(s["cleared_pool"], 3)
            pool.sem_inc(s["cleared"], 1)
            pool.wait_ge(s["prep_done"], 1)

            def step(a, t, u, p):
                q = 1 - p
                if t is not None:
                    pool.wait_ge(s["normed"], n(t))
                    pool.wait_ge(s["y_ready"], n(t) - 2)
                    nc.gpsimd.tensor_tensor(resid[:, q, :], h[:, q, :], bo[:], ALU.add).then_inc(s["resid_ready"], 1)
                if a is not None:
                    pool.wait_ge(s["key_var"], n(a))
                    nc.gpsimd.tensor_tensor(key_rstd[:], key_var[:], tw.minus_half[:].to_broadcast([P, HEADS]), ALU.pow).then_inc(s["key_rstd"], 1)

            tiles(pool, step)


PATCH = 16
GRID = 5
TILE_TOKENS = IMG_PER_TILE * TOKENS
KPOINTS = PATCH * PATCH
KHALVES = KPOINTS // P
CHANNELS = 3
IMAGE = 84
MARGIN = 3
WINDOW = PATCH + 2 * MARGIN
HALF_COLS = PATCH // KHALVES
WINDOW_X = HALF_COLS + 2 * MARGIN
COVER_Y = -(-IMAGE // WINDOW)
COVER_X = -(-IMAGE // WINDOW_X)
PADDED = MARGIN + max(COVER_Y * WINDOW, COVER_X * WINDOW_X)
SLABS = CHANNELS * KPOINTS // P


def offsets(tw, k, w):
    nc, ins = tw.nc, tw.ins
    names = "patches_used conv_in_psum biased pos rel_y rel_x range turned posT rel_saved".split()
    s = {x: tw.sem("offsets_" + x) for x in names}
    loaded = [tw.sem(f"offsets_patches_loaded_{p}") for p in range(2)]
    saved = [tw.sem(f"offsets_rel_saved_{p}") for p in range(2)]
    B = 2

    def n(t):
        return B + t + 1

    def tiles(eng, step):
        with eng.Fori(0, TILES // 2) as pair:
            step(2 * pair, 0, pair)
            step(2 * pair + 1, 1, pair)

    with tw.scratch(), nc.psum_tensor("ps_conv", [P, 2, 512], F32) as ps_conv, nc.psum_tensor("ps_turn", [P, 2, 512], F32) as ps_turn:
        patches = tw.sb("patches", [P, 2, SLABS, TILE_TOKENS])
        pos = tw.sb("pos", [TILE_TOKENS, 2, 2, KPOINTS])
        rel = tw.sb("rel", [TILE_TOKENS, 2, 2, KPOINTS])
        with nc.Block() as block:

            @block.sync
            def _(sp):
                src = ins["patchesT"].rearrange("(s q) (t n) -> t q s n", q=P, n=TILE_TOKENS)

                def step(t, p, pair):
                    sp.wait_ge(s["conv_in_psum"], n(t) - 2)
                    sp.dma_start(patches[:, p], src[t]).then_inc(loaded[p], 16)

                tiles(sp, step)

            @block.tensor
            def _(pe):
                def step(t, p, pair):
                    pe.wait_ge(loaded[p], 16 * (pair + 1))
                    pe.wait_ge(s["biased"], n(t) - 2)
                    for c in range(SLABS):
                        mm = nc.tensor.matmul(ps_conv[0:TILE_TOKENS, p, :], patches[:, p, c, :], w["offset_w"][:, c, :], start=(c == 0), stop=(c == SLABS - 1))
                    mm.then_inc(s["conv_in_psum"], 1)
                    pe.wait_ge(s["pos"], n(t))
                    pe.wait_ge(s["posT"], n(t) - 2)
                    for h in range(KHALVES):
                        mm = nc.tensor.transpose(ps_turn[:, p, h * TILE_TOKENS:(h + 1) * TILE_TOKENS], pos[:, p, 1, h * P:(h + 1) * P],
                                                 tw.identity[0:TILE_TOKENS, 0:TILE_TOKENS])
                    mm.then_inc(s["turned"], 1)

                tiles(pe, step)

            @block.vector
            def _(dve):
                for x in names:
                    dve.sem_inc(s[x], B)

                def step(t, p, pair):
                    both = lambda x: x.rearrange("n a k -> n (a k)")
                    dve.wait_ge(s["conv_in_psum"], n(t))
                    dve.wait_ge(s["turned"], n(t) - 2)
                    nc.vector.tensor_tensor(both(pos[:, p]), ps_conv[0:TILE_TOKENS, p, :], w["offset_b"][0:TILE_TOKENS, :], ALU.add).then_inc(s["biased"], 1)
                    dve.wait_ge(s["biased"], n(t))
                    nc.vector.tensor_tensor(both(pos[:, p]), both(pos[:, p]), w["base"][:], ALU.add).then_inc(s["pos"], 1)
                    dve.wait_ge(s["pos"], n(t))
                    dve.wait_ge(s["rel_saved"], n(t) - 2)
                    for h in range(KHALVES):
                        half = slice(h * P, (h + 1) * P)
                        x = nc.vector.tensor_scalar(rel[:, p, 1, half], pos[:, p, 1, half], w["origin"][:, 1 + h:2 + h], None, ALU.subtract)
                    x.then_inc(s["rel_x"], 1)
                    nc.vector.tensor_scalar(rel[:, p, 0, :], pos[:, p, 0, :], w["origin"][:, 0:1], None, ALU.subtract).then_inc(s["rel_y"], 1)
                    nc.vector.tensor_copy(k.pos_y[:, t, :], pos[:, p, 0, :])
                    dve.wait_ge(s["rel_y"], n(t))
                    nc.vector.tensor_reduce(k.range[:, 0, t, :], rel[:, p], AX_X, ALU.min)
                    nc.vector.tensor_reduce(k.range[:, 1, t, :], rel[:, p], AX_X, ALU.max).then_inc(s["range"], 1)

                tiles(dve, step)
                dve.wait_ge(s["range"], n(TILES - 1))

            @block.scalar
            def _(act):
                def step(t, p, pair):
                    act.wait_ge(s["turned"], n(t))
                    nc.scalar.copy(k.pos_xT[:, :, t, :], ps_turn[:, p, 0:KHALVES * TILE_TOKENS].rearrange("q (h n) -> q h n", h=KHALVES)).then_inc(s["posT"], 1)

                tiles(act, step)

            @block.gpsimd
            def _(pool):
                def step(t, p, pair):
                    pool.wait_ge(s["rel_y"], n(t))
                    pool.dma_start(k.rel_d[0].rearrange("(t n) c -> t n c", n=TILE_TOKENS)[t], rel[:, p, 0, :]).then_inc(saved[p], 16)
                    pool.wait_ge(s["range"], n(t))
                    pool.wait_ge(saved[p], 16 * (pair + 1))
                    pool.sem_inc(s["rel_saved"], 1)

                tiles(pool, step)


def sample(tw, k, w):
    nc, ins = tw.nc, tw.ins
    names = "hat_y_abs hat_y hat_x_sub hat_x_abs hat_x rows_in_psum multiplied summed added".split()
    NEAR, FAR = "near", "far"
    BUFFERS = 4
    sems = {kind: {x: tw.sem(f"{kind}_{x}") for x in names} for kind in (NEAR, FAR)}
    loads = {kind: {x: [tw.sem(f"{kind}_{x}_loaded_{p}") for p in range(BUFFERS)] for x in ("places", "pixels")} for kind in (NEAR, FAR)}
    moved, saved, cleared = tw.sem("places_moved"), tw.sem("places_saved"), tw.sem("samples_cleared")
    cols = IMG_PER_TILE * CHANNELS * WINDOW_X
    BANKS = (range(0, 3), range(3, GRID))
    B = BUFFERS

    def one_pass(eng, step, first, wy, wx):
        with eng.Fori(0, GRID) as ho:
            with eng.Fori(0, TILES // BUFFERS) as group:
                for p in range(BUFFERS):
                    step(first + ho * TILES + BUFFERS * group + p, ho, BUFFERS * group + p, p, wy, wx)

    def near_or_far(eng, step, before_far=None):
        far = eng.value_load(k.far[0:1, 0:1], min_val=0, max_val=1)
        with eng.If(far == 0):
            one_pass(eng, lambda *a: step(NEAR, *a), 0, 0, 0)
        with eng.Else():
            if before_far:
                before_far()
            with eng.Fori(0, COVER_Y) as wy:
                with eng.Fori(0, COVER_X) as wx:
                    one_pass(eng, lambda *a: step(FAR, *a), (wy * COVER_X + wx) * (GRID * TILES), wy, wx)

    def all_loaded(eng, kind, what, i, p):
        eng.wait_ge(loads[kind][what][p], 16 * IMG_PER_TILE // BUFFERS * (i - p + BUFFERS))

    with tw.scratch(), nc.psum_tensor("ps_rows", [P, 2, KHALVES, 2, 512], F32) as ps:
        hat_y = tw.sb("hat_y", [P, BUFFERS, GRID, KPOINTS])
        strip = tw.sb("strip", [P, BUFFERS, IMG_PER_TILE, CHANNELS, PADDED])
        window = strip[:, :, :, :, 0:WINDOW_X]
        hat_x = tw.sb("hat_x", [P, BUFFERS, KHALVES, GRID * IMG_PER_TILE, WINDOW_X])
        product = tw.sb("product", [P, 2, KHALVES, GRID * cols])
        part = tw.sb("part", [P, KHALVES * IMG_PER_TILE * GRID * CHANNELS])
        moved_places = product[0:TILE_TOKENS].rearrange("q b h n -> q (b h n)")[:, 0:TILES * KPOINTS].rearrange("q (t n) -> q t n", t=TILES)
        with nc.Block() as block:

            @block.gpsimd
            def _(pool):
                nc.gpsimd.memset(hat_y[:], 0.0)
                nc.gpsimd.memset(strip[:], 0.0)

        with nc.Block() as block:

            @block.sync
            def _(sp):
                def step(kind, i, ho, t, p, wy, wx):
                    n = B + i + 1
                    sp.wait_ge(sems[kind]["rows_in_psum"], n - BUFFERS)
                    for j in range(IMG_PER_TILE):
                        q = slice(QUAD * j, QUAD * j + WINDOW)
                        version = 0 if kind == NEAR else wy + 1
                        places = k.rel_d[version].rearrange("(t j h w) c -> t h j (w c)", t=TILES, j=IMG_PER_TILE, h=GRID)[t][ho][j:j + 1, :]
                        sp.dma_start(hat_y[q, p].rearrange("q w c -> q (w c)"), places.to_broadcast([WINDOW, GRID * KPOINTS])).then_inc(loads[kind]["places"][p], 16)
                        if kind == NEAR:
                            sp.dma_start(strip[q, p, j], ins["strips"][ho][t][j]).then_inc(loads[kind]["pixels"][p], 16)
                        else:
                            sp.dma_start(window[q, p, j], ins["windows"][wy][wx][t][j]).then_inc(loads[kind]["pixels"][p], 16)

                def store_places():
                    for wy in range(COVER_Y):
                        sp.wait_ge(moved, wy + 1)
                        sp.dma_start(k.rel_d[1 + wy].rearrange("(t n) c -> n t c", n=TILE_TOKENS), moved_places).then_inc(saved, 16)
                    sp.wait_ge(saved, 16 * COVER_Y)

                near_or_far(sp, step, store_places)

            @block.scalar
            def _(act):
                def step(kind, i, ho, t, p, wy, wx):
                    n, s = B + i + 1, sems[kind]
                    all_loaded(act, kind, "places", i, p)
                    y = hat_y[:, p].rearrange("q w c -> q (w c)")
                    nc.scalar.activation(y, y, ACT.Abs, bias=w["minus_row"][:]).then_inc(s["hat_y_abs"], 1)
                    act.wait_ge(s["hat_x_sub"], n)
                    x = hat_x[:, p].rearrange("q h w x -> q (h w x)")
                    nc.scalar.activation(x, x, ACT.Abs).then_inc(s["hat_x_abs"], 1)
                    act.wait_ge(s["hat_y_abs"], n)
                    nc.scalar.activation(y, y, ACT.Relu, scale=-1.0, bias=1.0).then_inc(s["hat_y"], 1)
                    act.wait_ge(s["hat_x_abs"], n)
                    nc.scalar.activation(x, x, ACT.Relu, scale=-1.0, bias=1.0).then_inc(s["hat_x"], 1)

                near_or_far(act, step)

            @block.gpsimd
            def _(pool):
                def step(kind, i, ho, t, p, wy, wx):
                    n, s = B + i + 1, sems[kind]
                    pool.wait_ge(s["multiplied"], n - BUFFERS)
                    for h in range(KHALVES):
                        shape = [P, GRID, IMG_PER_TILE, WINDOW_X]
                        places = k.pos_xT[:, h, t, :].rearrange("q (j g) -> q g j", j=IMG_PER_TILE)[:, bass.ds(ho * GRID, GRID), :]
                        grid = w["window_x"][:, h].unsqueeze(2) if kind == NEAR else w["cover_x"][:, wx, :].unsqueeze(1).unsqueeze(1)
                        x = nc.gpsimd.tensor_tensor(hat_x[:, p, h].rearrange("q (g j) x -> q g j x", j=IMG_PER_TILE), places.unsqueeze(3).to_broadcast(shape),
                                                    grid.to_broadcast(shape), ALU.subtract)
                    x.then_inc(s["hat_x_sub"], 1)

                near_or_far(pool, step)

            @block.tensor
            def _(pe):
                def step(kind, i, ho, t, p, wy, wx):
                    n, s = B + i + 1, sems[kind]
                    pe.wait_ge(s["hat_y"], n)
                    all_loaded(pe, kind, "pixels", i, p)
                    pe.wait_ge(s["multiplied"], n - 2)
                    for h in range(KHALVES):
                        for bank, patches in enumerate(BANKS):
                            for at, g in enumerate(patches):
                                left = PATCH * g + HALF_COLS * h
                                rhs = strip[:, p, :, :, left:left + WINDOW_X] if kind == NEAR else window[:, p]
                                mm = nc.tensor.matmul(ps[:, p % 2, h, bank, at * cols:(at + 1) * cols], hat_y[:, p, g, h * P:(h + 1) * P], rhs.rearrange("q j c x -> q (j c) x"), start=True, stop=True)
                    mm.then_inc(s["rows_in_psum"], 1)

                near_or_far(pe, step)

            @block.vector
            def _(dve):
                for s in sems.values():
                    for x in names:
                        dve.sem_inc(s[x], B)

                def move_places():
                    nc.vector.memset(k.samples[:], 0.0).then_inc(cleared, 1)
                    dve.wait_ge(cleared, 1)
                    for wy in range(COVER_Y):
                        if wy:
                            dve.wait_ge(saved, 16 * wy)
                        nc.vector.tensor_scalar(moved_places, k.pos_y[:], float(WINDOW * wy), None, ALU.subtract).then_inc(moved, 1)
                    dve.wait_ge(saved, 16 * COVER_Y)

                def step(kind, i, ho, t, p, wy, wx):
                    n, s = B + i + 1, sems[kind]
                    dve.wait_ge(s["hat_x"], n)
                    dve.wait_ge(s["rows_in_psum"], n)
                    dve.wait_ge(s["summed"], n - 2)
                    for h in range(KHALVES):
                        for bank, patches in enumerate(BANKS):
                            split = lambda x: x.rearrange("q (w c x) -> q w c x", c=CHANNELS, x=WINDOW_X)
                            windows = len(patches) * IMG_PER_TILE
                            weights = hat_x[:, p, h, patches[0] * IMG_PER_TILE:patches[0] * IMG_PER_TILE + windows].unsqueeze(2)
                            last = nc.vector.tensor_tensor(split(product[:, p % 2, h, patches[0] * cols:(patches[-1] + 1) * cols]),
                                                           split(ps[:, p % 2, h, bank, 0:len(patches) * cols]),
                                                           weights.to_broadcast([P, windows, CHANNELS, WINDOW_X]), ALU.mult)
                    last.then_inc(s["multiplied"], 1)
                    dve.wait_ge(s["multiplied"], n)
                    into = k.samples[:, ho * TILES + t, :]
                    by_window = product[:, p % 2].rearrange("q h (a x) -> q (h a) x", x=WINDOW_X)
                    if kind == NEAR:
                        nc.vector.tensor_reduce(into, by_window, AX_X, ALU.add).then_inc(s["summed"], 1)
                    else:
                        nc.vector.tensor_reduce(part[:], by_window, AX_X, ALU.add).then_inc(s["summed"], 1)
                        dve.wait_ge(s["summed"], n)
                        nc.vector.tensor_tensor(into, into, part[:], ALU.add).then_inc(s["added"], 1)

                near_or_far(dve, step, move_places)


def any_far(tw, k):
    nc = tw.nc
    reduced, compared, joined, turned, done = (tw.sem("far_" + x) for x in ("reduced", "compared", "joined", "turned", "done"))
    extreme = tw.sb("far_extreme", [TILE_TOKENS, 2, 2])
    outside = tw.sb("far_outside", [TILE_TOKENS, 2, 2])
    any_row = tw.sb("far_any_row", [TILE_TOKENS, 1])
    with nc.psum_tensor("ps_far", [1, 512], F32) as ps, nc.Block() as block:

        @block.vector
        def _(dve):
            nc.vector.tensor_reduce(extreme[:, 0], k.range[:, 0].rearrange("n t a -> n a t"), AX_X, ALU.min).then_inc(reduced, 1)
            nc.vector.tensor_reduce(extreme[:, 1], k.range[:, 1].rearrange("n t a -> n a t"), AX_X, ALU.max).then_inc(reduced, 1)
            dve.wait_ge(reduced, 2)
            nc.vector.tensor_scalar(outside[:, 0], extreme[:, 0], 0.0, None, ALU.is_lt).then_inc(compared, 1)
            nc.vector.tensor_scalar(outside[:, 1, 0:1], extreme[:, 1, 0:1], float(WINDOW - 1), None, ALU.is_gt).then_inc(compared, 1)
            nc.vector.tensor_scalar(outside[:, 1, 1:2], extreme[:, 1, 1:2], float(WINDOW_X - 1), None, ALU.is_gt).then_inc(compared, 1)
            dve.wait_ge(compared, 3)
            nc.vector.tensor_reduce(any_row[:], outside[:].rearrange("n a b -> n (a b)"), AX_X, ALU.max).then_inc(joined, 1)
            dve.wait_ge(turned, 1)
            nc.vector.tensor_reduce(k.far[:], ps[:, 0:TILE_TOKENS], AX_X, ALU.max).then_inc(done, 1)
            dve.wait_ge(done, 1)

        @block.tensor
        def _(pe):
            pe.wait_ge(joined, 1)
            nc.tensor.transpose(ps[:, 0:TILE_TOKENS], any_row[:], tw.identity[0:TILE_TOKENS, 0:TILE_TOKENS]).then_inc(turned, 1)


def project_and_norm(tw, k, w):
    nc = tw.nc
    names = "cleared product_in_psum stats aggregated rooted inverted normed activated turned y_ready".split()
    s = {x: tw.sem("tok_" + x) for x in names}
    half_cols = IMAGES * TOKENS // 2
    chunks = GRID * TILES // 2
    with tw.scratch(), ExitStack() as ctx:
        ps = ctx.enter_context(nc.psum_tensor("ps_tok", [HALF, HALVES, 2, 512], F32))
        ps_y = ctx.enter_context(nc.psum_tensor("ps_tok_y", [P, 2, 512], F32))
        stats = tw.sb("tok_stats", [HALF, HALVES, 2, 6])
        moments = tw.sb("tok_moments", [HALF, HALVES, 2])
        rstd = tw.sb("tok_rstd", [HALF, HALVES, 1])
        normed = tw.sb("tok_normed", [HALF, HALVES, IMAGES * TOKENS])
        yT = tw.sb("tok_yT", [HALF, HALVES, IMAGES, QUAD])
        with nc.Block() as block:

            @block.gpsimd
            def _(pool):
                nc.gpsimd.memset(yT[:], 0.0).then_inc(s["cleared"], 1)
                nc.gpsimd.memset(tw.mean[:], 0.0)
                nc.gpsimd.memset(tw.rstd[:], 1.0)

            @block.tensor
            def _(pe):
                for o in range(HALVES):
                    for half in range(2):
                        i = 0
                        for c in range(CHANNELS):
                            for h in range(KHALVES):
                                rhs = k.samples[:, half * chunks:(half + 1) * chunks, :].rearrange("q a (h g j c) -> q a j h g c", h=KHALVES, g=GRID, c=CHANNELS)[:, :, :, h, :, c]
                                mm = nc.tensor.matmul(ps[:, o, half, 0:half_cols], w["dconv"][:, c, h, o * HALF:(o + 1) * HALF], rhs,
                                                      start=(i == 0), stop=(i == CHANNELS * KHALVES - 1))
                                i += 1
                        mm.then_inc(s["product_in_psum"], 1)
                for t in range(TILES):
                    pe.wait_ge(s["activated"], HALVES)
                    if t >= 2:
                        pe.wait_ge(s["y_ready"], t - 1)
                    for o in range(HALVES):
                        mm = nc.tensor.transpose(ps_y[:, t % 2, o * HALF:(o + 1) * HALF], yT[:, o, 4 * t:4 * t + 4, :], tw.identity[0:HALF, 0:HALF])
                    mm.then_inc(s["turned"], 1)

            @block.vector
            def _(dve):
                for o in range(HALVES):
                    for half in range(2):
                        dve.wait_ge(s["product_in_psum"], 2 * o + half + 1)
                        nc.vector.bn_stats(stats[:, o, half, :], ps[:, o, half, 0:half_cols]).then_inc(s["stats"], 1)
                dve.wait_ge(s["stats"], 4)
                for o in range(HALVES):
                    nc.vector.bn_aggr(moments[:, o, :], stats[:, o].rearrange("q a b -> q (a b)")).then_inc(s["aggregated"], 1)
                dve.wait_ge(s["rooted"], 1)
                nc.vector.reciprocal(rstd[:], rstd[:]).then_inc(s["inverted"], 1)
                dve.wait_ge(s["inverted"], 1)
                for o in range(HALVES):
                    nc.vector.tensor_scalar(normed[:, o, :].rearrange("q (a b) -> q a b", a=2), ps[:, o, :, 0:half_cols], moments[:, o, 0:1], rstd[:, o, :],
                                            ALU.subtract, ALU.mult).then_inc(s["normed"], 1)
                for t in range(TILES):
                    dve.wait_ge(s["turned"], t + 1)
                    nc.vector.tensor_copy(tw.y[:, t, :], ps_y[:, t % 2, 0:DIM]).then_inc(s["y_ready"], 1)

            @block.scalar
            def _(act):
                act.wait_ge(s["aggregated"], HALVES)
                nc.scalar.activation(rstd[:], moments[:, :, 1:2], ACT.Sqrt, bias=tw.eps[0:HALF, :]).then_inc(s["rooted"], 1)
                act.wait_ge(s["cleared"], 1)
                for o in range(HALVES):
                    act.wait_ge(s["normed"], o + 1)
                    nc.scalar.activation(yT[:, o, :, 0:TOKENS].rearrange("q i (h w) -> q h i w", h=GRID),
                                         normed[:, o, :].rearrange("q (h i w) -> q h i w", h=GRID, w=GRID), ACT.Gelu,
                                         scale=w["gamma"][:, o:o + 1], bias=w["beta"][:, o:o + 1]).then_inc(s["activated"], 1)


class Tokenizer:

    def __init__(self, tw):
        self.pos_y = tw.sb("pos_y", [TILE_TOKENS, TILES, KPOINTS])
        self.pos_xT = tw.sb("pos_xT", [P, KHALVES, TILES, TILE_TOKENS])
        self.far = tw.scope.enter_context(tw.nc.sbuf_tensor("far", [1, 1], mybir.dt.int32))
        self.range = tw.sb("range", [TILE_TOKENS, 2, TILES, 2])
        self.samples = tw.sb("samples", [P, GRID * TILES, IMG_PER_TILE * KHALVES * GRID * CHANNELS])
        self.rel_d = tw.nc.dram_tensor("places_y", (1 + COVER_Y, IMAGES * TOKENS, KPOINTS), F32, kind="Internal").ap()


def tokenizer(tw, w):
    k = Tokenizer(tw)
    offsets(tw, k, w)
    any_far(tw, k)
    sample(tw, k, w)
    project_and_norm(tw, k, w)


def front(tw, m, name, wg, experts):
    nc = tw.nc
    base = m.front_base
    s = m.front_sem

    def n(t):
        return base + t + 1

    def tiles(eng, step):
        with eng.Fori(0, TILES - 1, 2) as i:
            step(i, 0)
            step(i + 1, 1)

    with nc.psum_tensor(name + "ps_hT", [HALF, 2, 512], F32) as ps_hT, \
            nc.psum_tensor(name + "ps_gate", [P, 2, 512], F32) as ps_gate, nc.Block() as block:

        @block.vector
        def _(dve):
            def step(t, p):
                dve.wait_ge(s["hT_in_psum"], n(t) - 2)
                dve.wait_ge(s["kept"], n(t) - 2)
                nc.vector.tensor_scalar(m.row[:, p, :], tw.y[:, t, :], tw.mean[:, t, :], tw.rstd[:, t, :],
                                        ALU.subtract, ALU.mult).then_inc(s["normed"], 1)
                dve.wait_ge(s["gated"], n(t))
                nc.vector.tensor_copy(m.logits[:, t, 0:experts], ps_gate[:, p, 0:experts]).then_inc(s["logits_ready"], 1)

            tiles(dve, step)

        @block.tensor
        def _(pe):
            def step(t, p):
                pe.wait_ge(s["normed"], n(t))
                pe.wait_ge(s["hT_ready"], n(t) - 2)
                for k in range(HALVES):
                    mm = nc.tensor.transpose(ps_hT[:, p, k * P:(k + 1) * P], m.row[:, p, k * HALF:(k + 1) * HALF], tw.identity[:])
                mm.then_inc(s["hT_in_psum"], 1)
                pe.wait_ge(s["hT_ready"], n(t))
                pe.wait_ge(s["logits_ready"], n(t) - 2)
                for k in range(HALVES):
                    mm = nc.tensor.matmul(ps_gate[:, p, 0:experts], m.rowT[:, p, k, :], wg[:, k, 0:experts],
                                          start=(k == 0), stop=(k == 1))
                mm.then_inc(s["gated"], 1)

            tiles(pe, step)

        @block.scalar
        def _(act):
            def step(t, p):
                act.wait_ge(s["hT_in_psum"], n(t))
                act.wait_ge(s["gated"], n(t) - 2)
                act.wait_ge(s["keptT"], n(t) - 2)
                nc.scalar.copy(m.rowT[:, p, :, :], ps_hT[:, p, 0:HALVES * P].rearrange("q (k n) -> q k n", n=P)).then_inc(s["hT_ready"], 1)

            tiles(act, step)

        @block.gpsimd
        def _(pool):
            def step(t, p):
                pool.wait_ge(s["normed"], n(t))
                nc.gpsimd.tensor_copy(m.h[:, t, :], m.row[:, p, :]).then_inc(s["kept"], 1)
                pool.wait_ge(s["hT_ready"], n(t))
                nc.gpsimd.tensor_copy(m.hT[:, :, t, :], m.rowT[:, p, :, :]).then_inc(s["keptT"], 1)

            tiles(pool, step)


class MoeBuffers:

    def __init__(self, tw):
        nc, sb = tw.nc, tw.sb
        self.row = sb("row", [P, 2, DIM])
        self.rowT = sb("rowT", [HALF, 2, HALVES, P])
        self.h = sb("h_all", [P, TILES, DIM])
        self.hT = sb("hT_all", [HALF, HALVES, TILES, P])
        self.logits = sb("logits", [P, TILES, 16])
        self.combine = sb("combine", [P, TILES, 8])
        self.score = sb("score", [P, TILES, 8])
        self.rest = sb("rest", [P, TILES, 8])
        self.cand = sb("cand", [P, TILES, 8])
        self.best = sb("best", [P, 2, TILES, 1])
        self.first = sb("first", [P, TILES, 1])
        self.total = sb("total", [P, TILES, 1])
        self.chosen = sb("chosen", [P, TILES, 2, 2, 8])
        self.countdown = sb("countdown", [P, 8])
        self.slot_rows = sb("slot_rows", [16, IMAGES, QUAD])
        self.weight_rows = sb("weight_rows", [32, IMAGES, QUAD])
        self.slot = sb("slot", [P, TILES, 16])
        self.slot_iota = sb("slot_iota", [P, 120])
        self.row_iota = sb("row_iota", [P, 1])
        dram = lambda nm: tw.keep(nm, lambda: nc.dram_tensor(nm, (2, 16, TILES * P), F32, kind="Internal").ap())
        self.slot_scratch, self.weight_scratch = dram("slot_scratch"), dram("weight_scratch")
        names = "normed hT_in_psum hT_ready gated logits_ready kept keptT".split()
        self.front_sem = {k: tw.sem("front_" + k) for k in names}
        self.step, self.steps = tw.sem("routing_step"), 0
        self.front_base = 2
        self.const = tw.sem("moe_constants")
        with nc.Block() as block:

            @block.gpsimd
            def _(pool):
                for e in range(8):
                    nc.gpsimd.memset(self.countdown[:, e:e + 1], float(8 - e))
                nc.gpsimd.iota(self.slot_iota[:], [[1, 120]], base=0, channel_multiplier=0, allow_small_or_imprecise_dtypes=True)
                nc.gpsimd.iota(self.row_iota[:], [[0, 1]], base=0, channel_multiplier=1, allow_small_or_imprecise_dtypes=True)
                nc.gpsimd.memset(self.slot_rows[:], -1.0)
                nc.gpsimd.memset(self.weight_rows[:], 0.0).then_inc(self.const, 1)

            @block.vector
            def _(dve):
                for x in self.front_sem.values():
                    dve.sem_inc(x, 2)
                dve.wait_ge(self.const, 1)


class RowScratch:

    def __init__(self, tw, m):
        nc, sb = tw.nc, tw.sb
        n = IMAGES * TOKENS
        m.rows = sb("rows", [32, IMAGES, TOKENS])
        m.work = sb("rows_work", [16, 2, n])
        m.top = sb("rows_top", [16, 16, 8])
        m.gt, m.eq, m.cum, m.ones = (sb("rows_" + k, [16, n]) for k in ("gt", "eq", "cum", "ones"))
        m.count = sb("rows_count", [16, 2])
        with nc.Block() as block:

            @block.gpsimd
            def _(pool):
                nc.gpsimd.memset(m.ones[:], 1.0)


class Chain:

    def __init__(self, eng, m):
        self.eng, self.m = eng, m

    def __call__(self, ins):
        ins.then_inc(self.m.step, 1)
        self.m.steps += 1
        self.eng.wait_ge(self.m.step, self.m.steps)


def pick_two(nc, m, after, scores):
    shape = [P, TILES, 8]
    for k in range(2):
        x = scores if k == 0 else m.rest
        after(nc.vector.tensor_reduce(m.best[:, k], x[:, :, 0:8], AX_X, ALU.max))
        after(nc.vector.tensor_tensor(m.cand[:], x[:, :, 0:8], m.best[:, k].to_broadcast(shape), ALU.is_equal))
        after(nc.vector.tensor_tensor(m.cand[:], m.cand[:], m.countdown[:].unsqueeze(1).to_broadcast(shape), ALU.mult))
        after(nc.vector.tensor_reduce(m.first[:], m.cand[:], AX_X, ALU.max))
        after(nc.vector.tensor_tensor(m.chosen[:, :, 0, k, :], m.cand[:], m.first[:].to_broadcast(shape), ALU.is_equal))
        if k == 0:
            after(nc.vector.scalar_tensor_tensor(out=m.rest[:], in0=m.chosen[:, :, 0, 0, :], scalar=-1e30,
                                                 in1=x[:, :, 0:8], op0=ALU.mult, op1=ALU.add))


def lora_gate(tw, m, name, bg):
    nc = tw.nc
    shape = [P, TILES, 8]
    shifted, exped = tw.sem(name + "_gate_shifted"), tw.sem(name + "_gate_exped")
    with nc.Block() as block:

        @block.vector
        def _(dve):
            after = Chain(dve, m)
            after(nc.vector.tensor_tensor(m.logits[:, :, 0:8], m.logits[:, :, 0:8], bg[:].unsqueeze(1).to_broadcast(shape), ALU.add))
            after(nc.vector.tensor_reduce(m.first[:], m.logits[:, :, 0:8], AX_X, ALU.max))
            nc.vector.tensor_tensor(m.score[:], m.logits[:, :, 0:8], m.first[:].to_broadcast(shape), ALU.subtract).then_inc(shifted, 1)
            dve.wait_ge(exped, 1)
            after(nc.vector.tensor_reduce(m.total[:], m.score[:], AX_X, ALU.add))
            after(nc.vector.reciprocal(m.total[:], m.total[:]))
            after(nc.vector.tensor_tensor(m.score[:], m.score[:], m.total[:].to_broadcast(shape), ALU.mult))
            pick_two(nc, m, after, m.score)
            after(nc.vector.tensor_tensor(m.cand[:], m.chosen[:, :, 0, 0, :], m.chosen[:, :, 0, 1, :], ALU.add))
            after(nc.vector.scalar_tensor_tensor(out=m.combine[:], in0=m.cand[:], scalar=2.0, in1=m.score[:],
                                                 op0=ALU.mult, op1=ALU.mult))

        @block.scalar
        def _(act):
            act.wait_ge(shifted, 1)
            nc.scalar.activation(m.score[:], m.score[:], ACT.Exp).then_inc(exped, 1)


def token_choice_rows(tw, m, name, ps):
    nc = tw.nc
    shifted, exped = tw.sem(name + "_pair_shifted"), tw.sem(name + "_pair_exped")
    turned, picked = tw.sem(name + "_turned"), tw.sem(name + "_picked")
    shape = [P, TILES, 8]
    with nc.Block() as block:

        @block.vector
        def _(dve):
            after = Chain(dve, m)
            pick_two(nc, m, after, m.logits)
            nc.vector.tensor_tensor(m.first[:], m.best[:, 1], m.best[:, 0], ALU.subtract).then_inc(shifted, 1)
            dve.wait_ge(exped, 1)
            after(nc.vector.tensor_scalar(m.total[:], m.first[:], 1.0, None, ALU.add))
            after(nc.vector.reciprocal(m.total[:], m.total[:]))
            after(nc.vector.tensor_tensor(m.first[:], m.first[:], m.total[:], ALU.mult))
            after(nc.vector.tensor_tensor(m.chosen[:, :, 1, 0, :], m.chosen[:, :, 0, 0, :], m.total[:].to_broadcast(shape), ALU.mult))
            nc.vector.tensor_tensor(m.chosen[:, :, 1, 1, :], m.chosen[:, :, 0, 1, :], m.first[:].to_broadcast(shape), ALU.mult).then_inc(picked, 1)
            dve.wait_ge(turned, 1)
            rows_in = ps[0:32, :, 0:4 * P].rearrange("r b (i n) -> r b i n", n=QUAD)
            for c in range(2):
                half = slice(IMAGES // 2 * c, IMAGES // 2 * (c + 1))
                after(nc.vector.tensor_copy(m.rows[:, half, :], rows_in[:, c, :, 0:TOKENS]))
                after(nc.vector.tensor_copy(m.weight_rows[:, half, :], rows_in[:, c, :, :]))
            sel = m.rows[0:16].rearrange("r i n -> r (i n)")
            after(nc.vector.tensor_tensor_scan(m.cum[:], m.ones[:], sel, 0.0, ALU.mult, ALU.add))
            after(nc.vector.tensor_tensor(m.cum[:], m.cum[:], sel, ALU.mult))
            after(nc.vector.tensor_scalar(m.slot_rows[:, :, 0:TOKENS], m.cum[:].rearrange("r (i n) -> r i n", n=TOKENS), 1.0, None, ALU.subtract))

        @block.scalar
        def _(act):
            act.wait_ge(shifted, 1)
            nc.scalar.activation(m.first[:], m.first[:], ACT.Exp).then_inc(exped, 1)

        @block.tensor
        def _(pe):
            pe.wait_ge(picked, 1)
            for t in range(TILES):
                mm = nc.tensor.transpose(ps[0:32, t // 4, (t % 4) * P:(t % 4 + 1) * P], m.chosen[:, t, :, :, :], tw.identity[:])
            mm.then_inc(turned, 1)


def expert_choice_rows(tw, m, name, ps, capacity):
    nc = tw.nc
    sigmoided, turned = tw.sem(name + "_sigmoided"), tw.sem(name + "_turned")
    with nc.Block() as block:

        @block.scalar
        def _(act):
            nc.scalar.activation(m.logits[:], m.logits[:], ACT.Sigmoid).then_inc(sigmoided, 1)

        @block.tensor
        def _(pe):
            pe.wait_ge(sigmoided, 1)
            for t in range(TILES):
                mm = nc.tensor.transpose(ps[0:16, t // 4, (t % 4) * P:(t % 4 + 1) * P], m.logits[:, t, :], tw.identity[:])
            mm.then_inc(turned, 1)

        @block.vector
        def _(dve):
            after = Chain(dve, m)
            dve.wait_ge(turned, 1)
            rows_in = ps[0:16, :, 0:4 * P].rearrange("r b (i n) -> r b i n", n=QUAD)
            for c in range(2):
                half = slice(IMAGES // 2 * c, IMAGES // 2 * (c + 1))
                after(nc.vector.tensor_copy(m.rows[0:16, half, :], rows_in[:, c, :, 0:TOKENS]))
                after(nc.vector.tensor_copy(m.weight_rows[0:16, half, :], rows_in[:, c, :, :]))
            score = m.rows[0:16].rearrange("r i n -> r (i n)")
            rounds = -(-capacity // 8)
            x = score
            for r in range(rounds):
                after(nc.vector.max(m.top[:, r, :], x))
                if r < rounds - 1:
                    after(nc.vector.match_replace(m.work[:, r % 2, :], m.top[:, r, :], x, -1.0))
                    x = m.work[:, r % 2, :]
            least = m.top[:, rounds - 1, (capacity - 1) % 8:(capacity - 1) % 8 + 1]
            after(nc.vector.tensor_scalar(m.gt[:], score, least, None, ALU.is_gt))
            after(nc.vector.tensor_reduce(m.count[:, 0:1], m.gt[:], AX_X, ALU.add))
            after(nc.vector.tensor_scalar(m.count[:, 1:2], m.count[:, 0:1], -1.0, float(capacity), ALU.mult, ALU.add))
            after(nc.vector.tensor_scalar(m.eq[:], score, least, None, ALU.is_equal))
            after(nc.vector.tensor_tensor_scan(m.cum[:], m.ones[:], m.eq[:], 0.0, ALU.mult, ALU.add))
            after(nc.vector.scalar_tensor_tensor(out=m.eq[:], in0=m.cum[:], scalar=m.count[:, 1:2], in1=m.eq[:],
                                                 op0=ALU.is_le, op1=ALU.mult))
            after(nc.vector.tensor_tensor(m.gt[:], m.gt[:], m.eq[:], ALU.add))
            after(nc.vector.tensor_tensor_scan(m.cum[:], m.ones[:], m.gt[:], 0.0, ALU.mult, ALU.add))
            after(nc.vector.tensor_tensor(m.cum[:], m.cum[:], m.gt[:], ALU.mult))
            after(nc.vector.tensor_scalar(m.slot_rows[:, :, 0:TOKENS], m.cum[:].rearrange("r (i n) -> r i n", n=TOKENS), 1.0, None, ALU.subtract))


def experts(tw, m, name, which, lists, capacity, hidden, w_in, w_out, weight_row, onto):
    nc = tw.nc
    n_exp = w_in.shape[0]
    ft = hidden // P
    fb = ft // 2
    C = capacity
    names = ("slots_in_psum slots_ready saved onehot gathered xT_ready up_in_psum silu gated "
             "down_in_psum down_ready returned back closed added").split()
    s = {k: tw.sem(name + "_" + k) for k in names}
    loaded = {k: [tw.sem(f"{name}_{k}_loaded_{p}") for p in range(2)] for k in ("win", "wout", "rows")}
    with ExitStack() as ctx:
        def sb(nm, shape):
            return ctx.enter_context(nc.sbuf_tensor(name + nm, shape, F32))

        def pb(nm, shape):
            return ctx.enter_context(nc.psum_tensor(name + nm, shape, F32))

        win = sb("win", [HALF, 2, HALVES, 2 * hidden])
        wout = sb("wout", [P, 2, ft, DIM])
        slot_b = sb("slot_b", [C, 2, lists, TILES * P])
        weight_b = sb("weight_b", [C, 2, lists, TILES * P])
        gather = sb("gather", [P, 2, TILES, lists * C])
        xT = sb("xT", [HALF, 2, HALVES, lists * C])
        act_gate = sb("act_gate", [P, 2, fb, lists * C])
        hid = sb("hid", [P, ft, lists * C])
        down = sb("down", [C, 2, lists, DIM])
        zeros = sb("zeros", [P, P])

        acc = pb("acc", [P, 4, 512])
        ps_x = pb("ps_x", [HALF, HALVES, lists * C])
        bank_g, bank_u = pb("bank_g", [P, 512]), pb("bank_u", [P, 512])
        ps_g = bank_g[:, 0:fb * lists * C].rearrange("p (f c) -> p f c", f=fb)
        ps_u = bank_u[:, 0:fb * lists * C].rearrange("p (f c) -> p f c", f=fb)
        ps_slots = bank_g[:, 0:TILES * 16].rearrange("p (t r) -> p t r", r=16)
        ps_d = pb("ps_d", [C, lists, DIM])
        block = ctx.enter_context(nc.Block())
        B = 4

        def n(e):
            return B + e + 1

        def experts_loop(eng, step):
            with eng.Fori(0, n_exp // 2) as pair:
                step(2 * pair, 0, pair)
                step(2 * pair + 1, 1, pair)

        @block.sync
        def _(sp):
            sp.dma_start(m.slot_scratch[which], m.slot_rows[:].rearrange("r i n -> r (i n)")).then_inc(s["saved"], 16)
            sp.dma_start(m.weight_scratch[which], m.weight_rows[weight_row:weight_row + 16].rearrange("r i n -> r (i n)")).then_inc(s["saved"], 16)
            sp.wait_ge(s["saved"], 32)

            def step(e, p, pair):
                sp.wait_ge(s["up_in_psum"], B + 2 * e - 2)
                sp.dma_start(win[:, p], w_in[e].rearrange("(k q) n -> q k n", q=HALF)).then_inc(loaded["win"][p], 16)
                sp.wait_ge(s["down_in_psum"], n(e) - 2)
                sp.dma_start(wout[:, p], w_out[e].rearrange("(f q) n -> q f n", q=P)).then_inc(loaded["wout"][p], 16)
                sp.wait_ge(s["returned"], n(e) - 2)
                for g in range(lists):
                    for scratch, dst in ((m.slot_scratch, slot_b), (m.weight_scratch, weight_b)):
                        row = scratch[which].rearrange("(g e) n -> e g n", g=lists)[e][g:g + 1, :]
                        sp.dma_start(dst[:, p, g, :], row.to_broadcast([C, TILES * P])).then_inc(loaded["rows"][p], 16)

            experts_loop(sp, step)

        @block.gpsimd
        def _(pool):
            nc.gpsimd.memset(zeros[:], 0.0).then_inc(s["slots_ready"], 1)

        @block.vector
        def _(dve):
            for x in ("gated", "down_in_psum", "back", "onehot", "gathered", "xT_ready", "returned", "down_ready", "silu", "up_in_psum"):
                dve.sem_inc(s[x], B)
            dve.wait_ge(s["slots_in_psum"], 1)
            nc.vector.tensor_copy(m.slot[:], ps_slots).then_inc(s["slots_ready"], 1)
            dve.wait_ge(s["slots_ready"], 2)

            def step(e, p, pair):
                dve.wait_ge(s["gathered"], n(e) - 2)
                for t in range(TILES):
                    for g in range(lists):
                        col = e + g * n_exp
                        ins = nc.vector.tensor_scalar(gather[:, p, t, g * C:(g + 1) * C], m.slot_iota[:, 0:C],
                                                      m.slot[:, t, bass.ds(col, 1)], None, ALU.is_equal)
                ins.then_inc(s["onehot"], 1)
                dve.wait_ge(loaded["rows"][p], 32 * lists * (pair + 1))
                for g in range(lists):
                    ins = nc.vector.scalar_tensor_tensor(out=weight_b[:, p, g, :], in0=slot_b[:, p, g, :], scalar=m.row_iota[0:C, :],
                                                         in1=weight_b[:, p, g, :], op0=ALU.is_equal, op1=ALU.mult)
                ins.then_inc(s["back"], 1)
                for c in range(2):
                    dve.wait_ge(s["silu"], B + 2 * e + c + 1)
                    if c == 0:
                        dve.wait_ge(s["down_in_psum"], n(e) - 1)
                    nc.vector.tensor_tensor(hid[:, c * fb:(c + 1) * fb, :], act_gate[:, c, :, :], ps_u, ALU.mult).then_inc(s["gated"], 1)

            experts_loop(dve, step)
            dve.wait_ge(s["closed"], 1)
            for t in range(TILES):
                nc.vector.tensor_tensor(tw.y[:, t, :], acc[:, t // 2, (t % 2) * DIM:(t % 2 + 1) * DIM], onto[:, t, :], ALU.add).then_inc(s["added"], 1)
                dve.wait_ge(s["added"], t + 1)
                nc.vector.bn_stats(tw.moments[:, t, :], tw.y[:, t, :])

        @block.scalar
        def _(act):
            def step(e, p, pair):
                act.wait_ge(s["gathered"], n(e))
                act.wait_ge(s["up_in_psum"], B + 2 * e - 2)
                nc.scalar.copy(xT[:, p], ps_x[:]).then_inc(s["xT_ready"], 1)
                for c in range(2):
                    act.wait_ge(s["up_in_psum"], B + 2 * e + c + 1)
                    act.wait_ge(s["gated"], B + 2 * e + c - 1)
                    nc.scalar.activation(act_gate[:, c, :, :], ps_g, ACT.Silu).then_inc(s["silu"], 1)
                act.wait_ge(s["down_in_psum"], n(e))
                act.wait_ge(s["returned"], n(e) - 2)
                nc.scalar.copy(down[:, p], ps_d[:]).then_inc(s["down_ready"], 1)

            experts_loop(act, step)

        @block.tensor
        def _(pe):
            for t in range(TILES):
                mm = nc.tensor.transpose(ps_slots[:, t, :], m.slot_rows[:, 4 * t:4 * t + 4, :], tw.identity[0:16, 0:16])
            mm.then_inc(s["slots_in_psum"], 1)
            pe.wait_ge(s["slots_ready"], 2)
            for c in range(4):
                nc.tensor.matmul(acc[:, c, 0:2 * DIM], zeros[:], m.h[:, 2 * c:2 * c + 2, :].rearrange("p t n -> p (t n)"), start=True, stop=False)

            def step(e, p, pair):
                pe.wait_ge(s["onehot"], n(e))
                pe.wait_ge(s["xT_ready"], n(e) - 1)
                for k in range(HALVES):
                    for t in range(TILES):
                        mm = nc.tensor.matmul(ps_x[:, k, :], m.h[:, t, k * HALF:(k + 1) * HALF], gather[:, p, t, :],
                                              start=(t == 0), stop=(t == TILES - 1))
                mm.then_inc(s["gathered"], 1)
                pe.wait_ge(loaded["win"][p], 16 * (pair + 1))
                pe.wait_ge(s["xT_ready"], n(e))
                for c in range(2):
                    pe.wait_ge(s["gated"], B + 2 * e + c)
                    for f in range(fb):
                        for ps, at in ((ps_g, 0), (ps_u, hidden)):
                            o = at + (c * fb + f) * P
                            for k in range(HALVES):
                                mm = nc.tensor.matmul(ps[:, f, :], win[:, p, k, o:o + P], xT[:, p, k, :], start=(k == 0), stop=(k == 1))
                    mm.then_inc(s["up_in_psum"], 1)
                pe.wait_ge(loaded["wout"][p], 16 * (pair + 1))
                pe.wait_ge(s["gated"], B + 2 * e + 2)
                pe.wait_ge(s["down_ready"], n(e) - 1)
                for g in range(lists):
                    for f in range(ft):
                        mm = nc.tensor.matmul(ps_d[:, g, :], hid[:, f, g * C:(g + 1) * C], wout[:, p, f, :], start=(f == 0), stop=(f == ft - 1))
                mm.then_inc(s["down_in_psum"], 1)
                pe.wait_ge(s["down_ready"], n(e))
                pe.wait_ge(s["back"], n(e))
                for t in range(TILES):
                    for g in range(lists):
                        mm = nc.tensor.matmul(acc[:, t // 2, (t % 2) * DIM:(t % 2 + 1) * DIM], weight_b[:, p, g, t * P:(t + 1) * P],
                                              down[:, p, g, :], start=False, stop=False, skip_group_check=True)
                mm.then_inc(s["returned"], 1)

            experts_loop(pe, step)
            for c in range(4):
                mm = nc.tensor.matmul(acc[:, c, 0:2 * DIM], zeros[:], m.h[:, 2 * c:2 * c + 2, :].rearrange("p t n -> p (t n)"),
                                      start=False, stop=True)
            mm.then_inc(s["closed"], 1)


def shared_ffn(tw, m, name, win, wout, hidden):
    nc = tw.nc
    ft = hidden // P
    names = "cleared up silu gated down added".split()
    s = {k: tw.sem(name + "_" + k) for k in names}
    half_cols = IMAGES // 2 * TOKENS
    with ExitStack() as ctx:
        hid = ctx.enter_context(nc.sbuf_tensor(name + "hid", [P, ft, IMAGES, QUAD], F32))
        act_gate = ctx.enter_context(nc.sbuf_tensor(name + "act_gate", [P, 2, IMAGES // 2, TOKENS], F32))
        ps_g = ctx.enter_context(nc.psum_tensor(name + "ps_g", [P, 2, 512], F32))
        ps_u = ctx.enter_context(nc.psum_tensor(name + "ps_u", [P, 2, 512], F32))
        ps_d = ctx.enter_context(nc.psum_tensor(name + "ps_d", [P, 4, 512], F32))
        block = ctx.enter_context(nc.Block())
        parts = [(f, c) for f in range(ft) for c in range(2)]

        @block.gpsimd
        def _(pool):
            nc.gpsimd.memset(hid[:], 0.0).then_inc(s["cleared"], 1)

        @block.tensor
        def _(pe):
            for i, (f, c) in enumerate(parts):
                if i >= 2:
                    pe.wait_ge(s["gated"], i - 1)
                for ps, at in ((ps_g, 0), (ps_u, hidden)):
                    for k in range(HALVES):
                        x = m.hT[:, k, :, :].rearrange("q t (j n) -> q (t j) n", n=QUAD)[:, IMAGES // 2 * c:IMAGES // 2 * (c + 1), 0:TOKENS]
                        mm = nc.tensor.matmul(ps[:, i % 2, 0:half_cols], win[:, k, at + f * P:at + (f + 1) * P], x, start=(k == 0), stop=(k == 1))
                mm.then_inc(s["up"], 1)
            pe.wait_ge(s["gated"], len(parts))
            for t in range(TILES):
                for f in range(ft):
                    mm = nc.tensor.matmul(ps_d[:, t // 2, (t % 2) * DIM:(t % 2 + 1) * DIM], hid[:, f, 4 * t:4 * t + 4, :], wout[:, f, :],
                                          start=(f == 0), stop=(f == ft - 1))
                mm.then_inc(s["down"], 1)

        @block.scalar
        def _(act):
            for i in range(len(parts)):
                act.wait_ge(s["up"], i + 1)
                if i >= 2:
                    act.wait_ge(s["gated"], i - 1)
                nc.scalar.activation(act_gate[:, i % 2].rearrange("p i n -> p (i n)"), ps_g[:, i % 2, 0:half_cols], ACT.Silu).then_inc(s["silu"], 1)

        @block.vector
        def _(dve):
            dve.wait_ge(s["cleared"], 1)
            for i, (f, c) in enumerate(parts):
                dve.wait_ge(s["silu"], i + 1)
                nc.vector.tensor_tensor(hid[:, f, IMAGES // 2 * c:IMAGES // 2 * (c + 1), 0:TOKENS], act_gate[:, i % 2],
                                        ps_u[:, i % 2, 0:half_cols].rearrange("p (i n) -> p i n", n=TOKENS), ALU.mult).then_inc(s["gated"], 1)
            for t in range(TILES):
                dve.wait_ge(s["down"], 2 * (t // 2) + 2)
                nc.vector.tensor_tensor(tw.y[:, t, :], ps_d[:, t // 2, (t % 2) * DIM:(t % 2 + 1) * DIM], m.h[:, t, :], ALU.add).then_inc(s["added"], 1)
            dve.wait_ge(s["added"], TILES)


def build(nc, ins, out, first, last):
    with ExitStack() as ctx:
        tw = Tower(nc, ctx, ins)
        setup(tw)
        loaded = tw.sem("weights_loaded")
        pending = []

        def weight(nm, src, shape):
            t = tw.sb(nm, shape)
            pending.append((t[:], src))
            return t

        def halves(nm):
            a = ins[nm]
            return weight("w_" + nm, a.rearrange("(k p) n -> p k n", p=HALF), [HALF, HALVES, a.shape[1]])

        def spread(nm):
            a = ins[nm]
            return weight("w_" + nm, a.rearrange("(o n) -> o n", o=1).to_broadcast([P, a.shape[0]]), [P, a.shape[0]])

        plan = {}
        if first == 0:
            def stage_0(tw):
                load = []

                def bring(nm, src, shape):
                    t = tw.sb("w_" + nm, shape)
                    load.append((t[:], src))
                    return t

                w = {"offset_w": bring("offset_w", ins["offset_wT"].rearrange("(s q) n -> q s n", q=P), [P, SLABS, 2 * KPOINTS]),
                     "offset_b": bring("offset_b", ins["offset_b"].rearrange("(o n) -> o n", o=1).to_broadcast([P, 2 * KPOINTS]), [P, 2 * KPOINTS]),
                     "base": bring("base", ins["base"], [TILE_TOKENS, 2 * KPOINTS]), "origin": bring("origin", ins["origin"], [TILE_TOKENS, 1 + KHALVES]),
                     "minus_row": bring("minus_row", ins["minus_row"], [P, 1]),
                     "window_x": bring("window_x", ins["window_x"], [P, KHALVES, GRID, WINDOW_X]), "cover_x": bring("cover_x", ins["cover_x"], [P, COVER_X, WINDOW_X]),
                     "dconv": bring("dconv", ins["dconv"], [P, CHANNELS, KHALVES, DIM]),
                     "gamma": bring("gamma", ins["gamma"], [HALF, HALVES]), "beta": bring("beta", ins["beta"], [HALF, HALVES])}
                arrived = tw.sem("tok_weights")
                with nc.Block() as block:
                    @block.sync
                    def _(sp):
                        for dst, src in load:
                            sp.dma_start(dst, src).then_inc(arrived, 16)
                        sp.wait_ge(arrived, 16 * len(load))
                tokenizer(tw, w)

            plan[0] = stage_0
        if first <= 2 <= last:
            w2 = halves("L0_ffn_Wg")

            def stage_2(tw):
                m = MoeBuffers(tw)
                front(tw, m, "L0_ffn", w2, 8)
                with nc.psum_tensor("L0_ffn_rows", [P, 2, 512], F32) as ps, tw.scratch():
                    RowScratch(tw, m)
                    token_choice_rows(tw, m, "L0_ffn", ps)
                experts(tw, m, "L0_ffn", 0, 2, 120, 512, ins["L0_ffn_Win"], ins["L0_ffn_W2"], 16, m.h)
                finish_norm(tw, "L0_ffn")

            plan[2] = stage_2
        if first <= 6 <= last:
            w6 = halves("L2_ffn_gate"), halves("L2_ffn_shared_in"), weight("w_shared_out", ins["L2_ffn_shared_out"].rearrange("(f q) n -> q f n", q=P), [P, 3, DIM])

            def stage_6(tw):
                m = MoeBuffers(tw)
                front(tw, m, "L2_ffn", w6[0], 16)
                shared_ffn(tw, m, "L2_shared", w6[1], w6[2], 384)
                with nc.psum_tensor("L2_ffn_rows", [P, 2, 512], F32) as ps, tw.scratch():
                    RowScratch(tw, m)
                    expert_choice_rows(tw, m, "L2_ffn", ps, 100)
                experts(tw, m, "L2_ffn", 1, 1, 100, 768, ins["L2_ffn_Win"], ins["L2_ffn_Wout"], 0, tw.y)
                finish_norm(tw, "L2_ffn")

            plan[6] = stage_6
        if first <= 1 <= last:
            w1 = halves("L0_attn_Wqkv"), halves("L0_attn_Wo"), tw.sb("w_L0_attn_bo", [P, DIM])
            rope = {"cos": tw.sb("rope_cos", [P, HEAD_DIM]), "sin": tw.sb("rope_sin", [P, HEAD_DIM]), "mask": tw.sb("rope_mask", [P, TOKENS]),
                    "context": tw.sb("is_context", [P, 1]), "latent": tw.sb("is_latent", [P, 1]),
                    "gain": spread("L0_attn_ln_g"), "shift": spread("L0_attn_ln_b")}
            for key, src in (("cos", "rope_cos"), ("sin", "rope_sin"), ("mask", "rope_mask"), ("context", "is_context"), ("latent", "is_latent")):
                pending.append((rope[key][:], ins[src]))
            pending.append((w1[2][:], ins["L0_attn_bo"]))

            def stage_1(tw):
                b = AttentionBuffers(tw)
                softmax_attention(tw, b, "L0_attn", "rope", *w1, rope=rope)
                finish_norm(tw, "L0_attn")

            plan[1] = stage_1
        if first <= 3 <= last:
            w3 = {"Wq": weight("w_L1_attn_Wq", ins["L1_attn_Wq"].rearrange("(g p) n -> p g n", p=P), [P, 6, DIM]),
                  "bq": weight("w_L1_attn_bq", ins["L1_attn_bq"], [P, 6]),
                  "Wkv": halves("L1_attn_Wkv"), "bk": spread("L1_attn_bk"), "bv": spread("L1_attn_bv"),
                  "A": weight("w_L1_attn_A", ins["L1_attn_A"], [P, P]), "AT": weight("w_L1_attn_AT", ins["L1_attn_AT"], [P, P]),
                  "diagonal": weight("w_L1_attn_diagonal", ins["L1_attn_diagonal"], [P, 6]),
                  "sink": weight("w_L1_attn_sink", ins["L1_attn_sink"], [P, HEADS]), "v_null": weight("w_L1_attn_v_null", ins["L1_attn_v_null"], [P, DIM]), "bo": spread("L1_attn_bo"),
                  "Wo": weight("w_L1_attn_Wo", ins["L1_attn_Wo"].rearrange("c (k p) n -> p c k n", p=HALF), [HALF, BRANCHES, HALVES, DIM]),
                  "cos": weight("w_cheb_cos", ins["cheb_cos"], [P, HEAD_DIM]), "sin": weight("w_cheb_sin", ins["cheb_sin"], [P, HEAD_DIM]),
                  "causal": weight("w_causal", ins["causal"], [P, TOKENS])}

            def stage_3(tw):
                branch_attention(tw, "L1_attn", w3)
                finish_norm(tw, "L1_attn")

            plan[3] = stage_3
        for i, l in ((4, "L1_ffn"), (8, "L3_ffn")):
            if first <= i <= last:
                w = halves(l + "_gate"), spread(l + "_bg"), halves(l + "_Wqkv"), halves(l + "_Wproj"), spread(l + "_bproj"), spread(l + "_bqkv")
                adapter = {"down": halves(l + "_down"), "up": weight(l + "_up", ins[l + "_up"], [P, 3 * DIM])}
                if l == "L1_ffn":
                    adapter["down_bias"] = spread(l + "_down_bias")
                    adapter["up_bias"] = weight(l + "_up_bias", ins[l + "_up_bias"], [8, 3 * DIM])

                def stage(tw, l=l, w=w, adapter=adapter):
                    m, b = MoeBuffers(tw), AttentionBuffers(tw)
                    front(tw, m, l, w[0], 8)
                    lora_gate(tw, m, l, w[1])
                    softmax_attention(tw, b, l, "adapted", w[2], w[3], w[4], bqkv=w[5], adapter={**adapter, "combine": m.combine})
                    finish_norm(tw, l)

                plan[i] = stage
        if first <= 5 <= last:
            w5 = halves("L2_attn_qkv"), halves("L2_attn_proj"), spread("L2_attn_proj_b")

            def stage_5(tw):
                b = AttentionBuffers(tw)
                softmax_attention(tw, b, "L2_attn", "unit", *w5)
                finish_norm(tw, "L2_attn")

            plan[5] = stage_5
        if first <= 7 <= last:
            w7 = (halves("L3_attn_Wqkv"), spread("L3_attn_bqkv"), halves("L3_attn_Wp"), spread("L3_attn_bp"))

            def stage_7(tw):
                b = AttentionBuffers(tw)
                softmax_attention(tw, b, "L3_attn", "biased", w7[0], w7[2], w7[3], bqkv=w7[1])
                finish_norm(tw, "L3_attn")

            plan[7] = stage_7
        pending.append((tw.is_pad[:], ins["is_pad"]))
        with nc.Block() as block:
            @block.sync
            def _(sp):
                for dst, src in pending:
                    sp.dma_start(dst, src).then_inc(loaded, 16)
                sp.wait_ge(loaded, 16 * len(pending))

        if first > 0:
            y_loaded, y_cleared = tw.sem("y_loaded"), tw.sem("y_cleared")
            with nc.Block() as block:
                @block.gpsimd
                def _(pool):
                    nc.gpsimd.memset(tw.mean[:], 0.0)
                    nc.gpsimd.memset(tw.rstd[:], 1.0)
                    nc.gpsimd.memset(tw.y[:], 0.0).then_inc(y_cleared, 1)

                @block.sync
                def _(sp):
                    sp.wait_ge(y_cleared, 1)
                    for j in range(IMG_PER_TILE):
                        sp.dma_start(tw.y[QUAD * j:QUAD * j + TOKENS, :, :],
                                     ins["dbg_h"].rearrange("(i j) n c -> j n i c", j=IMG_PER_TILE)[j]).then_inc(y_loaded, 16)
                    sp.wait_ge(y_loaded, 64)
        for i, stage in sorted(plan.items()):
            with tw.stage(f"stage{i}_"):
                stage(tw)

        normed, stored = tw.sem("result_normed"), tw.sem("result_stored")
        with nc.Block() as block:
            @block.vector
            def _(dve):
                for t in range(TILES):
                    nc.vector.tensor_scalar(tw.y[:, t, :], tw.y[:, t, :], tw.mean[:, t, :], tw.rstd[:, t, :],
                                            ALU.subtract, ALU.mult).then_inc(normed, 1)

            @block.sync
            def _(sp):
                sp.wait_ge(normed, TILES)
                for j in range(IMG_PER_TILE):
                    sp.dma_start(out.rearrange("(i j) n c -> j n i c", j=IMG_PER_TILE)[j],
                                 tw.y[QUAD * j:QUAD * j + TOKENS, :, :]).then_inc(stored, 16)
                sp.wait_ge(stored, 16 * IMG_PER_TILE)


_DEBUG = (0, 8)


def layout(x):
    a = {k: np.asarray(v) for k, v in x.items()}
    o = {}
    x = a["x"]
    p = x[:, :, :GRID * PATCH, :GRID * PATCH].reshape(IMAGES, CHANNELS, GRID, PATCH, GRID, PATCH)
    o["patchesT"] = p.transpose(1, 3, 5, 0, 2, 4).reshape(CHANNELS * KPOINTS, IMAGES * TOKENS)
    o["offset_wT"] = a["L0_tok_offset_w"].reshape(PATCH, PATCH, 2, -1).transpose(3, 2, 1, 0).reshape(-1, 2 * KPOINTS)
    o["offset_b"] = a["L0_tok_offset_b"].reshape(PATCH, PATCH, 2).T.reshape(-1)
    padded = np.zeros((IMAGES, CHANNELS, PADDED, PADDED), x.dtype)
    padded[:, :, MARGIN:MARGIN + IMAGE, MARGIN:MARGIN + IMAGE] = x
    rows = padded.transpose(0, 2, 1, 3).reshape(TILES, IMG_PER_TILE, PADDED, CHANNELS, PADDED)
    o["strips"] = np.stack([rows[:, :, PATCH * g:PATCH * g + WINDOW] for g in range(GRID)])
    at = lambda i, size: slice(MARGIN + size * i, MARGIN + size * (i + 1))
    o["windows"] = np.stack([np.stack([rows[:, :, at(i, WINDOW), :, at(j, WINDOW_X)] for j in range(COVER_X)]) for i in range(COVER_Y)])
    o["dconv"] = a["L0_tok_dconv_w"].transpose(1, 3, 2, 0).reshape(CHANNELS, KHALVES, P, DIM).transpose(2, 0, 1, 3)
    o["gamma"], o["beta"] = a["L0_tok_bn_gamma"].reshape(HALVES, HALF).T, a["L0_tok_bn_beta"].reshape(HALVES, HALF).T
    g, k = np.arange(GRID), np.arange(PATCH)
    place = np.zeros((IMG_PER_TILE, GRID, GRID, 2, PATCH, PATCH), np.float32)
    place[:, :, :, 0] = (PATCH * g)[None, :, None, None, None] + k[None, None, None, None, :]
    place[:, :, :, 1] = (PATCH * g)[None, None, :, None, None] + k[None, None, None, :, None]
    o["base"] = place.reshape(TILE_TOKENS, 2 * KPOINTS)
    place = o["base"].reshape(TILE_TOKENS, 2, KHALVES, P)
    o["origin"] = np.concatenate([place[:, 0, 0:1, 0], place[:, 1, :, 0]], 1) - MARGIN
    o["minus_row"] = -np.tile(np.arange(QUAD, dtype=np.float32), IMG_PER_TILE)[:, None]
    column, half = np.arange(WINDOW_X), np.arange(KHALVES)
    o["window_x"] = np.tile(HALF_COLS * half[:, None, None] + PATCH * g[:, None] - MARGIN + column, (P, 1, 1, 1)).astype(np.float32)
    o["cover_x"] = np.tile(WINDOW_X * np.arange(COVER_X)[:, None] + column, (P, 1, 1)).astype(np.float32)
    o["L3_attn_Wqkv"] = np.concatenate([a["L3_attn_Wq"], a["L3_attn_Wk"], a["L3_attn_Wv"]], 1)
    o["L3_attn_bqkv"] = np.concatenate([a["L3_attn_bq"], a["L3_attn_bk"], a["L3_attn_bv"]])
    o["L0_attn_Wqkv"] = np.concatenate([a["L0_attn_Wq"], a["L0_attn_Wkv"]], 1)
    o["L0_attn_Wo"] = np.concatenate([a["L0_attn_Wo_ctx"], a["L0_attn_Wo_lat"]], 1)
    context = TOKENS + (TOKENS - LATENT)
    bo = np.zeros((IMG_PER_TILE, QUAD, DIM), np.float32)
    bo[:, :context], bo[:, context:TOKENS] = a["L0_attn_bo_ctx"], a["L0_attn_bo_lat"]
    o["L0_attn_bo"] = bo.reshape(P, DIM)
    o["L0_attn_ln_g"], o["L0_attn_ln_b"] = a["L0_attn_ln_g"], a["L0_attn_ln_b"]
    inv = 1.0 / 10000.0 ** (np.arange(0, HEAD_DIM, 2, dtype=np.float32) / HEAD_DIM)
    angle = np.arange(TOKENS, dtype=np.float32)[:, None] * inv[None, :].astype(np.float32)
    quads = lambda x: np.tile(np.concatenate([x, np.zeros((QUAD - TOKENS, x.shape[1]), x.dtype)]).astype(np.float32), (IMG_PER_TILE, 1))
    o["rope_cos"] = quads(np.concatenate([np.cos(angle), np.cos(angle)], 1))
    o["rope_sin"] = quads(np.concatenate([-np.sin(angle), np.sin(angle)], 1))
    token = np.arange(TOKENS)
    o["rope_mask"] = quads(np.where((token[:, None] < context) & (token[None, :] >= context), -1e30, 0.0))
    o["is_pad"] = 1 - quads(np.ones((TOKENS, 1)))
    o["is_context"] = quads((token < context)[:, None])
    o["is_latent"] = quads((token >= context)[:, None])
    o["L1_attn_Wq"] = a["L1_attn_Wq"]
    o["L1_attn_bq"] = a["L1_attn_bq"].reshape(-1, P).T
    o["L1_attn_Wkv"] = np.concatenate([a["L1_attn_Wk"].T, a["L1_attn_Wv"].T], 1)
    o["L1_attn_bk"], o["L1_attn_bv"] = a["L1_attn_bk"], a["L1_attn_bv"]
    blocks = lambda x: np.block([[x if i == j else np.zeros_like(x) for j in range(P // HEAD_DIM)] for i in range(P // HEAD_DIM)])
    o["L1_attn_A"], o["L1_attn_AT"] = blocks(a["L1_attn_A"]), blocks(a["L1_attn_A"].T)
    o["L1_attn_diagonal"] = a["L1_attn_id_bias"].reshape(-1, P).T
    o["L1_attn_sink"] = np.repeat(a["L1_attn_sink_scalars"].reshape(BRANCHES, HEADS), QUAD, axis=0)
    o["L1_attn_v_null"] = np.repeat(a["L1_attn_v_nulls"].reshape(BRANCHES, DIM), QUAD, axis=0)
    o["L1_attn_bo"] = a["L1_attn_bo"].reshape(-1)
    o["L1_attn_Wo"] = a["L1_attn_Wo"]
    half = HEAD_DIM // 2
    pos = (np.float32(2) * np.arange(TOKENS, dtype=np.float32) / np.float32(TOKENS - 1) - np.float32(1)).astype(np.float32)
    cheb = [np.ones_like(pos), pos]
    for _ in range(2, HEAD_DIM + 1):
        cheb.append((np.float32(2) * pos * cheb[-1] - cheb[-2]).astype(np.float32))
    cheb = np.stack(cheb, 1)
    degree = np.clip(1 + np.round(np.arange(half, dtype=np.float32) / (half - 1) * (HEAD_DIM - 2)).astype(np.int32), 1, HEAD_DIM - 1)
    raw1, raw2 = cheb[:, degree], cheb[:, degree + 1]
    length = np.sqrt(raw1 * raw1 + raw2 * raw2 + np.float32(1e-8))
    o["cheb_cos"] = quads(np.concatenate([raw1 / length, raw1 / length], 1))
    o["cheb_sin"] = quads(np.concatenate([-raw2 / length, raw2 / length], 1))
    o["causal"] = quads(token[None, :] <= token[:, None])
    for l, g, bg, wqkv, bqkv, wp, bp, down, up in (
            ("L1_ffn", "Wg", "bg", "Wqkv", "bqkv", "Wproj", "bproj", "A", "Bm"),
            ("L3_ffn", "W_gate", "b_gate", "W_qkv", "b_qkv", "W_proj", "b_proj", "A", "B_lora")):
        x = lambda nm: a[l + "_" + nm]
        o[l + "_gate"], o[l + "_bg"] = x(g).T, x(bg)
        o[l + "_Wqkv"], o[l + "_bqkv"] = x(wqkv).T, x(bqkv)
        o[l + "_Wproj"], o[l + "_bproj"] = x(wp).T, x(bp)
        o[l + "_down"] = x(down).reshape(-1, DIM).T
        o[l + "_up"] = x(up).transpose(0, 2, 1).reshape(-1, 3 * DIM)
    o["L1_ffn_down_bias"], o["L1_ffn_up_bias"] = a["L1_ffn_ba"].reshape(-1), a["L1_ffn_bb"]
    o["L2_attn_qkv"], o["L2_attn_proj"], o["L2_attn_proj_b"] = a["L2_attn_qkv_w"].T, a["L2_attn_proj_w"].T, a["L2_attn_proj_b"]
    h = a["L0_ffn_W2"].shape[1]
    o["L0_ffn_Wg"] = a["L0_ffn_Wg"]
    o["L0_ffn_Win"] = np.concatenate([a["L0_ffn_W1"][..., h:], a["L0_ffn_W1"][..., :h]], 2)
    o["L0_ffn_W2"] = a["L0_ffn_W2"]
    o["L2_ffn_gate"] = a["L2_ffn_gate_weight"].T
    o["L2_ffn_Win"] = np.concatenate([a["L2_ffn_Wg"].transpose(0, 2, 1), a["L2_ffn_Wu"].transpose(0, 2, 1)], 2)
    o["L2_ffn_Wout"] = a["L2_ffn_Wd"].transpose(0, 2, 1)
    o["L2_ffn_shared_in"] = np.concatenate([a["L2_ffn_Ws_g"].T, a["L2_ffn_Ws_u"].T], 1)
    o["L2_ffn_shared_out"] = a["L2_ffn_Ws_d"].T
    o["L3_attn_Wp"], o["L3_attn_bp"] = a["L3_attn_Wp"], a["L3_attn_bp"]
    if "dbg_h" in a:
        o["dbg_h"] = a["dbg_h"]
    return {k: np.ascontiguousarray(v) for k, v in o.items()}


def kernel(**inputs):
    import concourse.bacc as bacc
    from concourse.bass_utils import run_bass_kernel_spmd

    nc = bacc.Bacc("TRN2", target_bir_lowering=False, num_devices=1)
    arrays = layout(inputs)
    ins = {k: nc.dram_tensor("in_" + k, v.shape, mybir.dt.from_np(v.dtype), kind="ExternalInput").ap() for k, v in arrays.items()}
    out = nc.dram_tensor("result", (IMAGES, TOKENS, DIM), F32, kind="ExternalOutput").ap()
    build(nc, ins, out, *_DEBUG)
    r = run_bass_kernel_spmd(nc, [{"in_" + k: v for k, v in arrays.items()}], core_ids=[0])
    return r.results[0]["result"]
```
